# Optimizing a Trainium2 kernel written in Bass

```python
import numpy as np
import jax
import jax.numpy as jnp

def _softmax(x, axis=-1):
    return jax.nn.softmax(x, axis=axis)

def _gelu(x):
    return jax.nn.gelu(x, approximate=True)

def _silu(x):
    return jax.nn.silu(x)

def _sigmoid(x):
    return jax.nn.sigmoid(x)

def _layernorm(x, axis=-1, eps=1e-05):
    m = jnp.mean(x, axis=axis, keepdims=True)
    v = jnp.var(x, axis=axis, keepdims=True)
    return (x - m) / jnp.sqrt(v + eps)

def _scatter_add(tgt, idx, src, axis=0):
    return tgt.at[idx].add(src)

def _segment_sum(src, seg, n):
    return jax.ops.segment_sum(src, seg, n)
kernel_name = 'mk_xattn_ffn_d1_seqx_r4_4895b5'

def setup_inputs(seed: int=0):
    np.random.seed(seed)
    _w = jnp.asarray

    def _rec_inputs():
        import jax
        import jax.numpy as jnp
        _rk = jax.random.key(seed)
        x = -0.0002928 + 1 * jax.random.normal(jax.random.fold_in(_rk, 1), (16, 112, 512), jnp.float32)
        _lenS = 112 - jax.random.randint(jax.random.fold_in(_rk, 7), (16,), 0, max(1, 112 // 4) + 1, jnp.int32)
        _lenS2 = 375 - jax.random.randint(jax.random.fold_in(_rk, 8), (16,), 0, max(1, 375 // 4) + 1, jnp.int32)
        _ctx_2048P = jax.random.normal(jax.random.fold_in(_rk, 11), (16, 16, 512), jnp.float32)
        _ctx_2048c = jax.random.dirichlet(jax.random.fold_in(_rk, 511), 0.3 * jnp.ones((16,), jnp.float32), (16, 375))
        _ctx_2048t = jnp.einsum('bsk,bkd->bsd', _ctx_2048c, _ctx_2048P)
        _ctx_2048t = _ctx_2048t * jax.lax.rsqrt(jnp.mean(jnp.square(_ctx_2048t)) + 1e-12) * 0.953939
        ctx_2048 = 4.13588e-05 + 0.999923 * (_ctx_2048t + 0.3 * jax.random.normal(jax.random.fold_in(_rk, 611), (16, 375, 512), jnp.float32))
        _validS = jnp.arange(112)[None, :] < _lenS[:, None]
        _validS2 = jnp.arange(375)[None, :] < _lenS2[:, None]
        _causal = jnp.tril(jnp.ones((112, 112), dtype=bool))
        mask_1xSxS2_ff0 = jnp.where(jnp.ones((1, 112, 375), dtype=bool), 0.0, -1000000000.0).astype(jnp.float32)
        return (x, ctx_2048, mask_1xSxS2_ff0)
    x, ctx_2048, mask_1xSxS2_ff0 = _rec_inputs()

    def _L0_xattn_setup():
        import jax, jax.numpy as jnp
        import numpy as np
        H = 512
        NH = 16
        NKV = 4
        HD = 128
        GROUPS = NH // NKV
        EPS = 1e-06
        B, S, SE = (1, 512, 1024)

        def _rmsnorm(x, w, eps=EPS):
            xf = x.astype(jnp.float32)
            var = jnp.mean(xf * xf, axis=-1, keepdims=True)
            return (xf * jax.lax.rsqrt(var + eps)).astype(x.dtype) * w
        key = jax.random.key(seed)
        ks = jax.random.split(key, 12)
        sc = 0.02
        return {'hidden_states': jax.random.normal(ks[0], (B, S, H), jnp.float32), 'encoder_hidden_states': jax.random.normal(ks[1], (B, SE, H), jnp.float32), 'attention_mask': jnp.zeros((B, S, SE), jnp.float32), 'Wq': jax.random.normal(ks[2], (H, NH * HD), jnp.float32) * sc, 'bq': jax.random.normal(ks[3], (NH * HD,), jnp.float32) * sc, 'Wk': jax.random.normal(ks[4], (H, NKV * HD), jnp.float32) * sc, 'bk': jax.random.normal(ks[5], (NKV * HD,), jnp.float32) * sc, 'Wv': jax.random.normal(ks[6], (H, NKV * HD), jnp.float32) * sc, 'bv': jax.random.normal(ks[7], (NKV * HD,), jnp.float32) * sc, 'Wo': jax.random.normal(ks[8], (NH * HD, H), jnp.float32) * sc, 'qn_w': jnp.ones((HD,), jnp.float32), 'kn_w': jnp.ones((HD,), jnp.float32)}
    _L0_xattn_all = _L0_xattn_setup()
    _L0_xattn_in = {k: v for k, v in _L0_xattn_all.items() if k in ('Wq', 'bq', 'Wk', 'bk', 'Wv', 'bv', 'Wo', 'qn_w', 'kn_w')}
    del _L0_xattn_all

    def _L0_ffn_setup():
        import jax, jax.numpy as jnp
        import numpy as np
        SEQ, BS, D, F, E = (256, 2, 512, 512, 8)
        key = jax.random.key(seed)
        ks = jax.random.split(key, 8)
        s = 0.02
        return {'hidden_states': jax.random.normal(ks[0], (SEQ, BS, D), jnp.float32), 'router_w': jax.random.normal(ks[1], (D, E), jnp.float32) * s, 'gate_w': jax.random.normal(ks[2], (E, D, F), jnp.float32) * s, 'up_w': jax.random.normal(ks[3], (E, D, F), jnp.float32) * s, 'down_w': jax.random.normal(ks[4], (E, F, D), jnp.float32) * s, 'shared_gate_w': jax.random.normal(ks[5], (D, F), jnp.float32) * s, 'shared_up_w': jax.random.normal(ks[6], (D, F), jnp.float32) * s, 'shared_down_w': jax.random.normal(ks[7], (F, D), jnp.float32) * s}
    _L0_ffn_all = _L0_ffn_setup()
    _L0_ffn_in = {k: v for k, v in _L0_ffn_all.items() if k in ('router_w', 'gate_w', 'up_w', 'down_w', 'shared_gate_w', 'shared_up_w', 'shared_down_w')}
    del _L0_ffn_all
    return {'x': x, 'ctx_2048': ctx_2048, 'mask_1xSxS2_ff0': mask_1xSxS2_ff0, 'L0_xattn_Wq': _L0_xattn_in['Wq'], 'L0_xattn_bq': _L0_xattn_in['bq'], 'L0_xattn_Wk': _L0_xattn_in['Wk'], 'L0_xattn_bk': _L0_xattn_in['bk'], 'L0_xattn_Wv': _L0_xattn_in['Wv'], 'L0_xattn_bv': _L0_xattn_in['bv'], 'L0_xattn_Wo': _L0_xattn_in['Wo'], 'L0_xattn_qn_w': _L0_xattn_in['qn_w'], 'L0_xattn_kn_w': _L0_xattn_in['kn_w'], 'L0_ffn_router_w': _L0_ffn_in['router_w'], 'L0_ffn_gate_w': _L0_ffn_in['gate_w'], 'L0_ffn_up_w': _L0_ffn_in['up_w'], 'L0_ffn_down_w': _L0_ffn_in['down_w'], 'L0_ffn_shared_gate_w': _L0_ffn_in['shared_gate_w'], 'L0_ffn_shared_up_w': _L0_ffn_in['shared_up_w'], 'L0_ffn_shared_down_w': _L0_ffn_in['shared_down_w']}

def reference(x, ctx_2048, mask_1xSxS2_ff0, L0_xattn_Wq, L0_xattn_bq, L0_xattn_Wk, L0_xattn_bk, L0_xattn_Wv, L0_xattn_bv, L0_xattn_Wo, L0_xattn_qn_w, L0_xattn_kn_w, L0_ffn_router_w, L0_ffn_gate_w, L0_ffn_up_w, L0_ffn_down_w, L0_ffn_shared_gate_w, L0_ffn_shared_up_w, L0_ffn_shared_down_w):
    import jax
    import jax.numpy as jnp

    def _L0_xattn_ref(hidden_states, encoder_hidden_states, attention_mask, Wq, bq, Wk, bk, Wv, bv, Wo, qn_w, kn_w):
        import jax, jax.numpy as jnp
        import numpy as np
        H = 512
        NH = 16
        NKV = 4
        HD = 128
        GROUPS = NH // NKV
        EPS = 1e-06
        B, S, SE = (1, 512, 1024)

        def _rmsnorm(x, w, eps=EPS):
            xf = x.astype(jnp.float32)
            var = jnp.mean(xf * xf, axis=-1, keepdims=True)
            return (xf * jax.lax.rsqrt(var + eps)).astype(x.dtype) * w
        b, s, _ = hidden_states.shape
        se = encoder_hidden_states.shape[1]
        q = (hidden_states @ Wq + bq).reshape(b, s, NH, HD).transpose(0, 2, 1, 3)
        k = (encoder_hidden_states @ Wk + bk).reshape(b, se, NKV, HD).transpose(0, 2, 1, 3)
        v = (encoder_hidden_states @ Wv + bv).reshape(b, se, NKV, HD).transpose(0, 2, 1, 3)
        k = jnp.repeat(k, GROUPS, axis=1)
        v = jnp.repeat(v, GROUPS, axis=1)
        q = _rmsnorm(q, qn_w)
        k = _rmsnorm(k, kn_w)
        scale = 1.0 / np.sqrt(HD).astype(np.float32)
        scores = jnp.einsum('bhsd,bhed->bhse', q, k) * scale
        scores = scores + attention_mask[:, None, :, :]
        probs = jax.nn.softmax(scores.astype(jnp.float32), axis=-1).astype(q.dtype)
        out = jnp.einsum('bhse,bhed->bhsd', probs, v)
        out = out.transpose(0, 2, 1, 3).reshape(b, s, NH * HD)
        return out @ Wo

    def _L0_ffn_ref(hidden_states, router_w, gate_w, up_w, down_w, shared_gate_w, shared_up_w, shared_down_w):
        import jax, jax.numpy as jnp
        import numpy as np
        SEQ, BS, D, F, E = (256, 2, 512, 512, 8)
        S, B, Dm = hidden_states.shape
        x = hidden_states.reshape(-1, Dm)
        logits = x @ router_w
        expert_idx = jnp.argmax(logits, axis=-1)
        score = jax.nn.sigmoid(jnp.max(logits, axis=-1))
        xs = x * score[:, None]
        n_experts = router_w.shape[1]
        out = jnp.zeros_like(x)
        for e in range(n_experts):
            m = (expert_idx == e)[:, None]
            xe = jnp.where(m, xs, 0.0)
            h = jax.nn.silu(xe @ gate_w[e]) * (xe @ up_w[e])
            out = out + jnp.where(m, h @ down_w[e], 0.0)
        shared = jax.nn.silu(x @ shared_gate_w) * (x @ shared_up_w) @ shared_down_w
        return (out + shared).reshape(S, B, Dm)
    x = x + _L0_xattn_ref(_layernorm(x, axis=-1), ctx_2048, mask_1xSxS2_ff0, L0_xattn_Wq, L0_xattn_bq, L0_xattn_Wk, L0_xattn_bk, L0_xattn_Wv, L0_xattn_bv, L0_xattn_Wo, L0_xattn_qn_w, L0_xattn_kn_w)
    x = x + _L0_ffn_ref(_layernorm(x, axis=-1), L0_ffn_router_w, L0_ffn_gate_w, L0_ffn_up_w, L0_ffn_down_w, L0_ffn_shared_gate_w, L0_ffn_shared_up_w, L0_ffn_shared_down_w)
    return x

_drawn_inputs = setup_inputs


def setup_inputs(seed=0):
    import zlib

    import numpy as np

    out = dict(_drawn_inputs(seed))
    spreads = {'L0_xattn_qn_w': (1.0, 0.6), 'L0_xattn_kn_w': (1.0, 0.6)}
    factors = {'L0_xattn_bq': 8.0,
     'L0_xattn_bk': 8.0,
     'L0_xattn_bv': 3.136,
     'L0_ffn_router_w': 2.9,
     'L0_ffn_gate_w': 2.772,
     'L0_ffn_up_w': 2.738,
     'L0_ffn_down_w': 2.748}
    for name, (base, spread) in spreads.items():
        noise = np.random.default_rng([zlib.crc32(name.encode()), seed]).standard_normal(out[name].shape)
        drawn = base * np.exp(spread * noise) if base else spread * noise
        out[name] = jnp.asarray(drawn.astype(out[name].dtype))
    for name, factor in factors.items():
        out[name] = (out[name] * factor).astype(out[name].dtype)
    return out
```

```python
from contextlib import ExitStack

import numpy as np
import concourse.bass as bass
from concourse import mybir

F32 = mybir.dt.float32
F32R = mybir.dt.float32r
BF16 = mybir.dt.bfloat16
I32 = mybir.dt.int32
U32 = mybir.dt.uint32
ALU = mybir.AluOpType
ACT = mybir.ActivationFunctionType
AX_X = mybir.AxisListType.X

B, S, H = 16, 112, 512
SE = 375
NH, NKV, HD = 16, 4, 128
G = NH // NKV
KC = H // 128
KT = 3
TK = SE // KT
SE_EVEN = SE + SE % 2
LN_EPS, RMS_EPS = 1e-5, 1e-6
TOK = B * S
NT = TOK // 128
F = 512
FC = F // 128
E = 8
SLOTS = (TOK - E) // 128 + E
PIECE = 2048
LOWEST = -3.0e38


def wait(eng, sem, value):
    if not isinstance(value, int) or value > 0:
        eng.wait_ge(sem, value)


def wait_apart(eng, passed, sem, value):
    eng.wait_ge(sem, value)
    eng.sem_inc(passed, 1)


def xattn_ffn_kernel(nc, x, ctxT, mask, wq, bq_rows, wk, bk_rows, wv, bv_cols, qn_col, kn_col, wo,
                     router, expert_w, shared_w, out):
    with ExitStack() as outer:
        def sb(name, shape, dt=F32, into=outer):
            return into.enter_context(nc.sbuf_tensor(name, shape, dt))

        def psum(name, shape, dt=F32):
            return outer.enter_context(nc.psum_tensor(name, shape, dt))

        def sem(name):
            return outer.enter_context(nc.semaphore(name))

        wq_part = [sb(f"wq_{n}", [128, KC, NH * HD], F32R) for n in ("hi", "lo")]
        wide_part = wq_part
        small = sb("small", [128, 64])
        ident = sb("ident", [128, 128])
        minus_half = sb("minus_half", [128, 4])
        a_phase = ExitStack()

        def a_sb(name, shape, dt=F32):
            return sb(name, shape, dt, a_phase)
        wk_part = [a_sb(f"wk_{n}", [128, KC, NKV * HD], F32R) for n in ("hi", "lo")]
        wv_part = [a_sb(f"wv_{n}", [128, KC, NKV * HD], F32R) for n in ("hi", "lo")]
        bq_sb = a_sb("bq_sb", [S, NH * HD])
        bk_sb = a_sb("bk_sb", [TK, NKV * HD])
        bv_sb = a_sb("bv_sb", [128, NKV])
        qw_sb = a_sb("qw_sb", [128, 1])
        kw_sb = a_sb("kw_sb", [128, 1])
        qws = a_sb("qws", [128, 1])
        mask_sb = a_sb("mask_sb", [S, SE])
        ctx_raw = a_sb("ctx_raw", [128, KC, SE])
        ctx_part = [a_sb(f"ctx_{n}", [128, KC, SE], F32R) for n in ("hi", "lo")]
        x_sb = a_sb("x_sb", [S, H])
        xT_part = [a_sb(f"xT_{n}", [128, KC, S], F32R) for n in ("hi", "lo")]
        q_sb = a_sb("q_sb", [S, G * HD])
        k_sb = a_sb("k_sb", [TK, NKV * HD])
        squares = a_sb("squares", [128, G * HD], BF16)
        kT_part = [[a_sb(f"kT_{n}{p}", [128, NKV, SE_EVEN], F32R) for n in ("hi", "lo")] for p in range(2)]
        v_part = [[a_sb(f"v_{n}{p}", [TK, KT, NKV * HD], F32R) for n in ("hi", "lo")] for p in range(2)]
        qT_part = [a_sb(f"qT_{n}", [128, G * S], F32R) for n in ("hi", "lo")]
        o_sb = a_sb("o_sb", [128, G * S])
        with ExitStack() as early:
            stage = [sb(f"stage{i}", [128, PIECE], F32, early) for i in range(2)]
        probs = a_sb("probs", [S, G, SE])
        pT_part = [a_sb(f"pT_{n}", [TK, KT, G * S], F32R) for n in ("hi", "lo")]

        a_phase.close()

        shared_raw = sb("shared_raw", [128, 3, KC * F])
        acc = sb("acc", [128, NT, H])
        router_sb = sb("router_sb", [128, KC, E])
        below = sb("below", [128, 128], BF16)
        ones = sb("ones", [128, 128], BF16)
        iota_e = sb("iota_e", [128, E])
        slot_row = sb("slot_row", [128, SLOTS])
        chosen = sb("chosen", [128, NT, E])
        chosen_b = sb("chosen_b", [128, E], BF16)
        seen_b = sb("seen_b", [128, E], BF16)
        best = sb("best", [128, NT])
        best8 = sb("best8", [128, 8])
        best_at = sb("best_at", [128, 8], U32)
        best_f = sb("best_f", [128, 1])
        logits = sb("logits", [128, E])
        rank = sb("rank", [128, NT])
        rank_now = sb("rank_now", [128, 1])
        chosen_now = sb("chosen_now", [128, E])
        spare = sb("spare", [128, E])
        count_i = sb("count_i", [128, 3, E], I32)
        padded = sb("padded", [128, E])
        start = sb("start", [128, E + 1])
        places = sb("places", [128, NT, E])
        place = sb("place", [128, NT])
        place_i = sb("place_i", [128, NT], I32)
        place_now = [sb(f"place_now{i}", [128, 1], I32) for i in range(2)]
        owner = sb("owner", [128, 2, SLOTS])
        owner_i = sb("owner_i", [128, SLOTS], I32)
        score = sb("score", [128, NT])
        zeros = sb("zeros", [128, H])
        b_phase = ExitStack()
        wo_stage = [sb(f"wo_stage{i}", [128, PIECE], F32, b_phase) for i in range(2)]
        at_raw = sb("at_raw", [128, NH, 128], F32, b_phase)
        at_part = [[sb(f"at_{n}{p}", [128, NH, 128], F32R, b_phase) for n in ("hi", "lo")] for p in range(2)]
        x_in = sb("x_in", [128, H], F32, b_phase)
        x1 = [sb(f"x1_{p}", [128, H], F32, b_phase) for p in range(2)]
        h_out = [sb(f"h_out{p}", [128, H], F32, b_phase) for p in range(2)]
        hT_f = sb("hT_f", [128, KC, 128], F32, b_phase)
        b_phase.close()
        c_phase = ExitStack()
        h_in = [sb(f"h_in{p}", [128, H], F32, c_phase) for p in range(2)]
        xs_out = [sb(f"xs_out{p}", [128, H], F32, c_phase) for p in range(2)]
        hT_part = [sb(f"hT_{n}", [128, KC, 128], F32R, c_phase) for n in ("hi", "lo")]
        mT_part = [sb(f"mT_{n}", [128, FC, 128], F32R, c_phase) for n in ("hi", "lo")]
        mid_sb = sb("mid_sb", [128, F], F32, c_phase)
        gate_sb = sb("gate_sb", [128, F], F32, c_phase)
        expert_sb = [sb(f"expert_sb{p}", [128, 3, KC, F], F32, c_phase) for p in range(2)]
        block_in = [sb(f"block_in{p}", [128, H], F32, c_phase) for p in range(2)]
        blockT = sb("blockT", [128, KC, 128], F32, c_phase)
        emid_sb = sb("emid_sb", [128, F], F32, c_phase)
        egate_sb = sb("egate_sb", [128, F], F32, c_phase)
        emidT = sb("emidT", [128, FC, 128], F32, c_phase)
        y_out = [sb(f"y_out{p}", [128, H], F32, c_phase) for p in range(2)]
        gathered = h_in
        c_phase.close()

        attended = nc.dram_tensor("attended", [128, NH, TOK], F32, kind="Internal").ap()
        h_dram = nc.dram_tensor("h_rows", [TOK, H], F32, kind="Internal").ap()
        xs_dram = nc.dram_tensor("xs_rows", [SLOTS * 128, H], F32, kind="Internal").ap()
        y_dram = nc.dram_tensor("y_rows", [SLOTS * 128, H], F32, kind="Internal").ap()

        bn, mv, ln_var, ln_rs = small[0:S, 0:6], small[0:S, 6:8], small[0:S, 8:9], small[0:S, 9:10]
        bn128, mv128, ln_var128, ln_rs128 = small[:, 0:6], small[:, 6:8], small[:, 8:9], small[:, 9:10]
        q_ss, q_ms, q_rs = (small[0:S, 12 + 4 * i:16 + 4 * i] for i in range(3))
        k_ss, k_ms, k_rs = (small[0:TK, 24 + 4 * i:28 + 4 * i] for i in range(3))
        top, neg_top, total, inv_total = (small[0:S, 36 + 4 * i:40 + 4 * i] for i in range(4))

        score_ps = [psum(f"score_ps{i}", [128, 512]) for i in range(2)]
        qv_ps = psum("qv_ps", [128, 512])
        k_ps = psum("k_ps", [128, 512])
        turn_ps = psum("turn_ps", [128, 512])
        pT_ps = [psum(f"pT_ps{i}", [128, 512]) for i in range(2)]
        o_ps = psum("o_ps", [128, 512])

        stage_loaded = [sem(f"stage_loaded{i}") for i in range(2)]
        consts_loaded, mask_loaded, ctx_loaded, x_loaded, o_stored = (
            sem(n) for n in ("consts_loaded", "mask_loaded", "ctx_loaded", "x_loaded", "o_stored"))
        w_hi, w_lo, made = sem("w_hi"), sem("w_lo"), sem("made")
        key_padded = sem("key_padded")
        ident_zeroed, ident_made, qws_made = sem("ident_zeroed"), sem("ident_made"), sem("qws_made")
        ctx_hi, ctx_lo = sem("ctx_hi"), sem("ctx_lo")
        ln_stats, ln_step, ln_rsqrt, x_normed, x_turned, xT_hi, xT_lo = (
            sem(n) for n in ("ln_stats", "ln_step", "ln_rsqrt", "x_normed", "x_turned", "xT_hi", "xT_lo"))
        q_proj, q_biased, q_squared, q_mean, q_rsqrt, q_normed, q_turned, qT_hi, qT_lo = (
            sem(n) for n in ("q_proj", "q_biased", "q_squared", "q_mean", "q_rsqrt", "q_normed", "q_turned", "qT_hi", "qT_lo"))
        k_proj, k_biased, k_squared, k_mean, k_rsqrt, k_normed, k_turned, kT_hi, kT_lo = (
            sem(n) for n in ("k_proj", "k_biased", "k_squared", "k_mean", "k_rsqrt", "k_normed", "k_turned", "kT_hi", "kT_lo"))
        v_proj, v_hi, v_lo = sem("v_proj"), sem("v_hi"), sem("v_lo")
        scored, masked, negated, exped, inverted, p_normed, p_turned, pT_hi, pT_lo, pv_done, o_made = (
            sem(n) for n in ("scored", "masked", "negated", "exped", "inverted", "p_normed", "p_turned",
                             "pT_hi", "pT_lo", "pv_done", "o_made"))

        b_consts, wo_hi, wo_lo, at_loaded, at_hi, at_lo, xin_loaded, projected, x_added = (
            sem(n) for n in ("b_consts", "wo_hi", "wo_lo", "at_loaded", "at_hi", "at_lo", "xin_loaded", "projected", "x_added"))
        wo_loaded = [sem(f"wo_loaded{i}") for i in range(2)]
        b_step, b_var, b_rsqrt, h_made, h_turned, hT_copied, routed, logits_out, best_found, best_done, onehot, ranked, rank_out = (
            sem(n) for n in ("b_step", "b_var", "b_rsqrt", "h_made", "h_turned", "hT_copied", "routed", "logits_out",
                             "best_found", "best_done", "onehot", "ranked", "rank_out"))
        tables, score_made, counted, plan, placed, owners, zeroed, rows_zeroed, shared_loaded, shared_hi, shared_lo = (
            sem(n) for n in ("tables", "score_made", "counted", "plan", "placed", "owners", "zeroed", "rows_zeroed",
                             "shared_loaded", "shared_hi", "shared_lo"))
        h2_turned, hT_hi, hT_lo, gated, upped, silued, mid_made, mid_turned, mT_hi, mT_lo, shared_out, shared_added = (
            sem(n) for n in ("h2_turned", "hT_hi", "hT_lo", "gated", "upped", "silued", "mid_made", "mid_turned",
                             "mT_hi", "mT_lo", "shared_out", "shared_added"))
        xs_made = sem("xs_made")
        e_turned, eT_copied, e_gated, e_upped, e_silued, e_mid, e_mid_turned, e_midT, e_down, y_made = (
            sem(n) for n in ("e_turned", "eT_copied", "e_gated", "e_upped", "e_silued", "e_mid",
                             "e_mid_turned", "e_midT", "e_down", "y_made"))
        h_loaded, h_stored, xs_stored, ew_loaded, block_loaded, y_stored, out_stored, rows_gathered = (
            [sem(f"{n}{p}") for p in range(2)] for n in ("h_loaded", "h_stored", "xs_stored", "ew_loaded", "block_loaded",
                                                         "y_stored", "out_stored", "rows_gathered"))
        dve_passed, pool_passed = sem("dve_passed"), sem("pool_passed")
        acc_made, chosen_kept, rank_kept = sem("acc_made"), sem("chosen_kept"), sem("rank_kept")
        now_copied, final_made = sem("now_copied"), sem("final_made")

        pieces = [(wk_part, None, wk), (wv_part, None, wv)] + [(wq_part, c, wq) for c in range(KC)]
        K_PIECE, V_PIECE, Q_PIECE = 1, 2, len(pieces)
        V_TILE = {0: 0, 1: 1, 3: 2}
        V_BEFORE = {0: 0, 1: 1, 2: 2, 3: 2}

        def piece_part(j, which):
            part, c, _ = pieces[j]
            return part[which][:].rearrange("p c n -> p (c n)") if c is None else part[which][:, c, :]

        def piece_source(j):
            _, c, w = pieces[j]
            w = w.rearrange("(c p) n -> p c n", p=128)
            return w if c is None else w[:, c, :]

        def products(pe, out, a, b, start, stop):
            nc.tensor.matmul(out, a[0], b[0], start=start, stop=False)
            nc.tensor.matmul(out, a[0], b[1], start=False, stop=False)
            return nc.tensor.matmul(out, a[1], b[0], start=False, stop=stop)

        def run(eng, slot, tail):
            for g in range(NKV):
                slot(-1, 1, g, False, True)
            for b in range(2):
                for g in range(NKV):
                    slot(b, b % 2, g, True, True)
            with eng.Fori(1, B // 2 - 1) as pair:
                for p in range(2):
                    for g in range(NKV):
                        slot(2 * pair + p, p, g, True, True)
            for b in range(B - 2, B):
                for g in range(NKV):
                    slot(b, b % 2, g, True, b < B - 1)
            tail()


        def steps(eng, n, step):
            pairs = (n - 2) // 2 if n % 2 == 0 else (n - 3) // 2
            for i in range(2):
                step(i, i, i == 0, False)
            with eng.Fori(1, pairs) as pair:
                for p in range(2):
                    step(2 * pair + p, p, False, False)
            for i in range(2 * pairs, n):
                step(i, i % 2, False, i == n - 1)

        def through(i, p, each=16):
            return (each // 2) * (i - p) + each

        def column(t, i):
            return t[:, bass.ds(i, 1)]

        def layer(t, i):
            return t[:, bass.ds(i, 1), :].rearrange("p a n -> p (a n)")

        def rows(t, i):
            return t[bass.ds(i * 128, 128), :]

        def later_sp(sp):
            for c in range(4):
                if c >= 2:
                    sp.wait_ge(wo_lo, c - 1)
                sp.dma_start(wo_stage[c % 2][:].rearrange("p (h n) -> p h n", h=4),
                             wo.rearrange("(h p) n -> p h n", p=128)[:, 4 * c:4 * c + 4, :]).then_inc(wo_loaded[c % 2], 16)
            sp.dma_start(router_sb[:], router.rearrange("(c p) e -> p c e", p=128)).then_inc(b_consts, 16)

            def load_tile(i, p, first, last):
                wait(sp, at_lo, i)
                sp.dma_start(at_raw[:], attended[:, :, bass.ds(i * 128, 128)]).then_inc(at_loaded, 16)
                wait(sp, x_added, i)
                sp.dma_start(x_in[:], rows(x.rearrange("b s h -> (b s) h"), i)).then_inc(xin_loaded, 16)
                if not first:
                    store_h(i - 1, 1 - p)

            def store_h(i, p):
                sp.wait_ge(h_made, i + 1)
                sp.dma_start(rows(h_dram, i), h_out[p][:]).then_inc(h_stored[p], 16)
            steps(sp, NT, load_tile)
            store_h(NT - 1, (NT - 1) % 2)
            for n in range(3):
                sp.dma_start(shared_raw[:, n, :].rearrange("p (c n) -> p c n", c=KC),
                             shared_w[n].rearrange("(c p) n -> p c n", p=128)).then_inc(shared_loaded, 16)
            sp.wait_ge(zeroed, 1)
            for n in range(SLOTS):
                sp.dma_start(rows(xs_dram, n), zeros[:]).then_inc(rows_zeroed, 16)
            for p in range(2):
                sp.wait_ge(h_stored[p], 8 * NT)

            def load_h(i, p, first, last):
                if not first:
                    wait(sp, h2_turned, i - 1)
                    wait(sp, xs_made, i - 1)
                sp.dma_start(h_in[p][:], rows(h_dram, i)).then_inc(h_loaded[p], 16)
            steps(sp, NT, load_h)

            for p in range(2):
                sp.wait_ge(xs_stored[p], 8 * NT)
            sp.wait_ge(owners, 1)

            def load_block(j, p, first, last):
                expert = sp.value_load(owner_i[0:1, bass.ds(j, 1)], min_val=0, max_val=E - 1)
                if not first:
                    wait(sp, e_turned, j - 1)
                sp.dma_start(block_in[p][:], rows(xs_dram, j)).then_inc(block_loaded[p], 16)
                if not first:
                    wait(sp, e_down, j - 1)
                for n in range(3):
                    sp.dma_start(expert_sb[p][:, n], expert_w[n][bass.ds(expert, 1)].rearrange("a (c p) n -> p (a c) n", p=128)).then_inc(ew_loaded[p], 16)
                if not first:
                    store_y(j - 1, 1 - p)

            def store_y(j, p):
                sp.wait_ge(y_made, j + 1)
                sp.dma_start(rows(y_dram, j), y_out[p][:]).then_inc(y_stored[p], 16)
            steps(sp, SLOTS, load_block)
            store_y(SLOTS - 1, (SLOTS - 1) % 2)

            def store_out(i, p, first, last):
                sp.wait_ge(final_made, i + 1)
                sp.dma_start(rows(out.rearrange("b s h -> (b s) h"), i), gathered[p][:]).then_inc(out_stored[p], 16)
            steps(sp, NT, store_out)
            for p in range(2):
                sp.wait_ge(out_stored[p], 8 * NT)

        def later_pool(pool):
            pool.wait_ge(pv_done, 4 * B)
            nc.gpsimd.memset(ones[:], 1.0).then_inc(tables, 1)
            nc.gpsimd.memset(below[:], 1.0).then_inc(tables, 1)
            nc.gpsimd.memset(seen_b[:], 0.0).then_inc(tables, 1)
            nc.gpsimd.memset(zeros[:], 0.0).then_inc(zeroed, 1)
            nc.gpsimd.iota(iota_e[:], pattern=[[1, E]], base=0, channel_multiplier=0, allow_small_or_imprecise_dtypes=True).then_inc(tables, 1)
            nc.gpsimd.iota(slot_row[:], pattern=[[128, SLOTS]], base=0, channel_multiplier=0, allow_small_or_imprecise_dtypes=True).then_inc(tables, 1)
            pool.wait_ge(tables, 5)
            nc.gpsimd.affine_select(out=below[:], in_=below[:], compare_op=ALU.is_gt, fill=0.0, base=0,
                                    pattern=[[1, 128]], channel_multiplier=-1).then_inc(tables, 1)

            def rsqrt(i, p, first, last):
                pool.wait_ge(b_var, i + 1)
                nc.gpsimd.tensor_tensor(ln_rs128, ln_var128, minus_half[:, 0:1], ALU.pow).then_inc(b_rsqrt, 1)
            steps(pool, NT, rsqrt)
            pool.wait_ge(placed, 1)
            pool.wait_ge(rows_zeroed, 16 * SLOTS)

            def scatter(i, p, first, last):
                wait_apart(pool, pool_passed, xs_made, i + 1)
                nc.gpsimd.indirect_dma_start(out=xs_dram[:, :], out_offset=bass.IndirectOffsetOnAxis(ap=place_now[p][:, 0:1], axis=0),
                                             in_=xs_out[p][:], in_offset=None).then_inc(xs_stored[p], 16)
            steps(pool, NT, scatter)
            for p in range(2):
                pool.wait_ge(y_stored[p], 16 * ((SLOTS + 1 - p) // 2))

            def gather(i, p, first, last):
                if not first:
                    wait(pool, out_stored[p], through(i - 2, p))
                wait_apart(pool, pool_passed, now_copied, NT + i + 1)
                nc.gpsimd.indirect_dma_start(out=gathered[p][:], out_offset=None, in_=y_dram[:, :],
                                             in_offset=bass.IndirectOffsetOnAxis(ap=place_now[p][:, 0:1], axis=0)).then_inc(rows_gathered[p], 16)
            steps(pool, NT, gather)

        def later_act(act):
            for c in range(4):
                act.wait_ge(wo_loaded[c % 2], 16 * (c // 2 + 1))
                nc.scalar.copy(wide_part[0][:, c, :], wo_stage[c % 2][:]).then_inc(wo_hi, 1)

            def tile(i, p, first, last):
                act.wait_ge(at_loaded, 16 * (i + 1))
                if not first:
                    wait(act, projected, i - 1)
                nc.scalar.copy(at_part[p][0][:], at_raw[:]).then_inc(at_hi, 1)
                if not first:
                    copy_hT(i - 1)

            def copy_hT(i):
                act.wait_ge(h_turned, i + 1)
                nc.scalar.copy(hT_f[:].rearrange("p c n -> p (c n)"), turn_ps[:]).then_inc(hT_copied, 1)
            steps(act, NT, tile)
            copy_hT(NT - 1)
            act.wait_ge(best_done, 2 * NT)
            nc.scalar.activation(score[:], best[:], ACT.Sigmoid).then_inc(score_made, 1)
            for n in range(3):
                act.wait_ge(shared_loaded, 16 * 3)
                act.wait_ge(projected, NT)
                nc.scalar.copy(wide_part[0][:, n, :], shared_raw[:, n, :]).then_inc(shared_hi, 1)

            def hT_high(i):
                act.wait_ge(h2_turned, i + 1)
                nc.scalar.copy(hT_part[0][:].rearrange("p c n -> p (c n)"), turn_ps[:]).then_inc(hT_hi, 1)
            hT_high(0)

            def shared(i, p, first, last):
                act.wait_ge(gated, i + 1)
                wait(act, mid_made, i)
                nc.scalar.activation(gate_sb[:], score_ps[0][:], ACT.Silu).then_inc(silued, 1)
                if not last:
                    hT_high(i + 1)
                act.wait_ge(mid_turned, i + 1)
                nc.scalar.copy(mT_part[0][:].rearrange("p c n -> p (c n)"), pT_ps[0][:]).then_inc(mT_hi, 1)
            steps(act, NT, shared)

            def block_turned(j):
                act.wait_ge(e_turned, j + 1)
                nc.scalar.copy(blockT[:].rearrange("p c n -> p (c n)"), turn_ps[:]).then_inc(eT_copied, 1)
            block_turned(0)

            def block(j, p, first, last):
                act.wait_ge(e_gated, j + 1)
                wait(act, e_mid, j)
                nc.scalar.activation(egate_sb[:], score_ps[0][:], ACT.Silu).then_inc(e_silued, 1)
                if not last:
                    block_turned(j + 1)
                act.wait_ge(e_mid_turned, j + 1)
                nc.scalar.copy(emidT[:].rearrange("p c n -> p (c n)"), pT_ps[0][:]).then_inc(e_midT, 1)
            steps(act, SLOTS, block)

        def later_dve(dve):
            for c in range(4):
                dve.wait_ge(wo_hi, c + 1)
                nc.vector.tensor_tensor(wide_part[1][:, c, :], wo_stage[c % 2][:], wide_part[0][:, c, :].bitcast(F32),
                                        ALU.subtract).then_inc(wo_lo, 1)

            def low(i, p):
                dve.wait_ge(at_hi, i + 1)
                nc.vector.tensor_tensor(at_part[p][1][:], at_raw[:], at_part[p][0][:].bitcast(F32), ALU.subtract).then_inc(at_lo, 1)
            low(0, 0)
            dve.wait_ge(tables, 6)

            def tile(i, p, first, last):
                if not last:
                    low(i + 1, 1 - p)
                dve.wait_ge(projected, i + 1)
                dve.wait_ge(xin_loaded, 16 * (i + 1))
                nc.vector.tensor_tensor(x1[p][:], score_ps[p][:], x_in[:], ALU.add).then_inc(x_added, 1)
                dve.wait_ge(x_added, i + 1)
                nc.vector.bn_stats(bn128, x1[p][:]).then_inc(b_step, 1)
                wait_apart(dve, dve_passed, b_step, 2 * i + 1)
                nc.vector.bn_aggr(mv128, bn128).then_inc(b_step, 1)
                dve.wait_ge(b_step, 2 * i + 2)
                nc.vector.tensor_scalar(ln_var128, mv128[:, 1:2], LN_EPS, None, ALU.add).then_inc(b_var, 1)
                if not first:
                    route(i - 1)
                dve.wait_ge(b_rsqrt, i + 1)
                if not first:
                    wait(dve, h_stored[p], through(i - 2, p))
                    wait(dve, h_turned, i - 1)
                nc.vector.tensor_scalar(layer(acc, i), x1[p][:], 1.0, None, ALU.mult).then_inc(acc_made, 1)
                nc.vector.tensor_scalar(h_out[p][:], x1[p][:], mv128[:, 0:1], ln_rs128, ALU.subtract, ALU.mult).then_inc(h_made, 1)

            def route(i):
                dve.wait_ge(routed, i + 1)
                nc.vector.tensor_copy(logits[:], k_ps[:, 0:E]).then_inc(logits_out, 1)
                dve.wait_ge(tables, 6)
                dve.wait_ge(logits_out, i + 1)
                nc.vector.max(out=best8[:], in_=logits[:]).then_inc(best_done, 1)
                dve.wait_ge(best_done, 2 * i + 1)
                nc.vector.tensor_scalar(column(best, i), best8[:, 0:1], 1.0, None, ALU.mult).then_inc(best_done, 1)
                nc.vector.max_index(best_at[:], best8[:], logits[:]).then_inc(best_found, 1)
                dve.wait_ge(best_found, 2 * i + 1)
                nc.vector.tensor_copy(best_f[:], best_at[:, 0:1]).then_inc(best_found, 1)
                dve.wait_ge(best_found, 2 * i + 2)
                nc.vector.tensor_scalar(chosen_now[:], iota_e[:], best_f[:, 0:1], None, ALU.is_equal).then_inc(onehot, 1)
                dve.wait_ge(onehot, 3 * i + 1)
                nc.vector.tensor_copy(chosen_b[:], chosen_now[:]).then_inc(onehot, 1)
                nc.vector.tensor_scalar(layer(chosen, i), chosen_now[:], 1.0, None, ALU.mult).then_inc(chosen_kept, 1)
                dve.wait_ge(ranked, i + 1)
                nc.vector.tensor_tensor_reduce(spare[:], o_ps[:, 0:E], chosen_now[:], 1.0, 0.0, ALU.mult, ALU.add,
                                               rank_now[:]).then_inc(rank_out, 1)
                dve.wait_ge(rank_out, i + 1)
                nc.vector.tensor_scalar(column(rank, i), rank_now[:], 1.0, None, ALU.mult).then_inc(rank_kept, 1)
                nc.vector.tensor_tensor(seen_b[:], seen_b[:], chosen_b[:], ALU.add).then_inc(onehot, 1)
            steps(dve, NT, tile)
            route(NT - 1)

            step_no = [0]

            def done(ins):
                step_no[0] += 1
                ins.then_inc(plan, 1)
                dve.wait_ge(plan, step_no[0])

            dve.wait_ge(counted, 1)
            dve.wait_ge(rank_kept, NT)
            dve.wait_ge(chosen_kept, NT)
            dve.wait_ge(acc_made, NT)
            done(nc.vector.tensor_scalar(spare[:], o_ps[:, 0:E], 127.0, None, ALU.add))
            done(nc.vector.tensor_copy(count_i[:, 0, :], spare[:]))
            done(nc.vector.tensor_single_scalar(count_i[:, 1, :], count_i[:, 0, :], 7, ALU.arith_shift_right))
            done(nc.vector.tensor_copy(spare[:], count_i[:, 1, :]))
            done(nc.vector.tensor_scalar(padded[:], spare[:], 128.0, None, ALU.mult))
            done(nc.vector.memset(start[:], 0.0))
            for e in range(E):
                done(nc.vector.tensor_tensor(start[:, e + 1:e + 2], start[:, e:e + 1], padded[:, e:e + 1], ALU.add))
            done(nc.vector.tensor_tensor(places[:], chosen[:], start[:, 0:E].rearrange("p (a e) -> p a e", a=1).broadcast_to([128, NT, E]), ALU.mult))
            done(nc.vector.tensor_reduce(place[:], places[:], AX_X, ALU.add))
            done(nc.vector.tensor_tensor(place[:], place[:], rank[:], ALU.add))
            nc.vector.tensor_copy(place_i[:], place[:]).then_inc(placed, 1)
            done(nc.vector.memset(owner[:], 0.0))
            for e in range(1, E):
                done(nc.vector.scalar_tensor_tensor(out=owner[:, e % 2, :], in0=slot_row[:], scalar=start[:, e:e + 1], in1=owner[:, (e - 1) % 2, :],
                                                    op0=ALU.is_ge, op1=ALU.add))
            nc.vector.tensor_copy(owner_i[:], owner[:, (E - 1) % 2, :]).then_inc(owners, 1)

            for n in range(3):
                dve.wait_ge(shared_hi, n + 1)
                nc.vector.tensor_tensor(wide_part[1][:, n, :], shared_raw[:, n, :], wide_part[0][:, n, :].bitcast(F32),
                                        ALU.subtract).then_inc(shared_lo, 1)
            dve.wait_ge(placed, 1)
            dve.wait_ge(score_made, 1)

            def hT_low(i):
                dve.wait_ge(hT_hi, i + 1)
                nc.vector.tensor_tensor(hT_part[1][:].rearrange("p c n -> p (c n)"), turn_ps[:],
                                        hT_part[0][:].rearrange("p c n -> p (c n)").bitcast(F32), ALU.subtract).then_inc(hT_lo, 1)
            hT_low(0)

            def add_shared(i):
                dve.wait_ge(shared_out, i + 1)
                nc.vector.tensor_tensor(layer(acc, i), o_ps[:], layer(acc, i), ALU.add).then_inc(shared_added, 1)

            def shared(i, p, first, last):
                dve.wait_ge(placed, 1)
                dve.wait_ge(h_loaded[p], through(i, p))
                if not first:
                    wait(dve, xs_stored[p], through(i - 2, p))
                nc.vector.tensor_copy(place_now[p][:], column(place_i, i)).then_inc(now_copied, 1)
                nc.vector.tensor_scalar(xs_out[p][:], h_in[p][:], column(score, i), None, ALU.mult).then_inc(xs_made, 1)
                dve.wait_ge(upped, i + 1)
                dve.wait_ge(silued, i + 1)
                wait(dve, mid_turned, i)
                nc.vector.tensor_tensor(mid_sb[:], score_ps[1][:], gate_sb[:], ALU.mult).then_inc(mid_made, 1)
                if not last:
                    hT_low(i + 1)
                if not first:
                    add_shared(i - 1)
                dve.wait_ge(mT_hi, i + 1)
                nc.vector.tensor_tensor(mT_part[1][:].rearrange("p c n -> p (c n)"), pT_ps[0][:],
                                        mT_part[0][:].rearrange("p c n -> p (c n)").bitcast(F32), ALU.subtract).then_inc(mT_lo, 1)
            steps(dve, NT, shared)
            add_shared(NT - 1)

            def out_y(j, p):
                dve.wait_ge(e_down, j + 1)
                if not (isinstance(j, int) and j < 2):
                    dve.wait_ge(y_stored[p], through(j - 2, p))
                nc.vector.tensor_copy(y_out[p][:], o_ps[:]).then_inc(y_made, 1)

            def block(j, p, first, last):
                dve.wait_ge(e_upped, j + 1)
                dve.wait_ge(e_silued, j + 1)
                wait(dve, e_mid_turned, j)
                nc.vector.tensor_tensor(emid_sb[:], score_ps[1][:], egate_sb[:], ALU.mult).then_inc(e_mid, 1)
                if not first:
                    out_y(j - 1, 1 - p)
            steps(dve, SLOTS, block)
            out_y(SLOTS - 1, (SLOTS - 1) % 2)

            def place_of(i, p):
                dve.wait_ge(placed, 1)
                if not (isinstance(i, int) and i < 2):
                    dve.wait_ge(rows_gathered[p], through(i - 2, p))
                nc.vector.tensor_copy(place_now[p][:], column(place_i, i)).then_inc(now_copied, 1)

            def finish(i, p, first, last):
                if first:
                    for q in range(2):
                        dve.wait_ge(xs_stored[q], 8 * NT)
                    place_of(0, 0)
                if not last:
                    place_of(i + 1, 1 - p)
                dve.wait_ge(rows_gathered[p], through(i, p))
                nc.vector.tensor_tensor(gathered[p][:], layer(acc, i), gathered[p][:], ALU.add).then_inc(final_made, 1)
            steps(dve, NT, finish)

        def later_pe(pe):
            pe.wait_ge(wo_lo, 4)
            pe.wait_ge(b_consts, 16)
            pe.wait_ge(tables, 6)

            def tile(i, p, first, last):
                pe.wait_ge(at_lo, i + 1)
                if not first:
                    wait(pe, x_added, i - 1)
                for h in range(NH):
                    ins = products(pe, score_ps[p][:], [a[:, h, :] for a in at_part[p]],
                                   [w[:, h // 4, (h % 4) * H:(h % 4 + 1) * H] for w in wide_part], h == 0, h == NH - 1)
                ins.then_inc(projected, 1)
                if not first:
                    route(i - 1, 1 - p, False)

            def route(i, p, last):
                pe.wait_ge(h_made, i + 1)
                for c in range(KC):
                    ins = nc.tensor.transpose(turn_ps[:, c * 128:(c + 1) * 128], h_out[p][:, c * 128:(c + 1) * 128], ident[:])
                ins.then_inc(h_turned, 1)
                pe.wait_ge(hT_copied, i + 1)
                wait(pe, logits_out, i)
                for c in range(KC):
                    ins = nc.tensor.matmul(k_ps[:, 0:E], hT_f[:, c, :], router_sb[:, c, :], start=(c == 0), stop=(c == KC - 1))
                ins.then_inc(routed, 1)
                pe.wait_ge(onehot, 3 * i + 2)
                wait(pe, rank_out, i)
                nc.tensor.matmul(o_ps[:, 0:E], below[:], chosen_b[:], start=True, stop=False)
                nc.tensor.matmul(o_ps[:, 0:E], ones[:], seen_b[:], start=False, stop=True).then_inc(ranked, 1)
                if last:
                    pe.wait_ge(onehot, 3 * NT)
                    nc.tensor.matmul(o_ps[:, 0:E], ones[:], seen_b[:], start=True, stop=True).then_inc(counted, 1)
            steps(pe, NT, tile)
            route(NT - 1, (NT - 1) % 2, True)

            def turn_h(i, p):
                pe.wait_ge(h_loaded[p], through(i, p))
                wait(pe, hT_lo, i)
                for c in range(KC):
                    ins = nc.tensor.transpose(turn_ps[:, c * 128:(c + 1) * 128], h_in[p][:, c * 128:(c + 1) * 128], ident[:])
                ins.then_inc(h2_turned, 1)
            turn_h(0, 0)
            pe.wait_ge(shared_lo, 3)
            pe.wait_ge(plan, 6)

            def weights(n):
                return [w[:, n, :].rearrange("p (c n) -> p c n", c=KC) for w in wide_part]

            def shared_down(i):
                pe.wait_ge(mT_lo, i + 1)
                wait(pe, shared_added, i)
                for c in range(FC):
                    ins = products(pe, o_ps[:], [m[:, c, :] for m in mT_part], [w[:, c, :] for w in weights(2)], c == 0, c == FC - 1)
                ins.then_inc(shared_out, 1)

            def shared(i, p, first, last):
                pe.wait_ge(hT_lo, i + 1)
                wait(pe, mid_made, i)
                for n, done in ((0, gated), (1, upped)):
                    for c in range(KC):
                        ins = products(pe, score_ps[n][:], [t[:, c, :] for t in hT_part], [w[:, c, :] for w in weights(n)],
                                       c == 0, c == KC - 1)
                    ins.then_inc(done, 1)
                if not last:
                    turn_h(i + 1, 1 - p)
                if not first:
                    shared_down(i - 1)
                pe.wait_ge(mid_made, i + 1)
                wait(pe, mT_lo, i)
                for c in range(FC):
                    ins = nc.tensor.transpose(pT_ps[0][:, c * 128:(c + 1) * 128], mid_sb[:, c * 128:(c + 1) * 128], ident[:])
                ins.then_inc(mid_turned, 1)
            steps(pe, NT, shared)
            shared_down(NT - 1)

            def turn_block(j, p):
                pe.wait_ge(block_loaded[p], through(j, p))
                wait(pe, eT_copied, j)
                for c in range(KC):
                    ins = nc.tensor.transpose(turn_ps[:, c * 128:(c + 1) * 128], block_in[p][:, c * 128:(c + 1) * 128], ident[:])
                ins.then_inc(e_turned, 1)
            turn_block(0, 0)

            def down(j, p):
                pe.wait_ge(e_midT, j + 1)
                if isinstance(j, int) and j == 0:
                    pe.wait_ge(shared_added, NT)
                wait(pe, y_made, j)
                for c in range(FC):
                    ins = nc.tensor.matmul(o_ps[:], emidT[:, c, :], expert_sb[p][:, 2, c, :], start=(c == 0), stop=(c == FC - 1))
                ins.then_inc(e_down, 1)

            def block(j, p, first, last):
                pe.wait_ge(eT_copied, j + 1)
                pe.wait_ge(ew_loaded[p], through(j, p, 48))
                wait(pe, e_mid, j)
                for n, done in ((0, e_gated), (1, e_upped)):
                    for c in range(KC):
                        ins = nc.tensor.matmul(score_ps[n][:], blockT[:, c, :], expert_sb[p][:, n, c, :], start=(c == 0), stop=(c == KC - 1))
                    ins.then_inc(done, 1)
                if not first:
                    down(j - 1, 1 - p)
                if not last:
                    turn_block(j + 1, 1 - p)
                pe.wait_ge(e_mid, j + 1)
                for c in range(FC):
                    ins = nc.tensor.transpose(pT_ps[0][:, c * 128:(c + 1) * 128], emid_sb[:, c * 128:(c + 1) * 128], ident[:])
                ins.then_inc(e_mid_turned, 1)
            steps(pe, SLOTS, block)
            down(SLOTS - 1, (SLOTS - 1) % 2)

        block = outer.enter_context(nc.Block())

        @block.sync
        def _(sp):
            sp.dma_start(ctx_raw[:], ctxT[0]).then_inc(ctx_loaded, 16)
            for j in range(len(pieces)):
                if j >= 2:
                    sp.wait_ge(w_lo, j - 1)
                dst = stage[j % 2][:] if pieces[j][1] is not None else stage[j % 2][:].rearrange("p (c n) -> p c n", c=KC)
                sp.dma_start(dst, piece_source(j)).then_inc(stage_loaded[j % 2], 16)
                if j == 1:
                    sp.dma_start(x_sb[:], x[0]).then_inc(x_loaded, 16)
                    for dst, src in ((bk_sb, bk_rows), (bq_sb, bq_rows), (bv_sb, bv_cols), (qw_sb, qn_col), (kw_sb, kn_col)):
                        sp.dma_start(dst[:], src).then_inc(consts_loaded, 16)
                    sp.dma_start(mask_sb[:], mask).then_inc(mask_loaded, 16)

            def store(b, g, s):
                sp.wait_ge(o_made, s + 1)
                sp.dma_start(attended[:, g * G:(g + 1) * G, bass.ds(b * S, S)],
                             o_sb[:].rearrange("p (h n) -> p h n", h=G)).then_inc(o_stored, 16)

            def load(dst, src, b, to):
                at = src[b] if isinstance(b, int) else src[bass.ds(b, 1)].rearrange(
                    "a p n -> (a p) n" if len(src.shape) == 3 else "a p c n -> p (a c) n")
                sp.dma_start(dst, at).then_inc(to, 16)

            def slot(b, p, g, attend, ahead):
                s = 4 * b + g
                if attend and not (isinstance(s, int) and s == 0):
                    store(b if g else b - 1, (g - 1) % NKV, s - 1)
                if g == 3:
                    if not isinstance(b, int) or b + 2 < B:
                        sp.wait_ge(x_turned, b + 2)
                        load(x_sb[:], x, b + 2, x_loaded)
                if g == 0 and (not isinstance(b, int) or b + 2 < B):
                    sp.wait_ge(ctx_lo, b + 2)
                    load(ctx_raw[:], ctxT, b + 2, ctx_loaded)

            def tail():
                store(B - 1, NKV - 1, 4 * B - 1)
                sp.wait_ge(o_stored, 16 * 4 * B)
            run(sp, slot, tail)
            later_sp(sp)

        @block.gpsimd
        def _(pool):
            nc.gpsimd.memset(minus_half[:], -0.5).then_inc(made, 1)
            for p in range(2):
                for part in kT_part[p]:
                    nc.gpsimd.memset(part[:, :, SE:SE_EVEN].bitcast(F32), 0.0).then_inc(key_padded, 1)
            nc.gpsimd.memset(ident[:], 0.0).then_inc(ident_zeroed, 1)
            pool.wait_ge(ident_zeroed, 1)
            nc.gpsimd.affine_select(out=ident[:], in_=ident[:], compare_op=ALU.not_equal, fill=1.0, base=0,
                                    pattern=[[-1, 128]], channel_multiplier=1).then_inc(ident_made, 1)
            pool.wait_ge(made, 1)

            def split_ctx(c):
                pool.wait_ge(ctx_hi, c + 1)
                nc.gpsimd.tensor_tensor(ctx_part[1][:], ctx_raw[:], ctx_part[0][:].bitcast(F32), ALU.subtract).then_inc(ctx_lo, 1)
            split_ctx(0)

            def slot(b, p, g, attend, ahead):
                s1, b1 = 4 * b + g + 1, b + 1
                if (g == 3 and ahead) or (g < 3 and attend):
                    pool.wait_ge(q_mean, s1 + 1)
                    nc.gpsimd.tensor_tensor(q_rs, q_ms, minus_half[0:S, :], ALU.pow).then_inc(q_rsqrt, 1)
                if ahead and g < 3:
                    pool.wait_ge(k_mean, 3 * b1 + g + 1)
                    nc.gpsimd.tensor_tensor(k_rs, k_ms, minus_half[0:TK, :], ALU.pow).then_inc(k_rsqrt, 1)
                if ahead and g == 0:
                    pool.wait_ge(ln_stats, b1 + 1)
                    nc.gpsimd.tensor_tensor(ln_rs, ln_var, minus_half[0:S, 0:1], ALU.pow).then_inc(ln_rsqrt, 1)
                if g == 3 and (not isinstance(b, int) or b + 2 < B):
                    split_ctx(b + 2)
            run(pool, slot, lambda: None)
            later_pool(pool)

        @block.scalar
        def _(act):
            for j in range(len(pieces)):
                act.wait_ge(stage_loaded[j % 2], 16 * (j // 2 + 1))
                nc.scalar.copy(piece_part(j, 0), stage[j % 2][:]).then_inc(w_hi, 1)

            def square(source, sums, rows, done, count, other, other_count):
                wait(act, done, count - 1)
                wait(act, other, other_count)
                for h in range(G):
                    at = slice(h * HD, (h + 1) * HD)
                    last = nc.scalar.activation(squares[0:rows, at], source[:, at], ACT.Square, accum_out=sums[:, h:h + 1])
                last.then_inc(done, 1)

            def slot(b, p, g, attend, ahead):
                s, s1, b1 = 4 * b + g, 4 * b + g + 1, b + 1
                next_q = (g == 3 and ahead) or (g < 3 and attend)
                if attend:
                    act.wait_ge(negated, s + 1)
                    for h in range(G):
                        nc.scalar.activation(probs[:, h, :], probs[:, h, :], ACT.Exp, bias=neg_top[:, h:h + 1],
                                             accum_out=total[:, h:h + 1]).then_inc(exped, 1)
                if ahead and g > 0:
                    n = 3 * b1 + g
                    act.wait_ge(k_turned, n)
                    at = slice((g - 1) * TK, g * TK)
                    nc.scalar.activation(kT_part[1 - p][0][:, :, at], turn_ps[:, 0:NKV * TK].rearrange("p (h n) -> p h n", h=NKV),
                                         ACT.Copy, scale=kw_sb[:, 0:1]).then_inc(kT_hi, 1)
                if next_q:
                    act.wait_ge(q_biased, s1 + 1)
                    square(q_sb, q_ss, S, q_squared, s1 + 1, k_squared, 3 * b1 + g * ahead)
                if ahead and g < 3:
                    act.wait_ge(k_biased, 3 * b1 + g + 1)
                    square(k_sb, k_ss, TK, k_squared, 3 * b1 + g + 1, q_squared, s1 + 1)
                if g == 0:
                    attended(attend, s, g)
                if ahead and g in V_TILE:
                    t = V_TILE[g]
                    act.wait_ge(v_proj, 3 * b1 + t + 1)
                    nc.scalar.copy(v_part[1 - p][0][:, t, :], qv_ps[0:TK, :]).then_inc(v_hi, 1)
                if ahead and g == 2:
                    act.wait_ge(x_turned, b1 + 1)
                    nc.scalar.copy(xT_part[0][:].rearrange("p c n -> p (c n)"), turn_ps[:, 0:KC * S]).then_inc(xT_hi, 1)
                if g > 0:
                    attended(attend, s, g)
                if next_q:
                    act.wait_ge(q_turned, s1 + 1)
                    nc.scalar.activation(qT_part[0][:], turn_ps[:, 0:G * S], ACT.Copy, scale=qws[:, 0:1]).then_inc(qT_hi, 1)
                if attend:
                    for t in range(KT):
                        act.wait_ge(p_turned, 3 * s + t + 1)
                        nc.scalar.copy(pT_part[0][:, t, :], pT_ps[(3 * g + t) % 2][0:TK, 0:G * S]).then_inc(pT_hi, 1)

            def attended(attend, s, g):
                if attend and not (isinstance(s, int) and s == 0):
                    out_of(s - 1, (g - 1) % NKV)

            def out_of(s, g):
                act.wait_ge(pv_done, s + 1)
                wait(act, o_stored, 16 * s)
                nc.scalar.activation(o_sb[:], o_ps[:, 0:G * S], ACT.Identity, bias=bv_sb[:, g:g + 1]).then_inc(o_made, 1)
            run(act, slot, lambda: out_of(4 * B - 1, NKV - 1))
            later_act(act)

        @block.vector
        def _(dve):
            def split_ctx(c):
                dve.wait_ge(ctx_loaded, 16 * (c + 1))
                wait(dve, v_proj, 3 * c)
                nc.vector.tensor_copy(ctx_part[0][:], ctx_raw[:]).then_inc(ctx_hi, 1)
            split_ctx(0)
            for j in range(len(pieces)):
                dve.wait_ge(w_hi, j + 1)
                nc.vector.tensor_tensor(piece_part(j, 1), stage[j % 2][:], piece_part(j, 0).bitcast(F32), ALU.subtract).then_inc(w_lo, 1)
            dve.wait_ge(consts_loaded, 16 * 5)
            dve.wait_ge(mask_loaded, 16)
            nc.vector.tensor_scalar(qws[:], qw_sb[:], HD ** -0.5, None, ALU.mult).then_inc(qws_made, 1)
            dve.wait_ge(qws_made, 1)

            def scaled(rows, scales, done):
                for h in range(G):
                    at = slice(h * HD, (h + 1) * HD)
                    last = nc.vector.tensor_scalar(rows[:, at], rows[:, at], scales[:, h:h + 1], None, ALU.mult)
                last.then_inc(done, 1)

            def slot(b, p, g, attend, ahead):
                s, s1, b1 = 4 * b + g, 4 * b + g + 1, b + 1
                next_q = (g == 3 and ahead) or (g < 3 and attend)
                if attend:
                    for h in range(G):
                        wait_apart(dve, dve_passed, scored, 4 * s + h + 1)
                        nc.vector.tensor_tensor_reduce(probs[:, h, :], score_ps[h % 2][0:S, 0:SE], mask_sb[:], 1.0, LOWEST,
                                                       ALU.add, ALU.max, top[:, h:h + 1]).then_inc(masked, 1)
                    dve.wait_ge(masked, 4 * s + 4)
                    nc.vector.tensor_scalar(neg_top, top, -1.0, None, ALU.mult).then_inc(negated, 1)
                if ahead and g > 0:
                    n = 3 * b1 + g
                    dve.wait_ge(kT_hi, n)
                    at = slice((g - 1) * TK, g * TK)
                    nc.vector.scalar_tensor_tensor(out=kT_part[1 - p][1][:, :, at], in0=turn_ps[:, 0:NKV * TK].rearrange("p (h n) -> p h n", h=NKV),
                                                   scalar=kw_sb[:, 0:1], in1=kT_part[1 - p][0][:, :, at].bitcast(F32),
                                                   op0=ALU.mult, op1=ALU.subtract).then_inc(kT_lo, 1)
                if next_q:
                    dve.wait_ge(q_proj, s1 + 1)
                    gq = (g + 1) % NKV
                    nc.vector.tensor_tensor(q_sb[:], qv_ps[0:S, :], bq_sb[:, gq * G * HD:(gq + 1) * G * HD], ALU.add).then_inc(q_biased, 1)
                if attend:
                    dve.wait_ge(exped, 4 * s + 4)
                    nc.vector.reciprocal(inv_total, total).then_inc(inverted, 1)
                    dve.wait_ge(inverted, s + 1)
                    for h in range(G):
                        last = nc.vector.tensor_scalar(probs[:, h, :], probs[:, h, :], inv_total[:, h:h + 1], None, ALU.mult)
                    last.then_inc(p_normed, 1)
                if next_q:
                    dve.wait_ge(q_squared, s1 + 1)
                    nc.vector.tensor_scalar(q_ms, q_ss, 1.0 / HD, RMS_EPS, ALU.mult, ALU.add).then_inc(q_mean, 1)
                if ahead and g < 3:
                    dve.wait_ge(k_proj, 3 * b1 + g + 1)
                    nc.vector.tensor_tensor(k_sb[:], k_ps[0:TK, :], bk_sb[:], ALU.add).then_inc(k_biased, 1)
                    dve.wait_ge(k_squared, 3 * b1 + g + 1)
                    nc.vector.tensor_scalar(k_ms, k_ss, 1.0 / HD, RMS_EPS, ALU.mult, ALU.add).then_inc(k_mean, 1)
                if ahead and g == 0:
                    dve.wait_ge(x_loaded, 16 * (b1 + 1))
                    nc.vector.bn_stats(bn, x_sb[:]).then_inc(ln_step, 1)
                    wait_apart(dve, dve_passed, ln_step, 2 * b1 + 1)
                    nc.vector.bn_aggr(mv, bn).then_inc(ln_step, 1)
                    dve.wait_ge(ln_step, 2 * b1 + 2)
                    nc.vector.tensor_scalar(ln_var, mv[:, 1:2], LN_EPS, None, ALU.add).then_inc(ln_stats, 1)
                if ahead and g == 1:
                    dve.wait_ge(ln_rsqrt, b1 + 1)
                    nc.vector.tensor_scalar(x_sb[:], x_sb[:], mv[:, 0:1], ln_rs, ALU.subtract, ALU.mult).then_inc(x_normed, 1)
                if next_q:
                    dve.wait_ge(q_rsqrt, s1 + 1)
                    scaled(q_sb, q_rs, q_normed)
                if ahead and g in V_TILE:
                    t = V_TILE[g]
                    dve.wait_ge(v_hi, 3 * b1 + t + 1)
                    nc.vector.tensor_tensor(v_part[1 - p][1][:, t, :], qv_ps[0:TK, :], v_part[1 - p][0][:, t, :].bitcast(F32),
                                            ALU.subtract).then_inc(v_lo, 1)
                if g == 3 and (not isinstance(b, int) or b + 2 < B):
                    split_ctx(b + 2)
                if ahead and g == 2:
                    dve.wait_ge(xT_hi, b1 + 1)
                    nc.vector.tensor_tensor(xT_part[1][:].rearrange("p c n -> p (c n)"), turn_ps[:, 0:KC * S],
                                            xT_part[0][:].rearrange("p c n -> p (c n)").bitcast(F32), ALU.subtract).then_inc(xT_lo, 1)
                if ahead and g < 3:
                    dve.wait_ge(k_rsqrt, 3 * b1 + g + 1)
                    scaled(k_sb, k_rs, k_normed)
                if next_q:
                    dve.wait_ge(qT_hi, s1 + 1)
                    nc.vector.scalar_tensor_tensor(out=qT_part[1][:], in0=turn_ps[:, 0:G * S], scalar=qws[:, 0:1],
                                                   in1=qT_part[0][:].bitcast(F32), op0=ALU.mult, op1=ALU.subtract).then_inc(qT_lo, 1)
                if attend:
                    for t in range(KT):
                        dve.wait_ge(pT_hi, 3 * s + t + 1)
                        nc.vector.tensor_tensor(pT_part[1][:, t, :], pT_ps[(3 * g + t) % 2][0:TK, 0:G * S],
                                                pT_part[0][:, t, :].bitcast(F32), ALU.subtract).then_inc(pT_lo, 1)
            run(dve, slot, lambda: None)
            later_dve(dve)

        @block.tensor
        def _(pe):
            pe.wait_ge(ident_made, 1)
            pe.wait_ge(key_padded, 4)

            def pv(b, s, g, p):
                pe.wait_ge(pT_lo, 3 * s + 3)
                pe.wait_ge(v_lo, 3 * b + 3)
                wait(pe, o_made, s)
                for t in range(KT):
                    v = [v_part[p][i][:, t, g * HD:(g + 1) * HD] for i in range(2)]
                    pT = [pT_part[i][:, t, :] for i in range(2)]
                    last = products(pe, o_ps[:, 0:G * S], v, pT, t == 0, t == KT - 1)
                last.then_inc(pv_done, 1)

            def slot(b, p, g, attend, ahead):
                s, s1, b1 = 4 * b + g, 4 * b + g + 1, b + 1
                next_q = (g == 3 and ahead) or (g < 3 and attend)
                if attend:
                    pe.wait_ge(qT_lo, s + 1)
                    if g == 0:
                        pe.wait_ge(kT_lo, 3 * b + 3)
                    for h in range(G):
                        wait(pe, masked, 4 * s + h - 1)
                        products(pe, score_ps[h % 2][0:S, 0:SE_EVEN], [q[:, h * S:(h + 1) * S] for q in qT_part],
                                 [k[:, g, :] for k in kT_part[p]], True, True).then_inc(scored, 1)
                if ahead and g > 0:
                    pe.wait_ge(k_normed, 3 * b1 + g)
                    wait(pe, qT_lo, s + 1)
                    if g == 3:
                        pe.wait_ge(xT_lo, b1 + 1)
                    for h in range(NKV):
                        last = nc.tensor.transpose(turn_ps[:, h * TK:(h + 1) * TK], k_sb[:, h * HD:(h + 1) * HD], ident[0:TK, 0:TK])
                    last.then_inc(k_turned, 1)
                if next_q:
                    pe.wait_ge(xT_lo, b1 + 1 if g == 3 else b + 1)
                    wait(pe, v_lo, 3 * b1 + V_BEFORE[g] if ahead else 3 * b1)
                    if isinstance(b, int) and b < 0:
                        pe.wait_ge(w_lo, Q_PIECE)
                    gq = (g + 1) % NKV
                    for c in range(KC):
                        last = products(pe, qv_ps[0:S, :], [xT[:, c, :] for xT in xT_part],
                                        [w[:, c, gq * G * HD:(gq + 1) * G * HD] for w in wq_part], c == 0, c == KC - 1)
                    last.then_inc(q_proj, 1)
                if ahead and g < 3:
                    pe.wait_ge(ctx_lo, b1 + 1)
                    if isinstance(b, int) and b < 0:
                        pe.wait_ge(w_lo, K_PIECE)
                    wait(pe, k_biased, 3 * b1 + g)
                    for c in range(KC):
                        last = products(pe, k_ps[0:TK, :], [a[:, c, g * TK:(g + 1) * TK] for a in ctx_part],
                                        [w[:, c, :] for w in wk_part], c == 0, c == KC - 1)
                    last.then_inc(k_proj, 1)
                if g == 0 and attend and not (isinstance(s, int) and s == 0):
                    pv(b - 1, s - 1, NKV - 1, 1 - p)
                if ahead and g in V_TILE:
                    t = V_TILE[g]
                    if isinstance(b, int) and b < 0:
                        pe.wait_ge(w_lo, V_PIECE)
                        wait(pe, v_lo, 3 * b1 + t)
                    wait(pe, q_biased, s1 + 1)
                    for c in range(KC):
                        last = products(pe, qv_ps[0:TK, :], [a[:, c, t * TK:(t + 1) * TK] for a in ctx_part],
                                        [w[:, c, :] for w in wv_part], c == 0, c == KC - 1)
                    last.then_inc(v_proj, 1)
                if ahead and g == 2:
                    pe.wait_ge(x_normed, b1 + 1)
                    wait(pe, kT_lo, 3 * b1 + g)
                    for c in range(KC):
                        last = nc.tensor.transpose(turn_ps[:, c * S:(c + 1) * S], x_sb[:, c * 128:(c + 1) * 128], ident[0:S, 0:S])
                    last.then_inc(x_turned, 1)
                if g > 0 and attend:
                    pv(b, s - 1, g - 1, p)
                if next_q:
                    pe.wait_ge(q_normed, s1 + 1)
                    if ahead and g > 0:
                        pe.wait_ge(kT_lo, 3 * b1 + g)
                    if ahead and g == 2:
                        pe.wait_ge(xT_lo, b1 + 1)
                    for h in range(G):
                        last = nc.tensor.transpose(turn_ps[:, h * S:(h + 1) * S], q_sb[:, h * HD:(h + 1) * HD], ident[0:S, 0:S])
                    last.then_inc(q_turned, 1)
                if attend:
                    pe.wait_ge(p_normed, s + 1)
                    for t in range(KT):
                        wait(pe, pT_lo, 3 * s + t - 1)
                        for h in range(G):
                            last = nc.tensor.transpose(pT_ps[(3 * g + t) % 2][0:TK, h * S:(h + 1) * S],
                                                       probs[:, h, t * TK:(t + 1) * TK], ident[0:S, 0:S])
                        last.then_inc(p_turned, 1)
            run(pe, slot, lambda: pv(B - 1, 4 * B - 1, NKV - 1, 1))
            later_pe(pe)


def kernel(x, ctx_2048, mask_1xSxS2_ff0, L0_xattn_Wq, L0_xattn_bq, L0_xattn_Wk, L0_xattn_bk, L0_xattn_Wv, L0_xattn_bv,
           L0_xattn_Wo, L0_xattn_qn_w, L0_xattn_kn_w, L0_ffn_router_w, L0_ffn_gate_w, L0_ffn_up_w, L0_ffn_down_w,
           L0_ffn_shared_gate_w, L0_ffn_shared_up_w, L0_ffn_shared_down_w):
    import concourse.bacc as bacc
    from concourse.bass_utils import run_bass_kernel_spmd

    ctx = np.asarray(ctx_2048)
    laid = {
        "x": np.asarray(x),
        "ctxT": ctx.reshape(B, SE, KC, 128).transpose(0, 3, 2, 1),
        "mask": np.asarray(mask_1xSxS2_ff0)[0],
        "wq": np.asarray(L0_xattn_Wq),
        "bq_rows": np.broadcast_to(np.asarray(L0_xattn_bq), (S, NH * HD)),
        "wk": np.asarray(L0_xattn_Wk),
        "bk_rows": np.broadcast_to(np.asarray(L0_xattn_bk), (TK, NKV * HD)),
        "wv": np.asarray(L0_xattn_Wv),
        "bv_cols": np.asarray(L0_xattn_bv).reshape(NKV, HD).T,
        "qn_col": np.asarray(L0_xattn_qn_w).reshape(HD, 1),
        "kn_col": np.asarray(L0_xattn_kn_w).reshape(HD, 1),
        "wo": np.asarray(L0_xattn_Wo),
        "router": np.asarray(L0_ffn_router_w),
        "expert_gate": np.asarray(L0_ffn_gate_w),
        "expert_up": np.asarray(L0_ffn_up_w),
        "expert_down": np.asarray(L0_ffn_down_w),
        "shared_gate": np.asarray(L0_ffn_shared_gate_w),
        "shared_up": np.asarray(L0_ffn_shared_up_w),
        "shared_down": np.asarray(L0_ffn_shared_down_w),
    }
    laid = {name: np.ascontiguousarray(a) for name, a in laid.items()}
    nc = bacc.Bacc("TRN2", target_bir_lowering=False, num_devices=1)
    t = {name: nc.dram_tensor(name, a.shape, mybir.dt.from_np(a.dtype), kind="ExternalInput").ap() for name, a in laid.items()}
    out = nc.dram_tensor("out", (B, S, H), F32, kind="ExternalOutput").ap()
    xattn_ffn_kernel(nc, *[t[n] for n in ("x", "ctxT", "mask", "wq", "bq_rows", "wk", "bk_rows", "wv", "bv_cols", "qn_col", "kn_col", "wo", "router")],
                     [t["expert_gate"], t["expert_up"], t["expert_down"]], [t["shared_gate"], t["shared_up"], t["shared_down"]], out)
    result = run_bass_kernel_spmd(nc, [laid], core_ids=[0])
    return result.results[0]["out"]
```

```python
from contextlib import ExitStack

import numpy as np
import concourse.bass as bass
from concourse import mybir

F32 = mybir.dt.float32
F32R = mybir.dt.float32r
BF16 = mybir.dt.bfloat16
I32 = mybir.dt.int32
U32 = mybir.dt.uint32
ALU = mybir.AluOpType
ACT = mybir.ActivationFunctionType
AX_X = mybir.AxisListType.X

B, S, H = 16, 112, 512
SE = 375
NH, NKV, HD = 16, 4, 128
G = NH // NKV
KC = H // 128
KT = 3
TK = SE // KT
SE_EVEN = SE + SE % 2
LN_EPS, RMS_EPS = 1e-5, 1e-6
TOK = B * S
NT = TOK // 128
F = 512
FC = F // 128
E = 8
SLOTS = (TOK - E) // 128 + E
HELD_FIRST, EARLY = 3, 3
GATHERS = 4
PIECE = 2048
LOWEST = -3.0e38


def held_at(e):
    return (e + HELD_FIRST) % E


def wait(eng, sem, value):
    if not isinstance(value, int) or value > 0:
        eng.wait_ge(sem, value)


def wait_apart(eng, passed, sem, value):
    eng.wait_ge(sem, value)
    eng.sem_inc(passed, 1)


def xattn_ffn_kernel(nc, x, ctxT, mask, wq, bq_rows, wk, bk_rows, wv, bv_cols, qn_col, kn_col, wo,
                     router, expert_w, shared_w, out):
    with ExitStack() as outer:
        def sb(name, shape, dt=F32, into=outer):
            return into.enter_context(nc.sbuf_tensor(name, shape, dt))

        def psum(name, shape, dt=F32):
            return outer.enter_context(nc.psum_tensor(name, shape, dt))

        def sem(name):
            return outer.enter_context(nc.semaphore(name))

        small = sb("small", [128, 64])
        ident = sb("ident", [128, 128])
        minus_half = sb("minus_half", [128, 4])
        a_small = ExitStack()
        bk_sb = sb("bk_sb", [TK, NKV * HD], F32, a_small)
        squares = sb("squares", [128, G * HD], BF16, a_small)
        a_small.close()

        router_sb = sb("router_sb", [128, KC, E])
        below = sb("below", [128, 128], BF16)
        ones = sb("ones", [128, 128], BF16)
        iota_e = sb("iota_e", [128, NT, E])
        slot_row = sb("slot_row", [128, SLOTS])
        chosen_b = sb("chosen_b", [128, NT, E], BF16)
        seen_b = sb("seen_b", [128, NT + 1, E], BF16)
        logits = sb("logits", [128, NT, E])
        best = sb("best", [128, NT])
        spare = sb("spare", [128, NT, E])
        lowest_at = sb("lowest_at", [128, NT])
        count_i = sb("count_i", [128, 3, E], I32)
        padded = sb("padded", [128, E])
        start = sb("start", [128, E + 1])
        place = sb("place", [128, NT])
        place_i = sb("place_i", [128, NT], I32)
        place_now = [sb(f"place_now{i}", [128, 1], I32) for i in range(2)]
        owner = sb("owner", [128, 2, SLOTS])
        owner_i = sb("owner_i", [128, SLOTS], I32)
        held_i = sb("held_i", [128, SLOTS], I32)
        score = sb("score", [128, NT])

        c_phase = ExitStack()
        expert_sb = sb("expert_sb", [128, E, 3, KC, F], F32, c_phase)
        block_in = sb("block_in", [128, H], F32, c_phase)
        blockT = sb("blockT", [128, KC, 128], F32, c_phase)
        emid_sb = sb("emid_sb", [128, F], F32, c_phase)
        emidT = sb("emidT", [128, FC, 128], F32, c_phase)
        y_out = sb("y_out", [128, H], F32, c_phase)
        c_phase.close()

        d_phase = ExitStack()
        gathered = sb("gathered", [128, NT, H], F32, d_phase)
        base = sb("base", [128, NT, H], F32, d_phase)
        d_phase.close()

        wq_part = [sb(f"wq_{n}", [128, KC, NH * HD], F32R) for n in ("hi", "lo")]
        wide_part = wq_part
        a_phase = ExitStack()

        def a_sb(name, shape, dt=F32):
            return sb(name, shape, dt, a_phase)
        wk_part = [a_sb(f"wk_{n}", [128, KC, NKV * HD], F32R) for n in ("hi", "lo")]
        wv_part = [a_sb(f"wv_{n}", [128, KC, NKV * HD], F32R) for n in ("hi", "lo")]
        ctx_raw = a_sb("ctx_raw", [128, KC, SE])
        ctx_part = [a_sb(f"ctx_{n}", [128, KC, SE], F32R) for n in ("hi", "lo")]
        x_sb = a_sb("x_sb", [S, H])
        xT_part = [a_sb(f"xT_{n}", [128, KC, S], F32R) for n in ("hi", "lo")]
        bq_sb = a_sb("bq_sb", [S, NH * HD])
        bv_sb = a_sb("bv_sb", [128, NKV])
        qw_sb = a_sb("qw_sb", [128, 1])
        kw_sb = a_sb("kw_sb", [128, 1])
        qws = a_sb("qws", [128, 1])
        mask_sb = a_sb("mask_sb", [S, SE])
        q_sb = a_sb("q_sb", [S, G * HD])
        k_sb = a_sb("k_sb", [TK, NKV * HD])
        kT_part = [[a_sb(f"kT_{n}{p}", [128, NKV, SE_EVEN], F32R) for n in ("hi", "lo")] for p in range(2)]
        v_part = [[a_sb(f"v_{n}{p}", [TK, KT, NKV * HD], F32R) for n in ("hi", "lo")] for p in range(2)]
        qT_part = [a_sb(f"qT_{n}", [128, G * S], F32R) for n in ("hi", "lo")]
        o_sb = a_sb("o_sb", [128, G * S])
        with ExitStack() as early:
            stage = [sb(f"stage{i}", [128, PIECE], F32, early) for i in range(2)]
        probs = a_sb("probs", [S, G, SE])
        pT_part = [a_sb(f"pT_{n}", [TK, KT, G * S], F32R) for n in ("hi", "lo")]

        a_phase.close()

        b_phase = ExitStack()
        b1_early = ExitStack()
        wo_stage = [sb(f"wo_stage{i}", [128, PIECE], F32, b1_early) for i in range(4)]
        at_raw = sb("at_raw", [128, NH, 128], F32, b1_early)
        at_part = [[sb(f"at_{n}{p}", [128, NH, 128], F32R, b1_early) for n in ("hi", "lo")] for p in range(2)]
        b1_early.close()
        sb("before_experts", [128, HELD_FIRST * 3 * KC * F - 2 * KC * NH * HD], F32, b_phase)
        sb("first_expert", [128, 3, KC, F], F32, b_phase)
        shared_raw = [sb(f"shared_raw{i}", [128, PIECE], F32, b_phase) for i in range(3)]
        sb("third_expert", [128, 3, KC, F], F32, b_phase)
        acc = sb("acc", [128, NT, H], F32, b_phase)
        b1_phase = ExitStack()
        zeros = sb("zeros", [128, H], F32, b1_phase)
        x_in = sb("x_in", [128, H], F32, b1_phase)
        x1 = [sb(f"x1_{p}", [128, H], F32, b1_phase) for p in range(2)]
        h_out = [sb(f"h_out{p}", [128, H], F32, b1_phase) for p in range(2)]
        hT_f = sb("hT_f", [128, KC, 128], F32, b1_phase)
        b1_phase.close()
        b2_phase = ExitStack()
        h_in = [sb(f"h_in{p}", [128, H], F32, b2_phase) for p in range(2)]
        xs_out = [sb(f"xs_out{p}", [128, H], F32, b2_phase) for p in range(2)]
        hT_part = [sb(f"hT_{n}", [128, KC, 128], F32R, b2_phase) for n in ("hi", "lo")]
        mT_part = [sb(f"mT_{n}", [128, FC, 128], F32R, b2_phase) for n in ("hi", "lo")]
        mid_sb = sb("mid_sb", [128, F], F32, b2_phase)
        gate_sb = sb("gate_sb", [128, F], F32, b2_phase)
        b2_phase.close()
        b_phase.close()

        attended = nc.dram_tensor("attended", [128, NH, TOK], F32, kind="Internal").ap()
        h_dram = nc.dram_tensor("h_rows", [TOK, H], F32, kind="Internal").ap()
        xs_dram = nc.dram_tensor("xs_rows", [SLOTS * 128, H], F32, kind="Internal").ap()
        x2_dram = nc.dram_tensor("x2_rows", [TOK, H], F32, kind="Internal").ap()
        y_dram = nc.dram_tensor("y_rows", [SLOTS * 128, H], F32, kind="Internal").ap()

        bn, mv, ln_var, ln_rs = small[0:S, 0:6], small[0:S, 6:8], small[0:S, 8:9], small[0:S, 9:10]
        bn128, mv128, ln_var128, ln_rs128 = small[:, 0:6], small[:, 6:8], small[:, 8:9], small[:, 9:10]
        q_ss, q_ms, q_rs = (small[0:S, 12 + 4 * i:16 + 4 * i] for i in range(3))
        k_ss, k_ms, k_rs = (small[0:TK, 24 + 4 * i:28 + 4 * i] for i in range(3))
        top, neg_top, total, inv_total = (small[0:S, 36 + 4 * i:40 + 4 * i] for i in range(4))

        score_ps = [psum(f"score_ps{i}", [128, 512]) for i in range(2)]
        qv_ps = psum("qv_ps", [128, 512])
        k_ps = psum("k_ps", [128, 512])
        turn_ps = psum("turn_ps", [128, 512])
        pT_ps = [psum(f"pT_ps{i}", [128, 512]) for i in range(2)]
        o_ps = psum("o_ps", [128, 512])

        stage_loaded = [sem(f"stage_loaded{i}") for i in range(2)]
        consts_loaded, mask_loaded, ctx_loaded, x_loaded, o_stored = (
            sem(n) for n in ("consts_loaded", "mask_loaded", "ctx_loaded", "x_loaded", "o_stored"))
        w_hi, w_lo, made = sem("w_hi"), sem("w_lo"), sem("made")
        key_padded = sem("key_padded")
        ident_zeroed, ident_made, qws_made = sem("ident_zeroed"), sem("ident_made"), sem("qws_made")
        ctx_hi, ctx_lo = sem("ctx_hi"), sem("ctx_lo")
        ln_stats, ln_step, ln_rsqrt, x_normed, x_turned, xT_hi, xT_lo = (
            sem(n) for n in ("ln_stats", "ln_step", "ln_rsqrt", "x_normed", "x_turned", "xT_hi", "xT_lo"))
        q_proj, q_biased, q_squared, q_mean, q_rsqrt, q_normed, q_turned, qT_hi, qT_lo = (
            sem(n) for n in ("q_proj", "q_biased", "q_squared", "q_mean", "q_rsqrt", "q_normed", "q_turned", "qT_hi", "qT_lo"))
        k_proj, k_biased, k_squared, k_mean, k_rsqrt, k_normed, k_turned, kT_hi, kT_lo = (
            sem(n) for n in ("k_proj", "k_biased", "k_squared", "k_mean", "k_rsqrt", "k_normed", "k_turned", "kT_hi", "kT_lo"))
        v_proj, v_hi, v_lo = sem("v_proj"), sem("v_hi"), sem("v_lo")
        scored, masked, negated, exped, inverted, p_normed, p_turned, pT_hi, pT_lo, pv_done, o_made = (
            sem(n) for n in ("scored", "masked", "negated", "exped", "inverted", "p_normed", "p_turned",
                             "pT_hi", "pT_lo", "pv_done", "o_made"))

        b_consts, wo_hi, wo_lo, at_loaded, at_hi, at_lo, xin_loaded, projected, x_added = (
            sem(n) for n in ("b_consts", "wo_hi", "wo_lo", "at_loaded", "at_hi", "at_lo", "xin_loaded", "projected", "x_added"))
        wo_loaded = [sem(f"wo_loaded{i}") for i in range(4)]
        b_step, b_var, b_rsqrt, h_made, h_turned, hT_copied, routed, best_found, ranked = (
            sem(n) for n in ("b_step", "b_var", "b_rsqrt", "h_made", "h_turned", "hT_copied", "routed",
                             "best_found", "ranked"))
        tables, score_made, counted, plan, placed, owners, zeroed, rows_zeroed, shared_hi, shared_lo = (
            sem(n) for n in ("tables", "score_made", "counted", "plan", "placed", "owners", "zeroed", "rows_zeroed",
                             "shared_hi", "shared_lo"))
        h2_turned, hT_hi, hT_lo, gated, upped, silued, mid_made, mid_turned, mT_hi, mT_lo, shared_out, shared_added = (
            sem(n) for n in ("h2_turned", "hT_hi", "hT_lo", "gated", "upped", "silued", "mid_made", "mid_turned",
                             "mT_hi", "mT_lo", "shared_out", "shared_added"))
        xs_made = sem("xs_made")
        e_turned, eT_copied, e_gated, e_upped, e_silued, e_mid, e_mid_turned, e_midT, e_down, y_made = (
            sem(n) for n in ("e_turned", "eT_copied", "e_gated", "e_upped", "e_silued", "e_mid",
                             "e_mid_turned", "e_midT", "e_down", "y_made"))
        h_loaded, h_stored, xs_stored = (
            [sem(f"{n}{p}") for p in range(2)] for n in ("h_loaded", "h_stored", "xs_stored"))
        block_loaded, y_stored = sem("block_loaded"), sem("y_stored")
        expert_loaded = [sem(f"expert_loaded{i}") for i in range(3)]
        rows_gathered = [sem(f"rows_gathered{i}") for i in range(-(-NT // GATHERS))]
        shared_loaded = [sem(f"shared_loaded{i}") for i in range(3)]
        x2_stored, base_loaded, out_stored, experts_held, chosen_made = (
            sem(n) for n in ("x2_stored", "base_loaded", "out_stored", "experts_held", "chosen_made"))
        dve_passed, pool_passed = sem("dve_passed"), sem("pool_passed")
        acc_made = sem("acc_made")
        now_copied, final_made = sem("now_copied"), sem("final_made")

        pieces = [(wk_part, None, wk), (wv_part, None, wv)] + [(wq_part, c, wq) for c in range(KC)]
        K_PIECE, V_PIECE, Q_PIECE = 1, 2, len(pieces)
        V_TILE = {0: 0, 1: 1, 3: 2}
        V_BEFORE = {0: 0, 1: 1, 2: 2, 3: 2}

        def piece_part(j, which):
            part, c, _ = pieces[j]
            return part[which][:].rearrange("p c n -> p (c n)") if c is None else part[which][:, c, :]

        def piece_source(j):
            _, c, w = pieces[j]
            w = w.rearrange("(c p) n -> p c n", p=128)
            return w if c is None else w[:, c, :]

        def products(pe, out, a, b, start, stop):
            nc.tensor.matmul(out, a[0], b[0], start=start, stop=False)
            nc.tensor.matmul(out, a[0], b[1], start=False, stop=False)
            return nc.tensor.matmul(out, a[1], b[0], start=False, stop=stop)

        def run(eng, slot, tail):
            for g in range(NKV):
                slot(-1, 1, g, False, True)
            for b in range(2):
                for g in range(NKV):
                    slot(b, b % 2, g, True, True)
            with eng.Fori(1, B // 2 - 1) as pair:
                for p in range(2):
                    for g in range(NKV):
                        slot(2 * pair + p, p, g, True, True)
            for b in range(B - 2, B):
                for g in range(NKV):
                    slot(b, b % 2, g, True, b < B - 1)
            tail()


        def steps(eng, n, step):
            pairs = (n - 2) // 2 if n % 2 == 0 else (n - 3) // 2
            for i in range(2):
                step(i, i, i == 0, False)
            with eng.Fori(1, pairs) as pair:
                for p in range(2):
                    step(2 * pair + p, p, False, False)
            for i in range(2 * pairs, n):
                step(i, i % 2, False, i == n - 1)

        def through(i, p, each=16):
            return (each // 2) * (i - p) + each

        def column(t, i):
            return t[:, bass.ds(i, 1)]

        def layer(t, i):
            return t[:, bass.ds(i, 1), :].rearrange("p a n -> p (a n)")

        def rows(t, i):
            return t[bass.ds(i * 128, 128), :]

        def wo_high(act, pieces_now):
            act.wait_ge(q_proj, 4 * B)
            for c in pieces_now:
                act.wait_ge(wo_loaded[c], 16)
                nc.scalar.copy(wide_part[0][:, c, :], wo_stage[c][:]).then_inc(wo_hi, 1)

        def wo_low(dve, pieces_now):
            for c in pieces_now:
                dve.wait_ge(wo_hi, c + 1)
                nc.vector.tensor_tensor(wide_part[1][:, c, :], wo_stage[c][:], wide_part[0][:, c, :].bitcast(F32),
                                        ALU.subtract).then_inc(wo_lo, 1)

        def later_sp(sp):
            sp.wait_ge(zeroed, 1)
            sp.dma_start(xs_dram.rearrange("(s p) n -> p s n", p=128),
                         zeros[:].rearrange("p (s n) -> p s n", s=1).broadcast_to([128, SLOTS, H])).then_inc(rows_zeroed, 16)
            sp.dma_start(router_sb[:], router.rearrange("(c p) e -> p c e", p=128)).then_inc(b_consts, 16)

            def load_tile(i, p, first, last):
                if isinstance(i, int) and i == 1:
                    sp.wait_ge(wo_lo, 4)
                    load_expert(sp, 0)
                wait(sp, x_added, i)
                sp.dma_start(x_in[:], rows(x.rearrange("b s h -> (b s) h"), i)).then_inc(xin_loaded, 16)
                if not last:
                    sp.wait_ge(at_lo, i + 1)
                    sp.dma_start(at_raw[:], attended[:, :, bass.ds((i + 1) * 128, 128)]).then_inc(at_loaded, 16)
                if not first:
                    store_h(i - 1, 1 - p)

            def store_h(i, p):
                sp.wait_ge(h_made, i + 1)
                sp.dma_start(rows(h_dram, i), h_out[p][:]).then_inc(h_stored[p], 16)
            steps(sp, NT, load_tile)
            sp.wait_ge(projected, NT)
            for n in range(3):
                sp.dma_start(shared_raw[n][:].rearrange("p (c n) -> p c n", c=KC),
                             shared_w[n].rearrange("(c p) n -> p c n", p=128)).then_inc(shared_loaded[n], 16)
            store_h(NT - 1, (NT - 1) % 2)
            for p in range(2):
                sp.wait_ge(h_stored[p], 8 * NT)

            def store_x2(i):
                sp.wait_ge(shared_added, i + 1)
                sp.dma_start(rows(x2_dram, i), layer(acc, i)).then_inc(x2_stored, 16)

            def load_h(i, p, first, last):
                if not first:
                    wait(sp, h2_turned, i - 1)
                    wait(sp, xs_made, i - 1)
                sp.dma_start(h_in[p][:], rows(h_dram, i)).then_inc(h_loaded[p], 16)
                if not (isinstance(i, int) and i < 2):
                    store_x2(i - 2)
            steps(sp, NT, load_h)
            for i in range(NT - 2, NT):
                store_x2(i)
            for p in range(2):
                sp.wait_ge(xs_stored[p], 8 * NT)
            load_block(sp, 0)

            def block(j, p, first, last):
                if not last:
                    sp.wait_ge(e_turned, j + 1)
                    load_block(sp, j + 1)
                if not first:
                    store_y(j - 1)

            def store_y(j):
                sp.wait_ge(y_made, j + 1)
                sp.dma_start(rows(y_dram, j), y_out[:]).then_inc(y_stored, 16)
            steps(sp, SLOTS, block)
            store_y(SLOTS - 1)
            sp.wait_ge(e_down, SLOTS)
            sp.wait_ge(x2_stored, 16 * NT)
            sp.dma_start(base[:], x2_dram.rearrange("(t p) n -> p t n", p=128)).then_inc(base_loaded, 16)
            for i in range(NT):
                sp.wait_ge(final_made, i + 1)
                sp.dma_start(rows(out.rearrange("b s h -> (b s) h"), i), gathered[:, i, :]).then_inc(out_stored, 16)
            sp.wait_ge(out_stored, 16 * NT)

        def load_expert(eng, e):
            for n in range(3):
                eng.dma_start(expert_sb[:, held_at(e), n], expert_w[n][e].rearrange("(c p) n -> p c n", p=128)).then_inc(expert_loaded[e % 3], 16)

        def load_block(sp, j):
            sp.dma_start(block_in[:], rows(xs_dram, j)).then_inc(block_loaded, 16)

        def later_pool(pool):
            pool.wait_ge(pv_done, 4 * B)
            make_tables(pool)

            def rsqrt(i, p, first, last):
                pool.wait_ge(b_var, i + 1)
                nc.gpsimd.tensor_tensor(ln_rs128, ln_var128, minus_half[:, 0:1], ALU.pow).then_inc(b_rsqrt, 1)
            steps(pool, NT, rsqrt)
            pool.wait_ge(placed, 1)
            pool.wait_ge(rows_zeroed, 16)

            def scatter(i, p, first, last):
                wait_apart(pool, pool_passed, xs_made, i + 1)
                nc.gpsimd.indirect_dma_start(out=xs_dram[:, :], out_offset=bass.IndirectOffsetOnAxis(ap=place_now[p][:, 0:1], axis=0),
                                             in_=xs_out[p][:], in_offset=None).then_inc(xs_stored[p], 16)
            steps(pool, NT, scatter)
            for e in range(E):
                pool.wait_ge(expert_loaded[e % 3], 48 * (e // 3 + 1))
                pool.sem_inc(experts_held, 1)
            pool.wait_ge(e_down, SLOTS)
            pool.wait_ge(y_stored, 16 * SLOTS)
            for i in range(NT):
                nc.gpsimd.indirect_dma_start(out=gathered[:, i, :], out_offset=None, in_=y_dram[:, :],
                                             in_offset=bass.IndirectOffsetOnAxis(ap=place_i[:, i:i + 1], axis=0)).then_inc(rows_gathered[i // GATHERS], 16)

        def make_tables(pool):
            nc.gpsimd.memset(zeros[:], 0.0).then_inc(zeroed, 1)
            nc.gpsimd.memset(ones[:], 1.0).then_inc(tables, 1)
            nc.gpsimd.memset(below[:], 1.0).then_inc(tables, 1)
            nc.gpsimd.memset(seen_b[:], 0.0).then_inc(tables, 1)
            nc.gpsimd.iota(iota_e[:], pattern=[[0, NT], [1, E]], base=0, channel_multiplier=0, allow_small_or_imprecise_dtypes=True).then_inc(tables, 1)
            nc.gpsimd.iota(slot_row[:], pattern=[[128, SLOTS]], base=0, channel_multiplier=0, allow_small_or_imprecise_dtypes=True).then_inc(tables, 1)
            pool.wait_ge(tables, 5)
            nc.gpsimd.affine_select(out=below[:], in_=below[:], compare_op=ALU.is_gt, fill=0.0, base=0,
                                    pattern=[[1, 128]], channel_multiplier=-1).then_inc(tables, 1)

        def later_act(act):
            def high(i, p):
                act.wait_ge(at_loaded, 16 * (i + 1))
                nc.scalar.copy(at_part[p][0][:], at_raw[:]).then_inc(at_hi, 1)

            def tile(i, p, first, last):
                if not first:
                    wait(act, projected, i - 1)
                    high(i, p)
                    copy_hT(i - 1)

            def copy_hT(i):
                act.wait_ge(h_turned, i + 1)
                nc.scalar.copy(hT_f[:].rearrange("p c n -> p (c n)"), turn_ps[:]).then_inc(hT_copied, 1)
            steps(act, NT, tile)
            copy_hT(NT - 1)
            for n in range(3):
                act.wait_ge(shared_loaded[n], 16)
                act.wait_ge(projected, NT)
                nc.scalar.copy(wide_part[0][:, n, :], shared_raw[n][:]).then_inc(shared_hi, 1)

            def hT_high(i):
                act.wait_ge(h2_turned, i + 1)
                nc.scalar.copy(hT_part[0][:].rearrange("p c n -> p (c n)"), turn_ps[:]).then_inc(hT_hi, 1)
            hT_high(0)
            act.wait_ge(shared_lo, 3)
            for e in range(1, EARLY):
                load_expert(act, e)
            act.wait_ge(best_found, 1)
            nc.scalar.activation(score[:], best[:], ACT.Sigmoid).then_inc(score_made, 1)

            def shared(i, p, first, last):
                act.wait_ge(gated, i + 1)
                wait(act, mid_made, i)
                nc.scalar.activation(gate_sb[:], score_ps[0][:], ACT.Silu).then_inc(silued, 1)
                if not last:
                    hT_high(i + 1)
                act.wait_ge(mid_turned, i + 1)
                nc.scalar.copy(mT_part[0][:].rearrange("p c n -> p (c n)"), pT_ps[0][:]).then_inc(mT_hi, 1)
            steps(act, NT, shared)

            act.wait_ge(x2_stored, 16 * NT)
            for p in range(2):
                act.wait_ge(xs_stored[p], 8 * NT)
            for e in range(EARLY, E):
                act.wait_ge(experts_held, e - EARLY + 1)
                load_expert(act, e)

            def block_turned(j):
                act.wait_ge(e_turned, j + 1)
                nc.scalar.copy(blockT[:].rearrange("p c n -> p (c n)"), turn_ps[:]).then_inc(eT_copied, 1)
            block_turned(0)

            def block(j, p, first, last):
                act.wait_ge(e_gated, j + 1)
                wait(act, e_mid_turned, j)
                nc.scalar.activation(emid_sb[:], score_ps[0][:], ACT.Silu).then_inc(e_silued, 1)
                if not last:
                    block_turned(j + 1)
                act.wait_ge(e_mid_turned, j + 1)
                nc.scalar.copy(emidT[:].rearrange("p c n -> p (c n)"), pT_ps[0][:]).then_inc(e_midT, 1)
            steps(act, SLOTS, block)

        def later_dve(dve):
            def low(i, p):
                dve.wait_ge(at_hi, i + 1)
                nc.vector.tensor_tensor(at_part[p][1][:], at_raw[:], at_part[p][0][:].bitcast(F32), ALU.subtract).then_inc(at_lo, 1)

            def tile(i, p, first, last):
                if not last:
                    low(i + 1, 1 - p)
                dve.wait_ge(projected, i + 1)
                dve.wait_ge(xin_loaded, 16 * (i + 1))
                nc.vector.tensor_tensor(x1[p][:], score_ps[p][:], x_in[:], ALU.add).then_inc(x_added, 1)
                dve.wait_ge(x_added, i + 1)
                nc.vector.bn_stats(bn128, x1[p][:]).then_inc(b_step, 1)
                wait_apart(dve, dve_passed, b_step, 2 * i + 1)
                nc.vector.bn_aggr(mv128, bn128).then_inc(b_step, 1)
                dve.wait_ge(b_step, 2 * i + 2)
                nc.vector.tensor_scalar(ln_var128, mv128[:, 1:2], LN_EPS, None, ALU.add).then_inc(b_var, 1)
                dve.wait_ge(b_rsqrt, i + 1)
                if not first:
                    wait(dve, h_stored[p], through(i - 2, p))
                    wait(dve, h_turned, i - 1)
                nc.vector.tensor_scalar(layer(acc, i), x1[p][:], 1.0, None, ALU.mult).then_inc(acc_made, 1)
                nc.vector.tensor_scalar(h_out[p][:], x1[p][:], mv128[:, 0:1], ln_rs128, ALU.subtract, ALU.mult).then_inc(h_made, 1)

            steps(dve, NT, tile)

            def hT_low(i):
                dve.wait_ge(hT_hi, i + 1)
                nc.vector.tensor_tensor(hT_part[1][:].rearrange("p c n -> p (c n)"), turn_ps[:],
                                        hT_part[0][:].rearrange("p c n -> p (c n)").bitcast(F32), ALU.subtract).then_inc(hT_lo, 1)

            def shared_low(n):
                dve.wait_ge(shared_hi, n + 1)
                nc.vector.tensor_tensor(wide_part[1][:, n, :], shared_raw[n][:], wide_part[0][:, n, :].bitcast(F32),
                                        ALU.subtract).then_inc(shared_lo, 1)
            shared_low(0)
            shared_low(1)
            hT_low(0)
            shared_low(2)
            dve.wait_ge(tables, 6)
            make_plan(dve)
            dve.wait_ge(placed, 1)
            dve.wait_ge(score_made, 1)

            def add_shared(i):
                dve.wait_ge(shared_out, i + 1)
                nc.vector.tensor_tensor(layer(acc, i), o_ps[:], layer(acc, i), ALU.add).then_inc(shared_added, 1)

            def shared(i, p, first, last):
                dve.wait_ge(placed, 1)
                dve.wait_ge(h_loaded[p], through(i, p))
                if not first:
                    wait(dve, xs_stored[p], through(i - 2, p))
                nc.vector.tensor_copy(place_now[p][:], column(place_i, i)).then_inc(now_copied, 1)
                nc.vector.tensor_scalar(xs_out[p][:], h_in[p][:], column(score, i), None, ALU.mult).then_inc(xs_made, 1)
                dve.wait_ge(upped, i + 1)
                dve.wait_ge(silued, i + 1)
                wait(dve, mid_turned, i)
                nc.vector.tensor_tensor(mid_sb[:], score_ps[1][:], gate_sb[:], ALU.mult).then_inc(mid_made, 1)
                if not last:
                    hT_low(i + 1)
                if not first:
                    add_shared(i - 1)
                dve.wait_ge(mT_hi, i + 1)
                nc.vector.tensor_tensor(mT_part[1][:].rearrange("p c n -> p (c n)"), pT_ps[0][:],
                                        mT_part[0][:].rearrange("p c n -> p (c n)").bitcast(F32), ALU.subtract).then_inc(mT_lo, 1)
            steps(dve, NT, shared)
            add_shared(NT - 1)

            def out_y(j):
                dve.wait_ge(e_down, j + 1)
                wait(dve, y_stored, 16 * j)
                nc.vector.tensor_copy(y_out[:], o_ps[:]).then_inc(y_made, 1)

            def block(j, p, first, last):
                dve.wait_ge(e_upped, j + 1)
                dve.wait_ge(e_silued, j + 1)
                nc.vector.tensor_tensor(emid_sb[:], score_ps[1][:], emid_sb[:], ALU.mult).then_inc(e_mid, 1)
                if not first:
                    out_y(j - 1)
            steps(dve, SLOTS, block)
            out_y(SLOTS - 1)

            dve.wait_ge(base_loaded, 16)
            for i in range(NT):
                dve.wait_ge(rows_gathered[i // GATHERS], 16 * min(GATHERS, NT - i // GATHERS * GATHERS))
                nc.vector.tensor_tensor(gathered[:, i, :], base[:, i, :], gathered[:, i, :], ALU.add).then_inc(final_made, 1)

        def make_plan(dve):
            step_no = [0]

            def done(ins):
                step_no[0] += 1
                ins.then_inc(plan, 1)
                dve.wait_ge(plan, step_no[0])

            def over_experts(t):
                return t.rearrange("p (t a) -> p t a", a=1).broadcast_to([128, NT, E])

            def over_tiles(t):
                return t.rearrange("p (a e) -> p a e", a=1).broadcast_to([128, NT, E])

            dve.wait_ge(routed, NT)
            done(nc.vector.tensor_copy(logits[:].rearrange("p t e -> p (t e)"), k_ps[:, 0:NT * E]))
            nc.vector.tensor_reduce(best[:], logits[:], AX_X, ALU.max).then_inc(best_found, 1)
            dve.wait_ge(best_found, 1)
            done(nc.vector.tensor_tensor(spare[:], logits[:], over_experts(best[:]), ALU.is_lt))
            done(nc.vector.scalar_tensor_tensor(out=spare[:], in0=spare[:], scalar=float(E), in1=iota_e[:], op0=ALU.mult, op1=ALU.add))
            done(nc.vector.tensor_reduce(lowest_at[:], spare[:], AX_X, ALU.min))
            done(nc.vector.tensor_tensor(chosen_b[:], iota_e[:], over_experts(lowest_at[:]), ALU.is_equal))
            for t in range(NT):
                done(nc.vector.tensor_tensor(seen_b[:, t + 1, :], seen_b[:, t, :], chosen_b[:, t, :], ALU.add))
            nc.vector.sem_inc(chosen_made, 1)
            dve.wait_ge(ranked, 1)
            done(nc.vector.tensor_scalar(spare[:, 0, :], o_ps[:, NT * E:(NT + 1) * E], 127.0, None, ALU.add))
            done(nc.vector.tensor_copy(count_i[:, 0, :], spare[:, 0, :]))
            done(nc.vector.tensor_single_scalar(count_i[:, 1, :], count_i[:, 0, :], 7, ALU.arith_shift_right))
            done(nc.vector.tensor_copy(spare[:, 0, :], count_i[:, 1, :]))
            done(nc.vector.tensor_scalar(padded[:], spare[:, 0, :], 128.0, None, ALU.mult))
            done(nc.vector.memset(start[:], 0.0))
            for e in range(E):
                done(nc.vector.tensor_tensor(start[:, e + 1:e + 2], start[:, e:e + 1], padded[:, e:e + 1], ALU.add))
            done(nc.vector.tensor_tensor(spare[:], o_ps[:, 0:NT * E].rearrange("p (t e) -> p t e", t=NT), over_tiles(start[:, 0:E]), ALU.add))
            done(nc.vector.tensor_tensor(spare[:], spare[:], chosen_b[:], ALU.mult))
            done(nc.vector.tensor_reduce(place[:], spare[:], AX_X, ALU.add))
            nc.vector.tensor_copy(place_i[:], place[:]).then_inc(placed, 1)
            done(nc.vector.memset(owner[:], 0.0))
            for e in range(1, E):
                done(nc.vector.scalar_tensor_tensor(out=owner[:, e % 2, :], in0=slot_row[:], scalar=start[:, e:e + 1], in1=owner[:, (e - 1) % 2, :],
                                                    op0=ALU.is_ge, op1=ALU.add))
            done(nc.vector.tensor_copy(owner_i[:], owner[:, (E - 1) % 2, :]))
            done(nc.vector.tensor_scalar(held_i[:], owner_i[:], HELD_FIRST, None, ALU.add))
            done(nc.vector.tensor_single_scalar(held_i[:], held_i[:], E - 1, ALU.bitwise_and))
            nc.vector.sem_inc(owners, 1)

        def later_pe(pe):
            pe.wait_ge(wo_lo, 4)

            def tile(i, p, first, last):
                pe.wait_ge(at_lo, i + 1)
                if not first:
                    wait(pe, x_added, i - 1)
                for h in range(NH):
                    ins = products(pe, score_ps[p][:], [a[:, h, :] for a in at_part[p]],
                                   [w[:, h // 4, (h % 4) * H:(h % 4 + 1) * H] for w in wide_part], h == 0, h == NH - 1)
                ins.then_inc(projected, 1)
                if not first:
                    route(i - 1, 1 - p)

            def route(i, p):
                pe.wait_ge(h_made, i + 1)
                wait(pe, hT_copied, i)
                for c in range(KC):
                    ins = nc.tensor.transpose(turn_ps[:, c * 128:(c + 1) * 128], h_out[p][:, c * 128:(c + 1) * 128], ident[:])
                ins.then_inc(h_turned, 1)
                pe.wait_ge(hT_copied, i + 1)
                if isinstance(i, int) and i == 0:
                    pe.wait_ge(b_consts, 16)
                for c in range(KC):
                    ins = nc.tensor.matmul(k_ps[:, bass.ds(i * E, E)], hT_f[:, c, :], router_sb[:, c, :], start=(c == 0), stop=(c == KC - 1))
                ins.then_inc(routed, 1)
            steps(pe, NT, tile)
            route(NT - 1, (NT - 1) % 2)

            def rank():
                pe.wait_ge(chosen_made, 1)
                nc.tensor.matmul(o_ps[:, 0:NT * E], below[:], chosen_b[:].rearrange("p t e -> p (t e)"), start=True, stop=False)
                nc.tensor.matmul(o_ps[:, 0:NT * E], ones[:], seen_b[:, 0:NT, :].rearrange("p t e -> p (t e)"), start=False, stop=True)
                nc.tensor.matmul(o_ps[:, NT * E:(NT + 1) * E], ones[:], seen_b[:, NT, :], start=True, stop=True).then_inc(ranked, 1)

            def turn_h(i, p):
                pe.wait_ge(h_loaded[p], through(i, p))
                wait(pe, hT_lo, i)
                for c in range(KC):
                    ins = nc.tensor.transpose(turn_ps[:, c * 128:(c + 1) * 128], h_in[p][:, c * 128:(c + 1) * 128], ident[:])
                ins.then_inc(h2_turned, 1)
            turn_h(0, 0)
            pe.wait_ge(shared_lo, 2)

            def weights(n):
                return [w[:, n, :].rearrange("p (c n) -> p c n", c=KC) for w in wide_part]

            def shared_down(i):
                pe.wait_ge(mT_lo, i + 1)
                wait(pe, shared_added, i)
                if isinstance(i, int) and i == 0:
                    pe.wait_ge(shared_lo, 3)
                    pe.wait_ge(placed, 1)
                for c in range(FC):
                    ins = products(pe, o_ps[:], [m[:, c, :] for m in mT_part], [w[:, c, :] for w in weights(2)], c == 0, c == FC - 1)
                ins.then_inc(shared_out, 1)

            def shared(i, p, first, last):
                pe.wait_ge(hT_lo, i + 1)
                wait(pe, mid_made, i)
                for n, done in ((0, gated), (1, upped)):
                    for c in range(KC):
                        ins = products(pe, score_ps[n][:], [t[:, c, :] for t in hT_part], [w[:, c, :] for w in weights(n)],
                                       c == 0, c == KC - 1)
                    ins.then_inc(done, 1)
                if first:
                    rank()
                if not last:
                    turn_h(i + 1, 1 - p)
                if not first:
                    shared_down(i - 1)
                pe.wait_ge(mid_made, i + 1)
                wait(pe, mT_lo, i)
                for c in range(FC):
                    ins = nc.tensor.transpose(pT_ps[0][:, c * 128:(c + 1) * 128], mid_sb[:, c * 128:(c + 1) * 128], ident[:])
                ins.then_inc(mid_turned, 1)
            steps(pe, NT, shared)
            shared_down(NT - 1)

            def turn_block(j):
                pe.wait_ge(block_loaded, 16 * (j + 1))
                wait(pe, eT_copied, j)
                for c in range(KC):
                    ins = nc.tensor.transpose(turn_ps[:, c * 128:(c + 1) * 128], block_in[:, c * 128:(c + 1) * 128], ident[:])
                ins.then_inc(e_turned, 1)
            turn_block(0)
            pe.wait_ge(owners, 1)

            def down(j, held):
                pe.wait_ge(e_midT, j + 1)
                if isinstance(j, int) and j == 0:
                    pe.wait_ge(shared_added, NT)
                wait(pe, y_made, j)
                for c in range(FC):
                    ins = nc.tensor.matmul(o_ps[:], emidT[:, c, :], expert_sb[:, bass.ds(held, 1), 2, c, :].rearrange("p a n -> p (a n)"), start=(c == 0), stop=(c == FC - 1))
                ins.then_inc(e_down, 1)

            def block(j, p, first, last):
                owner_now = pe.value_load(owner_i[0:1, bass.ds(j, 1)], min_val=0, max_val=E - 1)
                held = pe.value_load(held_i[0:1, bass.ds(j, 1)], min_val=0, max_val=E - 1)
                pe.wait_ge(experts_held, owner_now + 1)
                pe.wait_ge(eT_copied, j + 1)
                wait(pe, e_mid, j)
                for n, done in ((0, e_gated), (1, e_upped)):
                    for c in range(KC):
                        ins = nc.tensor.matmul(score_ps[n][:], blockT[:, c, :], expert_sb[:, bass.ds(held, 1), n, c, :].rearrange("p a n -> p (a n)"), start=(c == 0), stop=(c == KC - 1))
                    ins.then_inc(done, 1)
                if not last:
                    turn_block(j + 1)
                if not first:
                    held_before = pe.value_load(held_i[0:1, bass.ds(j - 1, 1)], min_val=0, max_val=E - 1)
                    down(j - 1, held_before)
                pe.wait_ge(e_mid, j + 1)
                for c in range(FC):
                    ins = nc.tensor.transpose(pT_ps[0][:, c * 128:(c + 1) * 128], emid_sb[:, c * 128:(c + 1) * 128], ident[:])
                ins.then_inc(e_mid_turned, 1)
            steps(pe, SLOTS, block)
            down(SLOTS - 1, pe.value_load(held_i[0:1, SLOTS - 1:SLOTS], min_val=0, max_val=E - 1))

        block = outer.enter_context(nc.Block())

        @block.sync
        def _(sp):
            sp.dma_start(ctx_raw[:], ctxT[0]).then_inc(ctx_loaded, 16)
            for j in range(len(pieces)):
                if j >= 2:
                    sp.wait_ge(w_lo, j - 1)
                dst = stage[j % 2][:] if pieces[j][1] is not None else stage[j % 2][:].rearrange("p (c n) -> p c n", c=KC)
                sp.dma_start(dst, piece_source(j)).then_inc(stage_loaded[j % 2], 16)
                if j == 1:
                    sp.dma_start(x_sb[:], x[0]).then_inc(x_loaded, 16)
                    for dst, src in ((bk_sb, bk_rows), (bq_sb, bq_rows), (bv_sb, bv_cols), (qw_sb, qn_col), (kw_sb, kn_col)):
                        sp.dma_start(dst[:], src).then_inc(consts_loaded, 16)
                    sp.dma_start(mask_sb[:], mask).then_inc(mask_loaded, 16)

            def store(b, g, s):
                sp.wait_ge(o_made, s + 1)
                sp.dma_start(attended[:, g * G:(g + 1) * G, bass.ds(b * S, S)],
                             o_sb[:].rearrange("p (h n) -> p h n", h=G)).then_inc(o_stored, 16)

            def load(dst, src, b, to):
                at = src[b] if isinstance(b, int) else src[bass.ds(b, 1)].rearrange(
                    "a p n -> (a p) n" if len(src.shape) == 3 else "a p c n -> p (a c) n")
                sp.dma_start(dst, at).then_inc(to, 16)

            def slot(b, p, g, attend, ahead):
                s = 4 * b + g
                if attend and not (isinstance(s, int) and s == 0):
                    store(b if g else b - 1, (g - 1) % NKV, s - 1)
                if g == 3:
                    if not isinstance(b, int) or b + 2 < B:
                        sp.wait_ge(x_turned, b + 2)
                        load(x_sb[:], x, b + 2, x_loaded)
                if g == 0 and (not isinstance(b, int) or b + 2 < B):
                    sp.wait_ge(ctx_lo, b + 2)
                    load(ctx_raw[:], ctxT, b + 2, ctx_loaded)

                if isinstance(b, int) and b == B - 1 and g == 0:
                    sp.wait_ge(v_proj, 3 * B)
                    for c in range(4):
                        sp.dma_start(wo_stage[c][:].rearrange("p (h n) -> p h n", h=4),
                                     wo.rearrange("(h p) n -> p h n", p=128)[:, 4 * c:4 * c + 4, :]).then_inc(wo_loaded[c], 16)
                if isinstance(b, int) and b == B - 1 and g == 3:
                    sp.wait_ge(q_biased, 4 * B)
                    sp.wait_ge(o_stored, 16 * (4 * B - 2))
                    sp.dma_start(at_raw[:], attended[:, :, 0:128]).then_inc(at_loaded, 16)

            def tail():
                store(B - 1, NKV - 1, 4 * B - 1)
                sp.wait_ge(o_stored, 16 * 4 * B)
            run(sp, slot, tail)
            later_sp(sp)

        @block.gpsimd
        def _(pool):
            nc.gpsimd.memset(minus_half[:], -0.5).then_inc(made, 1)
            for p in range(2):
                for part in kT_part[p]:
                    nc.gpsimd.memset(part[:, :, SE:SE_EVEN].bitcast(F32), 0.0).then_inc(key_padded, 1)
            nc.gpsimd.memset(ident[:], 0.0).then_inc(ident_zeroed, 1)
            pool.wait_ge(ident_zeroed, 1)
            nc.gpsimd.affine_select(out=ident[:], in_=ident[:], compare_op=ALU.not_equal, fill=1.0, base=0,
                                    pattern=[[-1, 128]], channel_multiplier=1).then_inc(ident_made, 1)
            pool.wait_ge(made, 1)

            def split_ctx(c):
                pool.wait_ge(ctx_hi, c + 1)
                nc.gpsimd.tensor_tensor(ctx_part[1][:], ctx_raw[:], ctx_part[0][:].bitcast(F32), ALU.subtract).then_inc(ctx_lo, 1)
            split_ctx(0)

            def slot(b, p, g, attend, ahead):
                s1, b1 = 4 * b + g + 1, b + 1
                if (g == 3 and ahead) or (g < 3 and attend):
                    pool.wait_ge(q_mean, s1 + 1)
                    nc.gpsimd.tensor_tensor(q_rs, q_ms, minus_half[0:S, :], ALU.pow).then_inc(q_rsqrt, 1)
                if ahead and g < 3:
                    pool.wait_ge(k_mean, 3 * b1 + g + 1)
                    nc.gpsimd.tensor_tensor(k_rs, k_ms, minus_half[0:TK, :], ALU.pow).then_inc(k_rsqrt, 1)
                if ahead and g == 0:
                    pool.wait_ge(ln_stats, b1 + 1)
                    nc.gpsimd.tensor_tensor(ln_rs, ln_var, minus_half[0:S, 0:1], ALU.pow).then_inc(ln_rsqrt, 1)
                if g == 3 and (not isinstance(b, int) or b + 2 < B):
                    split_ctx(b + 2)
            run(pool, slot, lambda: None)
            later_pool(pool)

        @block.scalar
        def _(act):
            for j in range(len(pieces)):
                act.wait_ge(stage_loaded[j % 2], 16 * (j // 2 + 1))
                nc.scalar.copy(piece_part(j, 0), stage[j % 2][:]).then_inc(w_hi, 1)

            def square(source, sums, rows, done, count, other, other_count):
                wait(act, done, count - 1)
                wait(act, other, other_count)
                for h in range(G):
                    at = slice(h * HD, (h + 1) * HD)
                    last = nc.scalar.activation(squares[0:rows, at], source[:, at], ACT.Square, accum_out=sums[:, h:h + 1])
                last.then_inc(done, 1)

            def slot(b, p, g, attend, ahead):
                s, s1, b1 = 4 * b + g, 4 * b + g + 1, b + 1
                next_q = (g == 3 and ahead) or (g < 3 and attend)
                if attend and not (isinstance(s, int) and s == 0):
                    high_p(s - 1, (g - 1) % NKV, [KT - 1])
                if next_q:
                    act.wait_ge(q_biased, s1 + 1)
                    square(q_sb, q_ss, S, q_squared, s1 + 1, k_squared, 3 * b1 + g * ahead)
                if ahead and g > 0:
                    n = 3 * b1 + g
                    act.wait_ge(k_turned, n)
                    at = slice((g - 1) * TK, g * TK)
                    nc.scalar.activation(kT_part[1 - p][0][:, :, at], turn_ps[:, 0:NKV * TK].rearrange("p (h n) -> p h n", h=NKV),
                                         ACT.Copy, scale=kw_sb[:, 0:1]).then_inc(kT_hi, 1)
                if attend:
                    act.wait_ge(negated, s + 1)
                    for h in range(G):
                        nc.scalar.activation(probs[:, h, :], probs[:, h, :], ACT.Exp, bias=neg_top[:, h:h + 1],
                                             accum_out=total[:, h:h + 1]).then_inc(exped, 1)
                if isinstance(b, int) and b == B - 1 and g == 3:
                    wo_high(act, (0, 1))
                if ahead and g < 3:
                    act.wait_ge(k_biased, 3 * b1 + g + 1)
                    square(k_sb, k_ss, TK, k_squared, 3 * b1 + g + 1, q_squared, s1 + 1)
                if g == 0:
                    attended(attend, s, g)
                if ahead and g in V_TILE:
                    t = V_TILE[g]
                    act.wait_ge(v_proj, 3 * b1 + t + 1)
                    nc.scalar.copy(v_part[1 - p][0][:, t, :], qv_ps[0:TK, :]).then_inc(v_hi, 1)
                if ahead and g == 2:
                    act.wait_ge(x_turned, b1 + 1)
                    nc.scalar.copy(xT_part[0][:].rearrange("p c n -> p (c n)"), turn_ps[:, 0:KC * S]).then_inc(xT_hi, 1)
                if g > 0:
                    attended(attend, s, g)
                if next_q:
                    act.wait_ge(q_turned, s1 + 1)
                    nc.scalar.activation(qT_part[0][:], turn_ps[:, 0:G * S], ACT.Copy, scale=qws[:, 0:1]).then_inc(qT_hi, 1)
                if attend:
                    high_p(s, g, range(KT - 1))

            def high_p(s, g, tiles):
                for t in tiles:
                    act.wait_ge(p_turned, 3 * s + t + 1)
                    nc.scalar.copy(pT_part[0][:, t, :], pT_ps[(3 * g + t) % 2][0:TK, 0:G * S]).then_inc(pT_hi, 1)

            def attended(attend, s, g):
                if attend and not (isinstance(s, int) and s == 0):
                    out_of(s - 1, (g - 1) % NKV)

            def out_of(s, g):
                act.wait_ge(pv_done, s + 1)
                wait(act, o_stored, 16 * s)
                nc.scalar.activation(o_sb[:], o_ps[:, 0:G * S], ACT.Identity, bias=bv_sb[:, g:g + 1]).then_inc(o_made, 1)

            def tail():
                high_p(4 * B - 1, NKV - 1, [KT - 1])
                act.wait_ge(at_loaded, 16)
                nc.scalar.copy(at_part[0][0][:], at_raw[:]).then_inc(at_hi, 1)
                wo_high(act, (2, 3))
                out_of(4 * B - 1, NKV - 1)
            run(act, slot, tail)
            later_act(act)

        @block.vector
        def _(dve):
            def split_ctx(c):
                dve.wait_ge(ctx_loaded, 16 * (c + 1))
                wait(dve, v_proj, 3 * c)
                nc.vector.tensor_copy(ctx_part[0][:], ctx_raw[:]).then_inc(ctx_hi, 1)
            split_ctx(0)
            for j in range(len(pieces)):
                dve.wait_ge(w_hi, j + 1)
                nc.vector.tensor_tensor(piece_part(j, 1), stage[j % 2][:], piece_part(j, 0).bitcast(F32), ALU.subtract).then_inc(w_lo, 1)
            dve.wait_ge(consts_loaded, 16 * 5)
            dve.wait_ge(mask_loaded, 16)
            nc.vector.tensor_scalar(qws[:], qw_sb[:], HD ** -0.5, None, ALU.mult).then_inc(qws_made, 1)
            dve.wait_ge(qws_made, 1)

            def scaled(rows, scales, done):
                for h in range(G):
                    at = slice(h * HD, (h + 1) * HD)
                    last = nc.vector.tensor_scalar(rows[:, at], rows[:, at], scales[:, h:h + 1], None, ALU.mult)
                last.then_inc(done, 1)

            def slot(b, p, g, attend, ahead):
                s, s1, b1 = 4 * b + g, 4 * b + g + 1, b + 1
                next_q = (g == 3 and ahead) or (g < 3 and attend)
                if next_q:
                    dve.wait_ge(q_proj, s1 + 1)
                    gq = (g + 1) % NKV
                    nc.vector.tensor_tensor(q_sb[:], qv_ps[0:S, :], bq_sb[:, gq * G * HD:(gq + 1) * G * HD], ALU.add).then_inc(q_biased, 1)
                if attend and not (isinstance(s, int) and s == 0):
                    low_p(s - 1, (g - 1) % NKV, [KT - 1])
                if attend:
                    for h in range(G):
                        wait_apart(dve, dve_passed, scored, 4 * s + h + 1)
                        nc.vector.tensor_tensor_reduce(probs[:, h, :], score_ps[h % 2][0:S, 0:SE], mask_sb[:], 1.0, LOWEST,
                                                       ALU.add, ALU.max, top[:, h:h + 1]).then_inc(masked, 1)
                    dve.wait_ge(masked, 4 * s + 4)
                    nc.vector.tensor_scalar(neg_top, top, -1.0, None, ALU.mult).then_inc(negated, 1)
                if isinstance(b, int) and b == B - 1 and g == 3:
                    wo_low(dve, (0, 1))
                if ahead and g > 0:
                    n = 3 * b1 + g
                    dve.wait_ge(kT_hi, n)
                    at = slice((g - 1) * TK, g * TK)
                    nc.vector.scalar_tensor_tensor(out=kT_part[1 - p][1][:, :, at], in0=turn_ps[:, 0:NKV * TK].rearrange("p (h n) -> p h n", h=NKV),
                                                   scalar=kw_sb[:, 0:1], in1=kT_part[1 - p][0][:, :, at].bitcast(F32),
                                                   op0=ALU.mult, op1=ALU.subtract).then_inc(kT_lo, 1)
                if next_q:
                    dve.wait_ge(q_squared, s1 + 1)
                    nc.vector.tensor_scalar(q_ms, q_ss, 1.0 / HD, RMS_EPS, ALU.mult, ALU.add).then_inc(q_mean, 1)
                if ahead and g < 3:
                    dve.wait_ge(k_proj, 3 * b1 + g + 1)
                    nc.vector.tensor_tensor(k_sb[:], k_ps[0:TK, :], bk_sb[:], ALU.add).then_inc(k_biased, 1)
                if attend:
                    dve.wait_ge(exped, 4 * s + 4)
                    nc.vector.reciprocal(inv_total, total).then_inc(inverted, 1)
                    dve.wait_ge(inverted, s + 1)
                    for h in range(G):
                        last = nc.vector.tensor_scalar(probs[:, h, :], probs[:, h, :], inv_total[:, h:h + 1], None, ALU.mult)
                    last.then_inc(p_normed, 1)
                if ahead and g < 3:
                    dve.wait_ge(k_squared, 3 * b1 + g + 1)
                    nc.vector.tensor_scalar(k_ms, k_ss, 1.0 / HD, RMS_EPS, ALU.mult, ALU.add).then_inc(k_mean, 1)
                if ahead and g == 0:
                    dve.wait_ge(x_loaded, 16 * (b1 + 1))
                    nc.vector.bn_stats(bn, x_sb[:]).then_inc(ln_step, 1)
                    wait_apart(dve, dve_passed, ln_step, 2 * b1 + 1)
                    nc.vector.bn_aggr(mv, bn).then_inc(ln_step, 1)
                    dve.wait_ge(ln_step, 2 * b1 + 2)
                    nc.vector.tensor_scalar(ln_var, mv[:, 1:2], LN_EPS, None, ALU.add).then_inc(ln_stats, 1)
                if ahead and g == 1:
                    dve.wait_ge(ln_rsqrt, b1 + 1)
                    nc.vector.tensor_scalar(x_sb[:], x_sb[:], mv[:, 0:1], ln_rs, ALU.subtract, ALU.mult).then_inc(x_normed, 1)
                if next_q:
                    dve.wait_ge(q_rsqrt, s1 + 1)
                    scaled(q_sb, q_rs, q_normed)
                if ahead and g in V_TILE:
                    t = V_TILE[g]
                    dve.wait_ge(v_hi, 3 * b1 + t + 1)
                    nc.vector.tensor_tensor(v_part[1 - p][1][:, t, :], qv_ps[0:TK, :], v_part[1 - p][0][:, t, :].bitcast(F32),
                                            ALU.subtract).then_inc(v_lo, 1)
                if g == 3 and (not isinstance(b, int) or b + 2 < B):
                    split_ctx(b + 2)
                if ahead and g == 2:
                    dve.wait_ge(xT_hi, b1 + 1)
                    nc.vector.tensor_tensor(xT_part[1][:].rearrange("p c n -> p (c n)"), turn_ps[:, 0:KC * S],
                                            xT_part[0][:].rearrange("p c n -> p (c n)").bitcast(F32), ALU.subtract).then_inc(xT_lo, 1)
                if ahead and g < 3:
                    dve.wait_ge(k_rsqrt, 3 * b1 + g + 1)
                    scaled(k_sb, k_rs, k_normed)
                if next_q:
                    dve.wait_ge(qT_hi, s1 + 1)
                    nc.vector.scalar_tensor_tensor(out=qT_part[1][:], in0=turn_ps[:, 0:G * S], scalar=qws[:, 0:1],
                                                   in1=qT_part[0][:].bitcast(F32), op0=ALU.mult, op1=ALU.subtract).then_inc(qT_lo, 1)
                if attend:
                    low_p(s, g, range(KT - 1))

            def low_p(s, g, tiles):
                for t in tiles:
                    dve.wait_ge(pT_hi, 3 * s + t + 1)
                    nc.vector.tensor_tensor(pT_part[1][:, t, :], pT_ps[(3 * g + t) % 2][0:TK, 0:G * S],
                                            pT_part[0][:, t, :].bitcast(F32), ALU.subtract).then_inc(pT_lo, 1)

            def tail():
                low_p(4 * B - 1, NKV - 1, [KT - 1])
                dve.wait_ge(at_hi, 1)
                nc.vector.tensor_tensor(at_part[0][1][:], at_raw[:], at_part[0][0][:].bitcast(F32), ALU.subtract).then_inc(at_lo, 1)
                wo_low(dve, (2, 3))
            run(dve, slot, tail)
            later_dve(dve)

        @block.tensor
        def _(pe):
            pe.wait_ge(ident_made, 1)
            pe.wait_ge(key_padded, 4)

            def pv(b, s, g, p):
                pe.wait_ge(pT_lo, 3 * s + 3)
                pe.wait_ge(v_lo, 3 * b + 3)
                wait(pe, o_made, s)
                for t in range(KT):
                    v = [v_part[p][i][:, t, g * HD:(g + 1) * HD] for i in range(2)]
                    pT = [pT_part[i][:, t, :] for i in range(2)]
                    last = products(pe, o_ps[:, 0:G * S], v, pT, t == 0, t == KT - 1)
                last.then_inc(pv_done, 1)

            def turn_p(s, g, tiles):
                for t in tiles:
                    wait(pe, pT_lo, 3 * s + t - 1)
                    for h in range(G):
                        last = nc.tensor.transpose(pT_ps[(3 * g + t) % 2][0:TK, h * S:(h + 1) * S],
                                                   probs[:, h, t * TK:(t + 1) * TK], ident[0:S, 0:S])
                    last.then_inc(p_turned, 1)

            def slot(b, p, g, attend, ahead):
                s, s1, b1 = 4 * b + g, 4 * b + g + 1, b + 1
                next_q = (g == 3 and ahead) or (g < 3 and attend)
                if next_q:
                    pe.wait_ge(xT_lo, b1 + 1 if g == 3 else b + 1)
                    wait(pe, v_lo, 3 * b1 + V_BEFORE[g] if ahead else 3 * b1)
                    if isinstance(b, int) and b < 0:
                        pe.wait_ge(w_lo, Q_PIECE)
                    gq = (g + 1) % NKV
                    for c in range(KC):
                        last = products(pe, qv_ps[0:S, :], [xT[:, c, :] for xT in xT_part],
                                        [w[:, c, gq * G * HD:(gq + 1) * G * HD] for w in wq_part], c == 0, c == KC - 1)
                    last.then_inc(q_proj, 1)
                if attend and not (isinstance(s, int) and s == 0):
                    turn_p(s - 1, (g - 1) % NKV, [KT - 1])
                if attend:
                    pe.wait_ge(qT_lo, s + 1)
                    if g == 0:
                        pe.wait_ge(kT_lo, 3 * b + 3)
                for h in range(G):
                    if attend:
                        wait(pe, masked, 4 * s + h - 1)
                        products(pe, score_ps[h % 2][0:S, 0:SE_EVEN], [q[:, h * S:(h + 1) * S] for q in qT_part],
                                 [k[:, g, :] for k in kT_part[p]], True, True).then_inc(scored, 1)
                    if h == 2 and ahead and g > 0:
                        pe.wait_ge(k_normed, 3 * b1 + g)
                        wait(pe, qT_lo, s + 1)
                        if g == 3:
                            pe.wait_ge(xT_lo, b1 + 1)
                        for hk in range(NKV):
                            last = nc.tensor.transpose(turn_ps[:, hk * TK:(hk + 1) * TK], k_sb[:, hk * HD:(hk + 1) * HD], ident[0:TK, 0:TK])
                        last.then_inc(k_turned, 1)
                if ahead and g < 3:
                    pe.wait_ge(ctx_lo, b1 + 1)
                    if isinstance(b, int) and b < 0:
                        pe.wait_ge(w_lo, K_PIECE)
                    wait(pe, k_biased, 3 * b1 + g)
                    for c in range(KC):
                        last = products(pe, k_ps[0:TK, :], [a[:, c, g * TK:(g + 1) * TK] for a in ctx_part],
                                        [w[:, c, :] for w in wk_part], c == 0, c == KC - 1)
                    last.then_inc(k_proj, 1)
                if g == 0 and attend and not (isinstance(s, int) and s == 0):
                    pv(b - 1, s - 1, NKV - 1, 1 - p)
                if ahead and g in V_TILE:
                    t = V_TILE[g]
                    if isinstance(b, int) and b < 0:
                        pe.wait_ge(w_lo, V_PIECE)
                        wait(pe, v_lo, 3 * b1 + t)
                    wait(pe, q_biased, s1 + 1)
                    for c in range(KC):
                        last = products(pe, qv_ps[0:TK, :], [a[:, c, t * TK:(t + 1) * TK] for a in ctx_part],
                                        [w[:, c, :] for w in wv_part], c == 0, c == KC - 1)
                    last.then_inc(v_proj, 1)
                if ahead and g == 2:
                    pe.wait_ge(x_normed, b1 + 1)
                    wait(pe, kT_lo, 3 * b1 + g)
                    for c in range(KC):
                        last = nc.tensor.transpose(turn_ps[:, c * S:(c + 1) * S], x_sb[:, c * 128:(c + 1) * 128], ident[0:S, 0:S])
                    last.then_inc(x_turned, 1)
                if g > 0 and attend:
                    pv(b, s - 1, g - 1, p)
                if next_q:
                    pe.wait_ge(q_normed, s1 + 1)
                    if ahead and g > 0:
                        pe.wait_ge(kT_lo, 3 * b1 + g)
                    if ahead and g == 2:
                        pe.wait_ge(xT_lo, b1 + 1)
                    for h in range(G):
                        last = nc.tensor.transpose(turn_ps[:, h * S:(h + 1) * S], q_sb[:, h * HD:(h + 1) * HD], ident[0:S, 0:S])
                    last.then_inc(q_turned, 1)
                if attend:
                    pe.wait_ge(p_normed, s + 1)
                    turn_p(s, g, range(KT - 1))

            def tail():
                turn_p(4 * B - 1, NKV - 1, [KT - 1])
                pv(B - 1, 4 * B - 1, NKV - 1, 1)
            run(pe, slot, tail)
            later_pe(pe)


def kernel(x, ctx_2048, mask_1xSxS2_ff0, L0_xattn_Wq, L0_xattn_bq, L0_xattn_Wk, L0_xattn_bk, L0_xattn_Wv, L0_xattn_bv,
           L0_xattn_Wo, L0_xattn_qn_w, L0_xattn_kn_w, L0_ffn_router_w, L0_ffn_gate_w, L0_ffn_up_w, L0_ffn_down_w,
           L0_ffn_shared_gate_w, L0_ffn_shared_up_w, L0_ffn_shared_down_w):
    import concourse.bacc as bacc
    from concourse.bass_utils import run_bass_kernel_spmd

    ctx = np.asarray(ctx_2048)
    laid = {
        "x": np.asarray(x),
        "ctxT": ctx.reshape(B, SE, KC, 128).transpose(0, 3, 2, 1),
        "mask": np.asarray(mask_1xSxS2_ff0)[0],
        "wq": np.asarray(L0_xattn_Wq),
        "bq_rows": np.broadcast_to(np.asarray(L0_xattn_bq), (S, NH * HD)),
        "wk": np.asarray(L0_xattn_Wk),
        "bk_rows": np.broadcast_to(np.asarray(L0_xattn_bk), (TK, NKV * HD)),
        "wv": np.asarray(L0_xattn_Wv),
        "bv_cols": np.asarray(L0_xattn_bv).reshape(NKV, HD).T,
        "qn_col": np.asarray(L0_xattn_qn_w).reshape(HD, 1),
        "kn_col": np.asarray(L0_xattn_kn_w).reshape(HD, 1),
        "wo": np.asarray(L0_xattn_Wo),
        "router": np.asarray(L0_ffn_router_w),
        "expert_gate": np.asarray(L0_ffn_gate_w),
        "expert_up": np.asarray(L0_ffn_up_w),
        "expert_down": np.asarray(L0_ffn_down_w),
        "shared_gate": np.asarray(L0_ffn_shared_gate_w),
        "shared_up": np.asarray(L0_ffn_shared_up_w),
        "shared_down": np.asarray(L0_ffn_shared_down_w),
    }
    laid = {name: np.ascontiguousarray(a) for name, a in laid.items()}
    nc = bacc.Bacc("TRN2", target_bir_lowering=False, num_devices=1)
    t = {name: nc.dram_tensor(name, a.shape, mybir.dt.from_np(a.dtype), kind="ExternalInput").ap() for name, a in laid.items()}
    out = nc.dram_tensor("out", (B, S, H), F32, kind="ExternalOutput").ap()
    xattn_ffn_kernel(nc, *[t[n] for n in ("x", "ctxT", "mask", "wq", "bq_rows", "wk", "bk_rows", "wv", "bv_cols", "qn_col", "kn_col", "wo", "router")],
                     [t["expert_gate"], t["expert_up"], t["expert_down"]], [t["shared_gate"], t["shared_up"], t["shared_down"]], out)
    result = run_bass_kernel_spmd(nc, [laid], core_ids=[0])
    return result.results[0]["out"]
```

```python
from contextlib import ExitStack

import numpy as np
import concourse.bass as bass
from concourse import mybir

F32 = mybir.dt.float32
F32R = mybir.dt.float32r
BF16 = mybir.dt.bfloat16
I32 = mybir.dt.int32
U32 = mybir.dt.uint32
ALU = mybir.AluOpType
ACT = mybir.ActivationFunctionType
AX_X = mybir.AxisListType.X

B, S, H = 16, 112, 512
SE = 375
NH, NKV, HD = 16, 4, 128
G = NH // NKV
KC = H // 128
KT = 3
TK = SE // KT
SE_EVEN = SE + SE % 2
LN_EPS, RMS_EPS = 1e-5, 1e-6
TOK = B * S
NT = TOK // 128
F = 512
FC = F // 128
E = 8
SLOTS = (TOK - E) // 128 + E
HELD = E - 1
LO_FROM = 5
RING = 4
HELD_FIRST, EARLY = 3, 3
TURN_AFTER = 10
GATHERS = 4
PIECE = 2048
LOWEST = -3.0e38


def held_at(e):
    return (e + HELD_FIRST) % HELD


def wait(eng, sem, value):
    if not isinstance(value, int) or value > 0:
        eng.wait_ge(sem, value)


def wait_apart(eng, passed, sem, value):
    eng.wait_ge(sem, value)
    eng.sem_inc(passed, 1)


def xattn_ffn_kernel(nc, x, ctxT, mask, wq, bq_rows, wk, bk_rows, wv, bv_cols, qn_col, kn_col, wo,
                     router, expert_w, shared_w, out):
    with ExitStack() as outer:
        def sb(name, shape, dt=F32, into=outer):
            return into.enter_context(nc.sbuf_tensor(name, shape, dt))

        def psum(name, shape, dt=F32):
            return outer.enter_context(nc.psum_tensor(name, shape, dt))

        def sem(name):
            return outer.enter_context(nc.semaphore(name))

        small = sb("small", [128, 64])
        ident = sb("ident", [128, 128])
        minus_half = sb("minus_half", [128, 4])
        zeros = sb("zeros", [128, 128])
        a_small = ExitStack()
        bk_sb = sb("bk_sb", [TK, NKV * HD], F32, a_small)
        squares = sb("squares", [128, G * HD], BF16, a_small)
        a_small.close()

        router_sb = sb("router_sb", [128, KC, E])
        below = sb("below", [128, 128], BF16)
        ones = sb("ones", [128, 128], BF16)
        iota_e = sb("iota_e", [128, NT, E])
        slot_row = sb("slot_row", [128, SLOTS])
        chosen_b = sb("chosen_b", [128, NT, E], BF16)
        seen_b = sb("seen_b", [128, NT + 1, E], BF16)
        logits = sb("logits", [128, NT, E])
        best = sb("best", [128, NT])
        spare = sb("spare", [128, NT, E])
        lowest_at = sb("lowest_at", [128, NT])
        count_i = sb("count_i", [128, 3, E], I32)
        padded = sb("padded", [128, E])
        start = sb("start", [128, E + 1])
        place = sb("place", [128, NT])
        place_i = sb("place_i", [128, NT], I32)
        place_now = [sb(f"place_now{i}", [128, 1], I32) for i in range(2)]
        owner = sb("owner", [128, 2, SLOTS])
        owner_i = sb("owner_i", [128, SLOTS], I32)
        held_i = sb("held_i", [128, SLOTS], I32)
        score = sb("score", [128, NT])

        c_phase = ExitStack()
        expert_sb = sb("expert_sb", [128, HELD, 3, KC, F], F32, c_phase)
        y_out = sb("y_out", [128, H], F32, c_phase)
        emid_sb = sb("emid_sb", [128, F], F32, c_phase)
        block_in = [sb(f"block_in{p}", [128, H], F32, c_phase) for p in range(2)]
        eT_part = [sb(f"eT_{n}", [128, KC, 128], F32R, c_phase) for n in ("hi", "lo")]
        emT_part = [sb(f"emT_{n}", [128, FC, 128], F32R, c_phase) for n in ("hi", "lo")]
        chunk_part = [[sb(f"chunk_{n}{r}", [128, F], F32R, c_phase) for n in ("hi", "lo")] for r in range(RING)]
        c_phase.close()

        d_phase = ExitStack()
        sb("places_before", [128, held_at(1) * 3 * KC * F], F32, d_phase)
        base = sb("base", [128, NT, H], F32, d_phase)
        gathered = sb("gathered", [128, NT, H], F32, d_phase)
        d_phase.close()

        wq_part = [sb(f"wq_{n}", [128, KC, NH * HD], F32R) for n in ("hi", "lo")]
        wide_part = wq_part
        a_phase = ExitStack()

        def a_sb(name, shape, dt=F32):
            return sb(name, shape, dt, a_phase)
        wk_part = [a_sb(f"wk_{n}", [128, KC, NKV * HD], F32R) for n in ("hi", "lo")]
        wv_part = [a_sb(f"wv_{n}", [128, KC, NKV * HD], F32R) for n in ("hi", "lo")]
        ctx_raw = a_sb("ctx_raw", [128, KC, SE])
        ctx_part = [a_sb(f"ctx_{n}", [128, KC, SE], F32R) for n in ("hi", "lo")]
        x_sb = a_sb("x_sb", [S, H])
        xT_part = [a_sb(f"xT_{n}", [128, KC, S], F32R) for n in ("hi", "lo")]
        bq_sb = a_sb("bq_sb", [S, NH * HD])
        bv_sb = a_sb("bv_sb", [128, NKV])
        qw_sb = a_sb("qw_sb", [128, 1])
        kw_sb = a_sb("kw_sb", [128, 1])
        qws = a_sb("qws", [128, 1])
        mask_sb = a_sb("mask_sb", [S, SE])
        q_sb = a_sb("q_sb", [S, G * HD])
        k_sb = a_sb("k_sb", [TK, NKV * HD])
        kT_part = [[a_sb(f"kT_{n}{p}", [128, NKV, SE_EVEN], F32R) for n in ("hi", "lo")] for p in range(2)]
        v_part = [[a_sb(f"v_{n}{p}", [TK, KT, NKV * HD], F32R) for n in ("hi", "lo")] for p in range(2)]
        qT_part = [a_sb(f"qT_{n}", [128, G * S], F32R) for n in ("hi", "lo")]
        o_sb = a_sb("o_sb", [128, G * S])
        with ExitStack() as early:
            stage = [sb(f"stage{i}", [128, PIECE], F32, early) for i in range(2)]
        probs = a_sb("probs", [S, G, SE])
        pT_part = [a_sb(f"pT_{n}", [TK, KT, G * S], F32R) for n in ("hi", "lo")]

        a_phase.close()

        b_phase = ExitStack()
        b1_early = ExitStack()
        wo_stage = [sb(f"wo_stage{i}", [128, PIECE], F32, b1_early) for i in range(4)]
        at_raw = sb("at_raw", [128, NH, 128], F32, b1_early)
        at_part = [[sb(f"at_{n}{p}", [128, NH, 128], F32R, b1_early) for n in ("hi", "lo")] for p in range(2)]
        b1_early.close()
        sb("before_experts", [128, HELD_FIRST * 3 * KC * F - 2 * KC * NH * HD], F32, b_phase)
        sb("first_expert", [128, 3, KC, F], F32, b_phase)
        shared_raw = [sb(f"shared_raw{i}", [128, PIECE], F32, b_phase) for i in range(3)]
        sb("third_expert", [128, 3, KC, F], F32, b_phase)
        acc = sb("acc", [128, NT, H], F32, b_phase)
        b1_phase = ExitStack()
        sb("first_rows", [128, H], F32, b1_phase)
        x_in = sb("x_in", [128, H], F32, b1_phase)
        x1 = [sb(f"x1_{p}", [128, H], F32, b1_phase) for p in range(2)]
        h_out = [sb(f"h_out{p}", [128, H], F32, b1_phase) for p in range(2)]
        hT_f = sb("hT_f", [128, KC, 128], F32, b1_phase)
        b1_phase.close()
        b2_phase = ExitStack()
        h_in = [sb(f"h_in{p}", [128, H], F32, b2_phase) for p in range(2)]
        hT_part = [sb(f"hT_{n}", [128, KC, 128], F32R, b2_phase) for n in ("hi", "lo")]
        xs_out = [sb(f"xs_out{p}", [128, H], F32, b2_phase) for p in range(2)]
        mT_part = [sb(f"mT_{n}", [128, FC, 128], F32R, b2_phase) for n in ("hi", "lo")]
        mid_sb = sb("mid_sb", [128, F], F32, b2_phase)
        gate_sb = sb("gate_sb", [128, F], F32, b2_phase)
        b2_phase.close()
        b_phase.close()

        attended = nc.dram_tensor("attended", [128, NH, TOK], F32, kind="Internal").ap()
        h_dram = nc.dram_tensor("h_rows", [TOK, H], F32, kind="Internal").ap()
        xs_dram = nc.dram_tensor("xs_rows", [SLOTS * 128, H], F32, kind="Internal").ap()
        x2_dram = nc.dram_tensor("x2_rows", [TOK, H], F32, kind="Internal").ap()
        y_dram = nc.dram_tensor("y_rows", [SLOTS * 128, H], F32, kind="Internal").ap()

        bn, mv, ln_var, ln_rs = small[0:S, 0:6], small[0:S, 6:8], small[0:S, 8:9], small[0:S, 9:10]
        bn128, mv128, ln_var128, ln_rs128 = small[:, 0:6], small[:, 6:8], small[:, 8:9], small[:, 9:10]
        q_ss, q_ms, q_rs = (small[0:S, 12 + 4 * i:16 + 4 * i] for i in range(3))
        k_ss, k_ms, k_rs = (small[0:TK, 24 + 4 * i:28 + 4 * i] for i in range(3))
        top, neg_top, total, inv_total = (small[0:S, 36 + 4 * i:40 + 4 * i] for i in range(4))

        score_ps = [psum(f"score_ps{i}", [128, 512]) for i in range(2)]
        qv_ps = psum("qv_ps", [128, 512])
        k_ps = psum("k_ps", [128, 512])
        turn_ps = psum("turn_ps", [128, 512])
        pT_ps = [psum(f"pT_ps{i}", [128, 512]) for i in range(2)]
        o_ps = psum("o_ps", [128, 512])

        stage_loaded = [sem(f"stage_loaded{i}") for i in range(2)]
        consts_loaded, mask_loaded, ctx_loaded, x_loaded, o_stored = (
            sem(n) for n in ("consts_loaded", "mask_loaded", "ctx_loaded", "x_loaded", "o_stored"))
        w_hi, w_lo, made = sem("w_hi"), sem("w_lo"), sem("made")
        key_padded = sem("key_padded")
        ident_zeroed, ident_made, qws_made = sem("ident_zeroed"), sem("ident_made"), sem("qws_made")
        ctx_hi, ctx_lo = sem("ctx_hi"), sem("ctx_lo")
        ln_stats, ln_step, ln_rsqrt, x_normed, x_turned, xT_hi, xT_lo = (
            sem(n) for n in ("ln_stats", "ln_step", "ln_rsqrt", "x_normed", "x_turned", "xT_hi", "xT_lo"))
        q_proj, q_biased, q_squared, q_mean, q_rsqrt, q_normed, q_turned, qT_hi, qT_lo = (
            sem(n) for n in ("q_proj", "q_biased", "q_squared", "q_mean", "q_rsqrt", "q_normed", "q_turned", "qT_hi", "qT_lo"))
        k_proj, k_biased, k_squared, k_mean, k_rsqrt, k_normed, k_turned, kT_hi, kT_lo = (
            sem(n) for n in ("k_proj", "k_biased", "k_squared", "k_mean", "k_rsqrt", "k_normed", "k_turned", "kT_hi", "kT_lo"))
        v_proj, v_hi, v_lo = sem("v_proj"), sem("v_hi"), sem("v_lo")
        scored, masked, negated, exped, inverted, p_normed, p_turned, pT_hi, pT_lo, pv_done, o_made = (
            sem(n) for n in ("scored", "masked", "negated", "exped", "inverted", "p_normed", "p_turned",
                             "pT_hi", "pT_lo", "pv_done", "o_made"))

        b_consts, wo_hi, wo_lo, at_loaded, at_hi, at_lo, xin_loaded, projected, x_added = (
            sem(n) for n in ("b_consts", "wo_hi", "wo_lo", "at_loaded", "at_hi", "at_lo", "xin_loaded", "projected", "x_added"))
        wo_loaded = [sem(f"wo_loaded{i}") for i in range(4)]
        b_step, b_var, b_rsqrt, h_made, h_turned, hT_copied, routed, best_found, ranked = (
            sem(n) for n in ("b_step", "b_var", "b_rsqrt", "h_made", "h_turned", "hT_copied", "routed",
                             "best_found", "ranked"))
        tables, score_made, counted, plan, placed, owners, zeroed, rows_zeroed, shared_hi, shared_lo = (
            sem(n) for n in ("tables", "score_made", "counted", "plan", "placed", "owners", "zeroed", "rows_zeroed",
                             "shared_hi", "shared_lo"))
        h2_turned, hT_hi, hT_lo, gated, upped, silued, mid_made, mid_turned, mT_hi, mT_lo, shared_out, shared_added = (
            sem(n) for n in ("h2_turned", "hT_hi", "hT_lo", "gated", "upped", "silued", "mid_made", "mid_turned",
                             "mT_hi", "mT_lo", "shared_out", "shared_added"))
        xs_made = sem("xs_made")
        e_turned, eT_hi, eT_lo, e_silued, e_mid, e_mid_turned, emT_hi, emT_lo, y_made, chunk_hi, chunk_lo, chunk_used, act_passed = (
            sem(n) for n in ("e_turned", "eT_hi", "eT_lo", "e_silued", "e_mid", "e_mid_turned", "emT_hi", "emT_lo", "y_made",
                             "chunk_hi", "chunk_lo", "chunk_used", "act_passed"))
        h_loaded, h_stored, xs_stored = (
            [sem(f"{n}{p}") for p in range(2)] for n in ("h_loaded", "h_stored", "xs_stored"))
        block_loaded, y_stored = [sem(f"block_loaded{p}") for p in range(2)], sem("y_stored")
        expert_loaded = [sem(f"expert_loaded{e}") for e in range(E)]
        rows_gathered = [sem(f"rows_gathered{i}") for i in range(-(-NT // GATHERS))]
        base_loaded = [sem(f"base_loaded{i}") for i in range(-(-NT // GATHERS))]
        shared_loaded = [sem(f"shared_loaded{i}") for i in range(3)]
        x2_stored, out_stored, experts_held, downs_held, chosen_made = (
            sem(n) for n in ("x2_stored", "out_stored", "experts_held", "downs_held", "chosen_made"))
        dve_passed, pool_passed = sem("dve_passed"), sem("pool_passed")
        acc_made = sem("acc_made")
        now_copied, final_made = sem("now_copied"), sem("final_made")

        pieces = [(wk_part, None, wk), (wv_part, None, wv)] + [(wq_part, c, wq) for c in range(KC)]
        K_PIECE, V_PIECE, Q_PIECE = 1, 2, len(pieces)
        PIECES_BEFORE, PIECES_WITHIN = {0: (0, 1), 1: (3,), 2: (5,)}, {0: (2,), 1: (4,)}
        V_TILE = {0: 0, 1: 1, 3: 2}

        V_BEFORE = {0: 0, 1: 1, 2: 2, 3: 2}

        def piece_part(j, which):
            part, c, _ = pieces[j]
            return part[which][:].rearrange("p c n -> p (c n)") if c is None else part[which][:, c, :]

        def piece_source(j):
            _, c, w = pieces[j]
            w = w.rearrange("(c p) n -> p c n", p=128)
            return w if c is None else w[:, c, :]

        def products(pe, out, a, b, start, stop):
            nc.tensor.matmul(out, a[0], b[0], start=start, stop=False)
            nc.tensor.matmul(out, a[0], b[1], start=False, stop=False)
            return nc.tensor.matmul(out, a[1], b[0], start=False, stop=stop)

        def run(eng, slot, tail):
            for g in range(NKV):
                slot(-1, 1, g, False, True)
            for b in range(2):
                for g in range(NKV):
                    slot(b, b % 2, g, True, True)
            with eng.Fori(1, B // 2 - 1) as pair:
                for p in range(2):
                    for g in range(NKV):
                        slot(2 * pair + p, p, g, True, True)
            for b in range(B - 2, B):
                for g in range(NKV):
                    slot(b, b % 2, g, True, b < B - 1)
            tail()


        def steps(eng, n, step):
            pairs = (n - 2) // 2 if n % 2 == 0 else (n - 3) // 2
            for i in range(2):
                step(i, i, i == 0, False)
            with eng.Fori(1, pairs) as pair:
                for p in range(2):
                    step(2 * pair + p, p, False, False)
            for i in range(2 * pairs, n):
                step(i, i % 2, False, i == n - 1)

        def through(i, p, each=16):
            return (each // 2) * (i - p) + each

        def column(t, i):
            return t[:, bass.ds(i, 1)]

        def layer(t, i):
            return t[:, bass.ds(i, 1), :].rearrange("p a n -> p (a n)")

        def rows(t, i):
            return t[bass.ds(i * 128, 128), :]

        def wo_high(act, pieces_now):
            act.wait_ge(q_proj, 4 * B)
            for c in pieces_now:
                act.wait_ge(wo_loaded[c], 16)
                nc.scalar.copy(wide_part[0][:, c, :], wo_stage[c][:]).then_inc(wo_hi, 1)

        def wo_low(dve, pieces_now):
            for c in pieces_now:
                dve.wait_ge(wo_hi, c + 1)
                nc.vector.tensor_tensor(wide_part[1][:, c, :], wo_stage[c][:], wide_part[0][:, c, :].bitcast(F32),
                                        ALU.subtract).then_inc(wo_lo, 1)

        def load_at(sp, i):
            sp.wait_ge(at_lo, i)
            sp.dma_start(at_raw[:], attended[:, :, bass.ds(i * 128, 128)]).then_inc(at_loaded, 16)

        def chunks_through(j, k):
            if isinstance(j, int) and j == 0:
                return k + 1
            if isinstance(j, int) and j == SLOTS:
                return 3 * KC * j - 3 * KC + k + 1
            return 3 * KC * j - KC + k + 1

        def chunk_of(held, k):
            return expert_sb[:, bass.ds(held, 1), k // KC, k % KC, :].rearrange("p a n -> p (a n)")

        def place_of_slot(eng, j):
            return eng.value_load(held_i[0:1, bass.ds(j, 1)], min_val=0, max_val=HELD - 1)

        class Places:
            def __init__(self, eng):
                self.eng, self.known = eng, {}

            def of(self, j, p, ahead):
                looped = not isinstance(j, int)
                if looped and p == 0 and ("body", looped) not in self.known:
                    self.known = {("body", looped): True}
                key = (looped, (p if looped else j) + ahead)
                if key not in self.known:
                    self.known[key] = place_of_slot(self.eng, j + ahead)
                return self.known[key]

        GATE, UP, DOWN = range(KC), range(KC, 2 * KC), range(2 * KC, 3 * KC)

        def chunk_high(act, j, held, chunks):
            for k in chunks:
                before = chunks_through(j, k) - RING
                if not isinstance(before, int) or before > 0:
                    wait_apart(act, act_passed, chunk_used, before)
                nc.scalar.copy(chunk_part[k % RING][0][:], chunk_of(held, k)).then_inc(chunk_hi, 1)

        def chunk_low(dve, j, held, chunks):
            for k in chunks:
                dve.wait_ge(chunk_hi, chunks_through(j, k))
                nc.vector.tensor_tensor(chunk_part[k % RING][1][:], chunk_of(held, k), chunk_part[k % RING][0][:].bitcast(F32),
                                        ALU.subtract).then_inc(chunk_lo, 1)

        def later_sp(sp):
            sp.wait_ge(pv_done, 4 * B)
            sp.dma_start(router_sb[:], router.rearrange("(c p) e -> p c e", p=128)).then_inc(b_consts, 16)

            def load_tile(i, p, first, last):
                if isinstance(i, int) and i in (1, NT - 2, NT - 1):
                    sp.wait_ge(wo_lo, 4)
                    load_expert(sp, 0, [(1, NT - 2, NT - 1).index(i)])
                if not first and not last:
                    load_at(sp, i + 1)
                wait(sp, x_added, i)
                sp.dma_start(x_in[:], rows(x.rearrange("b s h -> (b s) h"), i)).then_inc(xin_loaded, 16)
                if not first:
                    store_h(i - 1, 1 - p)

            def store_h(i, p):
                sp.wait_ge(h_made, i + 1)
                sp.dma_start(rows(h_dram, i), h_out[p][:]).then_inc(h_stored[p], 16)
            steps(sp, NT, load_tile)
            sp.wait_ge(at_lo, NT)
            sp.wait_ge(projected, NT - 1)
            for n in range(3):
                sp.dma_start(shared_raw[n][:].rearrange("p (c n) -> p c n", c=KC),
                             shared_w[n].rearrange("(c p) n -> p c n", p=128)).then_inc(shared_loaded[n], 16)
            sp.wait_ge(h_stored[0], 8 * NT)
            sp.dma_start(h_in[0][:], rows(h_dram, 0)).then_inc(h_loaded[0], 16)
            store_h(NT - 1, (NT - 1) % 2)
            sp.wait_ge(h_stored[1], 8 * NT)

            def store_x2(i):
                sp.wait_ge(shared_added, i + 1)
                sp.dma_start(rows(x2_dram, i), layer(acc, i)).then_inc(x2_stored, 16)

            def load_h(i, p, first, last):
                if not first:
                    wait(sp, h2_turned, i - 1)
                    wait(sp, xs_made, i - 1)
                if not first:
                    sp.dma_start(h_in[p][:], rows(h_dram, i)).then_inc(h_loaded[p], 16)
                if not (isinstance(i, int) and i < 2):
                    store_x2(i - 2)
            steps(sp, NT, load_h)
            for i in range(NT - 2, NT):
                store_x2(i)
            for p in range(2):
                sp.wait_ge(xs_stored[p], 8 * NT)
            load_block(sp, 0, 0)
            load_block(sp, 1, 1)

            def load_base():
                sp.wait_ge(x2_stored, 16 * NT)
                sp.wait_ge(y_made, SLOTS - 4 + 1)
                for i in range(0, NT, GATHERS):
                    end = min(NT, i + GATHERS)
                    sp.dma_start(base[:, i:end, :], x2_dram.rearrange("(t p) n -> p t n", p=128)[:, i:end, :]).then_inc(base_loaded[i // GATHERS], 16)

            def block(j, p, first, last):
                if isinstance(j, int) and j == SLOTS - 3:
                    load_base()
                if not (isinstance(j, int) and j + 2 >= SLOTS):
                    sp.wait_ge(e_turned, j + 1)
                    load_block(sp, j + 2, p)
                if not first:
                    store_y(j - 1)

            def store_y(j):
                sp.wait_ge(y_made, j + 2)
                sp.dma_start(rows(y_dram, j), y_out[:]).then_inc(y_stored, 16)
            steps(sp, SLOTS, block)
            store_y(SLOTS - 1)
            sp.wait_ge(y_made, SLOTS + 1)
            for i in range(NT):
                sp.wait_ge(final_made, i + 1)
                sp.dma_start(rows(out.rearrange("b s h -> (b s) h"), i), gathered[:, i, :]).then_inc(out_stored, 16)
            sp.wait_ge(out_stored, 16 * NT)

        def load_expert(eng, e, matrices=range(3)):
            for n in matrices:
                eng.dma_start(expert_sb[:, held_at(e), n], expert_w[n][e].rearrange("(c p) n -> p c n", p=128)).then_inc(expert_loaded[e], 16)

        def load_block(sp, j, p):
            sp.dma_start(block_in[p][:], rows(xs_dram, j)).then_inc(block_loaded[p], 16)

        def later_pool(pool):
            pool.wait_ge(pv_done, 4 * B)
            make_tables(pool)

            def rsqrt(i, p, first, last):
                pool.wait_ge(b_var, i + 1)
                nc.gpsimd.tensor_tensor(ln_rs128, ln_var128, minus_half[:, 0:1], ALU.pow).then_inc(b_rsqrt, 1)
            steps(pool, NT, rsqrt)
            pool.wait_ge(placed, 1)
            pool.wait_ge(rows_zeroed, 16)

            def scatter(i, p, first, last):
                wait_apart(pool, pool_passed, xs_made, i + 1)
                nc.gpsimd.indirect_dma_start(out=xs_dram[:, :], out_offset=bass.IndirectOffsetOnAxis(ap=place_now[p][:, 0:1], axis=0),
                                             in_=xs_out[p][:], in_offset=None).then_inc(xs_stored[p], 16)
            steps(pool, NT, scatter)
            for e in range(EARLY):
                pool.wait_ge(expert_loaded[e], 48)
                pool.sem_inc(experts_held, 1)
                pool.sem_inc(downs_held, 1)
            pool.wait_ge(x2_stored, 16 * NT)
            pool.wait_ge(shared_out, NT)
            for p in range(2):
                pool.wait_ge(xs_stored[p], 8 * NT)
            for e in range(EARLY, E):
                if e == HELD:
                    slots = pool.value_load(count_i[0:1, 1, 0:1], min_val=0, max_val=NT)
                    wait_apart(pool, pool_passed, chunk_lo, 3 * KC * slots - KC + LO_FROM)
                for n in range(2):
                    load_expert(pool, e, [n])
                    pool.wait_ge(expert_loaded[e], 16 * (n + 1))
                pool.sem_inc(experts_held, 1)
                if e == HELD:
                    wait_apart(pool, pool_passed, chunk_lo, 3 * KC * slots + 2 * KC + LO_FROM)
                load_expert(pool, e, [2])
                pool.wait_ge(expert_loaded[e], 48)
                pool.sem_inc(downs_held, 1)
            pool.wait_ge(y_made, SLOTS + 1)
            pool.wait_ge(y_stored, 16 * SLOTS)
            for i in range(NT):
                nc.gpsimd.indirect_dma_start(out=gathered[:, i, :], out_offset=None, in_=y_dram[:, :],
                                             in_offset=bass.IndirectOffsetOnAxis(ap=place_i[:, i:i + 1], axis=0)).then_inc(rows_gathered[i // GATHERS], 16)

        def make_tables(pool):
            nc.gpsimd.memset(ones[:], 1.0).then_inc(tables, 1)
            nc.gpsimd.memset(below[:], 1.0).then_inc(tables, 1)
            nc.gpsimd.memset(seen_b[:], 0.0).then_inc(tables, 1)
            nc.gpsimd.iota(iota_e[:], pattern=[[0, NT], [1, E]], base=0, channel_multiplier=0, allow_small_or_imprecise_dtypes=True).then_inc(tables, 1)
            nc.gpsimd.iota(slot_row[:], pattern=[[128, SLOTS]], base=0, channel_multiplier=0, allow_small_or_imprecise_dtypes=True).then_inc(tables, 1)
            pool.wait_ge(tables, 5)
            nc.gpsimd.affine_select(out=below[:], in_=below[:], compare_op=ALU.is_gt, fill=0.0, base=0,
                                    pattern=[[1, 128]], channel_multiplier=-1).then_inc(tables, 1)

        def later_act(act):
            def high(i, p):
                if isinstance(i, int) and i == 1:
                    act.wait_ge(o_made, 4 * B)
                act.wait_ge(at_loaded, 16 * (i + 1))
                nc.scalar.copy(at_part[p][0][:], at_raw[:]).then_inc(at_hi, 1)

            def tile(i, p, first, last):
                if not last:
                    wait(act, projected, i)
                    high(i + 1, 1 - p)
                if not first:
                    copy_hT(i - 1)

            def copy_hT(i):
                if isinstance(i, int) and i == 0:
                    act.wait_ge(o_stored, 16 * 4 * B)
                act.wait_ge(h_turned, i + 1)
                nc.scalar.copy(hT_f[:].rearrange("p c n -> p (c n)"), turn_ps[:]).then_inc(hT_copied, 1)
            steps(act, NT, tile)

            def shared_high(n):
                act.wait_ge(shared_loaded[n], 16)
                act.wait_ge(projected, NT)
                nc.scalar.copy(wide_part[0][:, n, :], shared_raw[n][:]).then_inc(shared_hi, 1)
            shared_high(0)
            shared_high(1)
            copy_hT(NT - 1)
            shared_high(2)

            def hT_high(i):
                act.wait_ge(h2_turned, i + 1)
                nc.scalar.copy(hT_part[0][:].rearrange("p c n -> p (c n)"), turn_ps[:]).then_inc(hT_hi, 1)
            hT_high(0)
            act.wait_ge(shared_lo, 3)
            for e in range(1, EARLY):
                load_expert(act, e)

            def shared(i, p, first, last):
                act.wait_ge(gated, i + 1)
                wait(act, mid_made, i)
                nc.scalar.activation(gate_sb[:], score_ps[0][:], ACT.Silu).then_inc(silued, 1)
                if isinstance(i, int) and i == 1:
                    act.wait_ge(best_found, 1)
                    nc.scalar.activation(score[:], best[:], ACT.Sigmoid).then_inc(score_made, 1)
                if not last:
                    hT_high(i + 1)
                act.wait_ge(mid_turned, i + 1)
                nc.scalar.copy(mT_part[0][:].rearrange("p c n -> p (c n)"), pT_ps[0][:]).then_inc(mT_hi, 1)
            steps(act, NT, shared)

            act.sem_inc(y_made, 1)
            act.wait_ge(owners, 1)
            act.wait_ge(shared_out, NT)

            def gate_high(j, held):
                owner_now = act.value_load(owner_i[0:1, bass.ds(j, 1)], min_val=0, max_val=E - 1)
                act.wait_ge(experts_held, owner_now + 1)
                chunk_high(act, j, held, GATE)

            def down_high(step, j, held):
                owner_then = act.value_load(owner_i[0:1, bass.ds(j, 1)], min_val=0, max_val=E - 1)
                act.wait_ge(downs_held, owner_then + 1)
                chunk_high(act, step, held, DOWN)

            def block_high(j):
                act.wait_ge(e_turned, j + 1)
                nc.scalar.copy(eT_part[0][:].rearrange("p c n -> p (c n)"), turn_ps[:]).then_inc(eT_hi, 1)

            def out_y(j):
                if isinstance(j, int) and j == SLOTS - 1:
                    act.wait_ge(chunk_used, 3 * KC * SLOTS)
                else:
                    act.wait_ge(chunk_used, chunks_through(j + 1, 3 * KC - 1))
                wait(act, y_stored, 16 * j)
                nc.scalar.copy(y_out[:], o_ps[:]).then_inc(y_made, 1)
            gate_high(0, place_of_slot(act, 0))
            places_now = Places(act)
            block_high(0)
            act.wait_ge(x2_stored, 16 * NT)

            def block(j, p, first, last):
                chunk_high(act, j, places_now.of(j, p, 0), UP)
                act.wait_ge(chunk_used, chunks_through(j, KC - 1))
                wait(act, e_mid_turned, j)
                nc.scalar.activation(emid_sb[:], score_ps[0][:], ACT.Silu).then_inc(e_silued, 1)
                if not first:
                    down_high(j, j - 1, places_now.of(j, p, -1))
                if not last:
                    held = places_now.of(j, p, 1)
                    block_high(j + 1)
                    gate_high(j + 1, held)
                act.wait_ge(e_mid_turned, j + 1)
                nc.scalar.copy(emT_part[0][:].rearrange("p c n -> p (c n)"), pT_ps[0][:]).then_inc(emT_hi, 1)
                if not first:
                    out_y(j - 1)
            steps(act, SLOTS, block)
            down_high(SLOTS, SLOTS - 1, place_of_slot(act, SLOTS - 1))
            out_y(SLOTS - 1)

        def later_dve(dve):
            def low(i, p):
                dve.wait_ge(at_hi, i + 1)
                nc.vector.tensor_tensor(at_part[p][1][:], at_raw[:], at_part[p][0][:].bitcast(F32), ALU.subtract).then_inc(at_lo, 1)

            def tile(i, p, first, last):
                if not last:
                    low(i + 1, 1 - p)
                dve.wait_ge(projected, i + 1)
                dve.wait_ge(xin_loaded, 16 * (i + 1))
                nc.vector.tensor_tensor(x1[p][:], score_ps[p][:], x_in[:], ALU.add).then_inc(x_added, 1)
                dve.wait_ge(x_added, i + 1)
                nc.vector.bn_stats(bn128, x1[p][:]).then_inc(b_step, 1)
                wait_apart(dve, dve_passed, b_step, 2 * i + 1)
                nc.vector.bn_aggr(mv128, bn128).then_inc(b_step, 1)
                dve.wait_ge(b_step, 2 * i + 2)
                nc.vector.tensor_scalar(ln_var128, mv128[:, 1:2], LN_EPS, None, ALU.add).then_inc(b_var, 1)
                dve.wait_ge(b_rsqrt, i + 1)
                if not first:
                    wait(dve, h_stored[p], through(i - 2, p))
                    wait(dve, h_turned, i - 1)
                nc.vector.tensor_scalar(layer(acc, i), x1[p][:], 1.0, None, ALU.mult).then_inc(acc_made, 1)
                nc.vector.tensor_scalar(h_out[p][:], x1[p][:], mv128[:, 0:1], ln_rs128, ALU.subtract, ALU.mult).then_inc(h_made, 1)

            steps(dve, NT, tile)

            def hT_low(i):
                dve.wait_ge(hT_hi, i + 1)
                nc.vector.tensor_tensor(hT_part[1][:].rearrange("p c n -> p (c n)"), turn_ps[:],
                                        hT_part[0][:].rearrange("p c n -> p (c n)").bitcast(F32), ALU.subtract).then_inc(hT_lo, 1)

            def shared_low(n):
                dve.wait_ge(shared_hi, n + 1)
                nc.vector.tensor_tensor(wide_part[1][:, n, :], shared_raw[n][:], wide_part[0][:, n, :].bitcast(F32),
                                        ALU.subtract).then_inc(shared_lo, 1)
            shared_low(0)
            shared_low(1)
            hT_low(0)
            shared_low(2)

            def add_shared(i):
                dve.wait_ge(shared_out, i + 1)
                nc.vector.tensor_tensor(layer(acc, i), o_ps[:], layer(acc, i), ALU.add).then_inc(shared_added, 1)

            def shared(i, p, first, last):
                dve.wait_ge(upped, i + 1)
                dve.wait_ge(silued, i + 1)
                wait(dve, mid_turned, i)
                nc.vector.tensor_tensor(mid_sb[:], score_ps[1][:], gate_sb[:], ALU.mult).then_inc(mid_made, 1)
                if isinstance(i, int) and i == 1:
                    lay_out(dve)
                    dve.wait_ge(score_made, 1)
                    scale(0, 0)
                    scale(1, 1)
                if not last:
                    hT_low(i + 1)
                if not first:
                    add_shared(i - 1)
                dve.wait_ge(mT_hi, i + 1)
                nc.vector.tensor_tensor(mT_part[1][:].rearrange("p c n -> p (c n)"), pT_ps[0][:],
                                        mT_part[0][:].rearrange("p c n -> p (c n)").bitcast(F32), ALU.subtract).then_inc(mT_lo, 1)
                if isinstance(i, int) and i == 0:
                    choose(dve)
                elif isinstance(i, int) and i == 1:
                    own(dve)
                else:
                    scale(i, p)

            def scale(i, p):
                dve.wait_ge(placed, 1)
                dve.wait_ge(h_loaded[p], through(i, p))
                if not (isinstance(i, int) and i < 2):
                    dve.wait_ge(xs_stored[p], through(i - 2, p))
                nc.vector.tensor_copy(place_now[p][:], column(place_i, i)).then_inc(now_copied, 1)
                nc.vector.tensor_scalar(xs_out[p][:], h_in[p][:], column(score, i), None, ALU.mult).then_inc(xs_made, 1)
            steps(dve, NT, shared)
            add_shared(NT - 1)

            def block_low(j):
                dve.wait_ge(eT_hi, j + 1)
                nc.vector.tensor_tensor(eT_part[1][:].rearrange("p c n -> p (c n)"), turn_ps[:],
                                        eT_part[0][:].rearrange("p c n -> p (c n)").bitcast(F32), ALU.subtract).then_inc(eT_lo, 1)
            dve.sem_inc(chunk_lo, LO_FROM)
            chunk_low(dve, 0, place_of_slot(dve, 0), GATE)
            places_now = Places(dve)
            block_low(0)

            def block(j, p, first, last):
                chunk_low(dve, j, places_now.of(j, p, 0), UP)
                if not first:
                    chunk_low(dve, j, places_now.of(j, p, -1), DOWN[:2])
                dve.wait_ge(chunk_used, chunks_through(j, 2 * KC - 1))
                dve.wait_ge(e_silued, j + 1)
                nc.vector.tensor_tensor(emid_sb[:], score_ps[1][:], emid_sb[:], ALU.mult).then_inc(e_mid, 1)
                if not first:
                    chunk_low(dve, j, places_now.of(j, p, -1), DOWN[2:])
                if not last:
                    block_low(j + 1)
                    chunk_low(dve, j + 1, places_now.of(j, p, 1), GATE)
                dve.wait_ge(emT_hi, j + 1)
                nc.vector.tensor_tensor(emT_part[1][:].rearrange("p c n -> p (c n)"), pT_ps[0][:],
                                        emT_part[0][:].rearrange("p c n -> p (c n)").bitcast(F32), ALU.subtract).then_inc(emT_lo, 1)
            steps(dve, SLOTS, block)
            chunk_low(dve, SLOTS, place_of_slot(dve, SLOTS - 1), DOWN)

            for i in range(NT):
                dve.wait_ge(base_loaded[i // GATHERS], 16)
                dve.wait_ge(rows_gathered[i // GATHERS], 16 * min(GATHERS, NT - i // GATHERS * GATHERS))
                nc.vector.tensor_tensor(gathered[:, i, :], base[:, i, :], gathered[:, i, :], ALU.add).then_inc(final_made, 1)

        step_no = [0]

        def done(dve, ins):
            step_no[0] += 1
            ins.then_inc(plan, 1)
            dve.wait_ge(plan, step_no[0])

        def over_experts(t):
            return t.rearrange("p (t a) -> p t a", a=1).broadcast_to([128, NT, E])

        def over_tiles(t):
            return t.rearrange("p (a e) -> p a e", a=1).broadcast_to([128, NT, E])

        def choose(dve):
            dve.wait_ge(tables, 6)
            dve.wait_ge(routed, NT)
            done(dve, nc.vector.tensor_copy(logits[:].rearrange("p t e -> p (t e)"), k_ps[:, 0:NT * E]))
            nc.vector.tensor_reduce(best[:], logits[:], AX_X, ALU.max).then_inc(best_found, 1)
            dve.wait_ge(best_found, 1)
            done(dve, nc.vector.tensor_tensor(spare[:], logits[:], over_experts(best[:]), ALU.is_lt))
            done(dve, nc.vector.scalar_tensor_tensor(out=spare[:], in0=spare[:], scalar=float(E), in1=iota_e[:], op0=ALU.mult, op1=ALU.add))
            done(dve, nc.vector.tensor_reduce(lowest_at[:], spare[:], AX_X, ALU.min))
            done(dve, nc.vector.tensor_tensor(chosen_b[:], iota_e[:], over_experts(lowest_at[:]), ALU.is_equal))
            for t in range(NT):
                done(dve, nc.vector.tensor_tensor(seen_b[:, t + 1, :], seen_b[:, t, :], chosen_b[:, t, :], ALU.add))
            nc.vector.sem_inc(chosen_made, 1)

        def lay_out(dve):
            dve.wait_ge(ranked, 1)
            done(dve, nc.vector.tensor_scalar(spare[:, 0, :], pT_ps[1][:, NT * E:(NT + 1) * E], 127.0, None, ALU.add))
            done(dve, nc.vector.tensor_copy(count_i[:, 0, :], spare[:, 0, :]))
            done(dve, nc.vector.tensor_single_scalar(count_i[:, 1, :], count_i[:, 0, :], 7, ALU.arith_shift_right))
            done(dve, nc.vector.tensor_copy(spare[:, 0, :], count_i[:, 1, :]))
            done(dve, nc.vector.tensor_scalar(padded[:], spare[:, 0, :], 128.0, None, ALU.mult))
            done(dve, nc.vector.memset(start[:], 0.0))
            for e in range(E):
                done(dve, nc.vector.tensor_tensor(start[:, e + 1:e + 2], start[:, e:e + 1], padded[:, e:e + 1], ALU.add))
            done(dve, nc.vector.tensor_tensor(spare[:], pT_ps[1][:, 0:NT * E].rearrange("p (t e) -> p t e", t=NT), over_tiles(start[:, 0:E]), ALU.add))
            done(dve, nc.vector.tensor_tensor(spare[:], spare[:], chosen_b[:], ALU.mult))
            done(dve, nc.vector.tensor_reduce(place[:], spare[:], AX_X, ALU.add))
            nc.vector.tensor_copy(place_i[:], place[:]).then_inc(placed, 1)

        def own(dve):
            done(dve, nc.vector.memset(owner[:], 0.0))
            for e in range(1, E):
                done(dve, nc.vector.scalar_tensor_tensor(out=owner[:, e % 2, :], in0=slot_row[:], scalar=start[:, e:e + 1], in1=owner[:, (e - 1) % 2, :],
                                                    op0=ALU.is_ge, op1=ALU.add))
            held, past = owner[:, E % 2, :], owner[:, (E - 1) % 2, :]
            done(dve, nc.vector.tensor_copy(owner_i[:], past))
            done(dve, nc.vector.tensor_scalar(held, past, float(HELD - HELD_FIRST), -float(HELD), ALU.is_ge, ALU.mult))
            done(dve, nc.vector.tensor_tensor(held, held, past, ALU.add))
            done(dve, nc.vector.tensor_scalar(held, held, float(HELD_FIRST), None, ALU.add))
            done(dve, nc.vector.tensor_copy(held_i[:], held))
            nc.vector.sem_inc(owners, 1)

        def later_pe(pe):
            pe.wait_ge(wo_lo, 4)

            def tile(i, p, first, last):
                pe.wait_ge(at_lo, i + 1)
                if not first:
                    wait(pe, x_added, i - 1)
                project(p, range(TURN_AFTER))
                if not first:
                    turn(i - 1, 1 - p)
                project(p, range(TURN_AFTER, NH))
                if not first:
                    route(i - 1)

            def project(p, heads):
                for h in heads:
                    ins = products(pe, score_ps[p][:], [a[:, h, :] for a in at_part[p]],
                                   [w[:, h // 4, (h % 4) * H:(h % 4 + 1) * H] for w in wide_part], h == 0, h == NH - 1)
                if NH - 1 in heads:
                    ins.then_inc(projected, 1)

            def turn(i, p):
                pe.wait_ge(h_made, i + 1)
                wait(pe, hT_copied, i)
                for c in range(KC):
                    ins = nc.tensor.transpose(turn_ps[:, c * 128:(c + 1) * 128], h_out[p][:, c * 128:(c + 1) * 128], ident[:])
                ins.then_inc(h_turned, 1)

            def route(i):
                pe.wait_ge(hT_copied, i + 1)
                if isinstance(i, int) and i == 0:
                    pe.wait_ge(b_consts, 16)
                for c in range(KC):
                    ins = nc.tensor.matmul(k_ps[:, bass.ds(i * E, E)], hT_f[:, c, :], router_sb[:, c, :], start=(c == 0), stop=(c == KC - 1))
                ins.then_inc(routed, 1)
            steps(pe, NT, tile)
            turn(NT - 1, (NT - 1) % 2)
            route(NT - 1)

            def rank():
                pe.wait_ge(chosen_made, 1)
                nc.tensor.matmul(pT_ps[1][:, 0:NT * E], below[:], chosen_b[:].rearrange("p t e -> p (t e)"), start=True, stop=False)
                nc.tensor.matmul(pT_ps[1][:, 0:NT * E], ones[:], seen_b[:, 0:NT, :].rearrange("p t e -> p (t e)"), start=False, stop=True)
                nc.tensor.matmul(pT_ps[1][:, NT * E:(NT + 1) * E], ones[:], seen_b[:, NT, :], start=True, stop=True).then_inc(ranked, 1)

            def turn_h(i, p):
                pe.wait_ge(h_loaded[p], through(i, p))
                wait(pe, hT_lo, i)
                for c in range(KC):
                    ins = nc.tensor.transpose(turn_ps[:, c * 128:(c + 1) * 128], h_in[p][:, c * 128:(c + 1) * 128], ident[:])
                ins.then_inc(h2_turned, 1)
            turn_h(0, 0)

            def weights(n):
                return [w[:, n, :].rearrange("p (c n) -> p c n", c=KC) for w in wide_part]

            def shared_down(i):
                pe.wait_ge(mT_lo, i + 1)
                wait(pe, shared_added, i)
                if isinstance(i, int) and i == 0:
                    pe.wait_ge(shared_lo, 3)
                for c in range(FC):
                    ins = products(pe, o_ps[:], [m[:, c, :] for m in mT_part], [w[:, c, :] for w in weights(2)], c == 0, c == FC - 1)
                ins.then_inc(shared_out, 1)

            def shared(i, p, first, last):
                pe.wait_ge(hT_lo, i + 1)
                wait(pe, mid_made, i)
                for n, done in ((0, gated), (1, upped)):
                    if isinstance(i, int) and i == 0:
                        pe.wait_ge(shared_lo, n + 1)
                    for c in range(KC):
                        ins = products(pe, score_ps[n][:], [t[:, c, :] for t in hT_part], [w[:, c, :] for w in weights(n)],
                                       c == 0, c == KC - 1)
                    ins.then_inc(done, 1)
                if isinstance(i, int) and i == 1:
                    rank()
                    shared_down(0)
                if not last:
                    turn_h(i + 1, 1 - p)
                if not (isinstance(i, int) and i < 2):
                    shared_down(i - 1)
                pe.wait_ge(mid_made, i + 1)
                wait(pe, mT_lo, i)
                for c in range(FC):
                    ins = nc.tensor.transpose(pT_ps[0][:, c * 128:(c + 1) * 128], mid_sb[:, c * 128:(c + 1) * 128], ident[:])
                ins.then_inc(mid_turned, 1)
            steps(pe, NT, shared)
            shared_down(NT - 1)

            def turn_block(j, p):
                pe.wait_ge(block_loaded[p], through(j, p))
                wait(pe, eT_lo, j)
                for c in range(KC):
                    ins = nc.tensor.transpose(turn_ps[:, c * 128:(c + 1) * 128], block_in[p][:, c * 128:(c + 1) * 128], ident[:])
                ins.then_inc(e_turned, 1)

            def by_chunks(j, out, rows_part, chunks):
                for k in chunks:
                    pe.wait_ge(chunk_lo, chunks_through(j, k) + LO_FROM)
                    c = k % KC
                    products(pe, out, [t[:, c, :] for t in rows_part], [w[:] for w in chunk_part[k % RING]], c == 0, c == KC - 1).then_inc(chunk_used, 1)

            def down(j, step):
                pe.wait_ge(emT_lo, j + 1)
                if isinstance(j, int) and j == 0:
                    pe.wait_ge(shared_added, NT)
                pe.wait_ge(y_made, j + 1)
                by_chunks(step, o_ps[:], emT_part, DOWN)

            turn_block(0, 0)

            def block(j, p, first, last):
                pe.wait_ge(eT_lo, j + 1)
                wait(pe, e_mid, j)
                by_chunks(j, score_ps[0][:], eT_part, GATE)
                by_chunks(j, score_ps[1][:], eT_part, UP)
                if not last:
                    turn_block(j + 1, 1 - p)
                if not first:
                    down(j - 1, j)
                pe.wait_ge(e_mid, j + 1)
                wait(pe, emT_lo, j)
                for c in range(FC):
                    ins = nc.tensor.transpose(pT_ps[0][:, c * 128:(c + 1) * 128], emid_sb[:, c * 128:(c + 1) * 128], ident[:])
                ins.then_inc(e_mid_turned, 1)
            steps(pe, SLOTS, block)
            down(SLOTS - 1, SLOTS)

        block = outer.enter_context(nc.Block())

        @block.sync
        def _(sp):
            sp.dma_start(ctx_raw[:], ctxT[0]).then_inc(ctx_loaded, 16)
            for j in range(len(pieces)):
                if j >= 2:
                    sp.wait_ge(w_lo, j - 1)
                dst = stage[j % 2][:] if pieces[j][1] is not None else stage[j % 2][:].rearrange("p (c n) -> p c n", c=KC)
                sp.dma_start(dst, piece_source(j)).then_inc(stage_loaded[j % 2], 16)
                if j == 1:
                    sp.dma_start(x_sb[:], x[0]).then_inc(x_loaded, 16)
                    for dst, src in ((bk_sb, bk_rows), (bq_sb, bq_rows), (bv_sb, bv_cols), (qw_sb, qn_col), (kw_sb, kn_col)):
                        sp.dma_start(dst[:], src).then_inc(consts_loaded, 16)
                    sp.dma_start(mask_sb[:], mask).then_inc(mask_loaded, 16)

            def store(b, g, s):
                sp.wait_ge(o_made, s + 1)
                sp.dma_start(attended[:, g * G:(g + 1) * G, bass.ds(b * S, S)],
                             o_sb[:].rearrange("p (h n) -> p h n", h=G)).then_inc(o_stored, 16)

            def load(dst, src, b, to):
                at = src[b] if isinstance(b, int) else src[bass.ds(b, 1)].rearrange(
                    "a p n -> (a p) n" if len(src.shape) == 3 else "a p c n -> p (a c) n")
                sp.dma_start(dst, at).then_inc(to, 16)

            def slot(b, p, g, attend, ahead):
                s = 4 * b + g
                if attend and not (isinstance(s, int) and s == 0):
                    store(b if g else b - 1, (g - 1) % NKV, s - 1)
                if g == 3:
                    if not isinstance(b, int) or b + 2 < B:
                        sp.wait_ge(x_turned, b + 2)
                        load(x_sb[:], x, b + 2, x_loaded)
                if g == 0 and (not isinstance(b, int) or b + 2 < B):
                    sp.wait_ge(ctx_lo, b + 2)
                    load(ctx_raw[:], ctxT, b + 2, ctx_loaded)

                if isinstance(b, int) and b == 1 and g == 0:
                    sp.wait_ge(zeroed, 1)
                    sp.dma_start(xs_dram.rearrange("(p s) (q n) -> p (s q) n", p=128, n=128),
                                 zeros[:].rearrange("p (s n) -> p s n", s=1).broadcast_to([128, SLOTS * H // 128, 128])).then_inc(rows_zeroed, 16)
                if isinstance(b, int) and b == B - 1 and g == 0:
                    sp.wait_ge(v_proj, 3 * B)
                    for c in range(4):
                        sp.dma_start(wo_stage[c][:].rearrange("p (h n) -> p h n", h=4),
                                     wo.rearrange("(h p) n -> p h n", p=128)[:, 4 * c:4 * c + 4, :]).then_inc(wo_loaded[c], 16)
                if isinstance(b, int) and b == B - 1 and g == 1:
                    sp.wait_ge(o_stored, 16 * (4 * B - 4))
                    sp.dma_start(at_raw[:], attended[:, :, 0:128]).then_inc(at_loaded, 16)

            def tail():
                load_at(sp, 1)
                store(B - 1, NKV - 1, 4 * B - 1)
                sp.wait_ge(o_stored, 16 * 4 * B)
            run(sp, slot, tail)
            later_sp(sp)

        @block.gpsimd
        def _(pool):
            nc.gpsimd.memset(minus_half[:], -0.5).then_inc(made, 1)
            nc.gpsimd.memset(zeros[:], 0.0).then_inc(zeroed, 1)
            for p in range(2):
                for part in kT_part[p]:
                    nc.gpsimd.memset(part[:, :, SE:SE_EVEN].bitcast(F32), 0.0).then_inc(key_padded, 1)
            nc.gpsimd.memset(ident[:], 0.0).then_inc(ident_zeroed, 1)
            pool.wait_ge(ident_zeroed, 1)
            nc.gpsimd.affine_select(out=ident[:], in_=ident[:], compare_op=ALU.not_equal, fill=1.0, base=0,
                                    pattern=[[-1, 128]], channel_multiplier=1).then_inc(ident_made, 1)
            pool.wait_ge(made, 1)

            def split_ctx(c):
                pool.wait_ge(ctx_hi, c + 1)
                nc.gpsimd.tensor_tensor(ctx_part[1][:], ctx_raw[:], ctx_part[0][:].bitcast(F32), ALU.subtract).then_inc(ctx_lo, 1)
            split_ctx(0)

            def slot(b, p, g, attend, ahead):
                s1, b1 = 4 * b + g + 1, b + 1
                if (g == 3 and ahead) or (g < 3 and attend):
                    pool.wait_ge(q_mean, s1 + 1)
                    nc.gpsimd.tensor_tensor(q_rs, q_ms, minus_half[0:S, :], ALU.pow).then_inc(q_rsqrt, 1)
                if ahead and g < 3:
                    pool.wait_ge(k_mean, 3 * b1 + g + 1)
                    nc.gpsimd.tensor_tensor(k_rs, k_ms, minus_half[0:TK, :], ALU.pow).then_inc(k_rsqrt, 1)
                    pool.wait_ge(k_rsqrt, 3 * b1 + g + 1)
                    nc.gpsimd.tensor_tensor(k_sb[:].rearrange("p (h n) -> p h n", h=NKV), k_sb[:].rearrange("p (h n) -> p h n", h=NKV),
                                            k_rs.rearrange("p (h a) -> p h a", a=1).broadcast_to([TK, NKV, HD]), ALU.mult).then_inc(k_normed, 1)
                if ahead and g == 0:
                    pool.wait_ge(ln_stats, b1 + 1)
                    nc.gpsimd.tensor_tensor(ln_rs, ln_var, minus_half[0:S, 0:1], ALU.pow).then_inc(ln_rsqrt, 1)
                if g == 3 and (not isinstance(b, int) or b + 2 < B):
                    split_ctx(b + 2)
            run(pool, slot, lambda: None)
            later_pool(pool)

        @block.scalar
        def _(act):
            def weights_high(which):
                for j in which:
                    act.wait_ge(stage_loaded[j % 2], 16 * (j // 2 + 1))
                    nc.scalar.copy(piece_part(j, 0), stage[j % 2][:]).then_inc(w_hi, 1)
            weights_high(PIECES_BEFORE[0])

            def square(source, sums, rows, done, count, other, other_count):
                wait(act, done, count - 1)
                wait(act, other, other_count)
                for h in range(G):
                    at = slice(h * HD, (h + 1) * HD)
                    last = nc.scalar.activation(squares[0:rows, at], source[:, at], ACT.Square, accum_out=sums[:, h:h + 1])
                last.then_inc(done, 1)

            def slot(b, p, g, attend, ahead):
                s, s1, b1 = 4 * b + g, 4 * b + g + 1, b + 1
                next_q = (g == 3 and ahead) or (g < 3 and attend)
                if isinstance(b, int) and b < 0 and g in (1, 2):
                    weights_high(PIECES_BEFORE[g])
                if attend and not (isinstance(s, int) and s == 0):
                    high_p(s - 1, (g - 1) % NKV, [KT - 1])
                if next_q:
                    act.wait_ge(q_biased, s1 + 1)
                    square(q_sb, q_ss, S, q_squared, s1 + 1, k_squared, 3 * b1 + g * ahead)
                if ahead and g == 2:
                    act.wait_ge(x_turned, b1 + 1)
                    nc.scalar.copy(xT_part[0][:].rearrange("p c n -> p (c n)"), turn_ps[:, 0:KC * S]).then_inc(xT_hi, 1)
                if ahead and g > 0:
                    n = 3 * b1 + g
                    act.wait_ge(k_turned, n)
                    at = slice((g - 1) * TK, g * TK)
                    nc.scalar.activation(kT_part[1 - p][0][:, :, at], turn_ps[:, 0:NKV * TK].rearrange("p (h n) -> p h n", h=NKV),
                                         ACT.Copy, scale=kw_sb[:, 0:1]).then_inc(kT_hi, 1)
                if isinstance(b, int) and b == B - 1 and g >= 2:
                    wo_high(act, ((0,), (2,))[g - 2])
                if attend:
                    act.wait_ge(negated, s + 1)
                    for h in range(G):
                        nc.scalar.activation(probs[:, h, :], probs[:, h, :], ACT.Exp, bias=neg_top[:, h:h + 1],
                                             accum_out=total[:, h:h + 1]).then_inc(exped, 1)
                if isinstance(b, int) and b == B - 1 and g == 2:
                    wo_high(act, (1,))
                if isinstance(b, int) and b == B - 1 and g == 3:
                    act.wait_ge(at_loaded, 16)
                    act.wait_ge(q_biased, 4 * B)
                    nc.scalar.copy(at_part[0][0][:], at_raw[:]).then_inc(at_hi, 1)
                if ahead and g < 3:
                    act.wait_ge(k_biased, 3 * b1 + g + 1)
                    square(k_sb, k_ss, TK, k_squared, 3 * b1 + g + 1, q_squared, s1 + 1)
                if g == 0:
                    attended(attend, s, g)
                if isinstance(b, int) and b < 0 and g in PIECES_WITHIN:
                    weights_high(PIECES_WITHIN[g])
                if ahead and g in V_TILE:
                    t = V_TILE[g]
                    act.wait_ge(v_proj, 3 * b1 + t + 1)
                    nc.scalar.copy(v_part[1 - p][0][:, t, :], k_ps[0:TK, :]).then_inc(v_hi, 1)
                if g > 0:
                    attended(attend, s, g)
                if next_q:
                    act.wait_ge(q_turned, s1 + 1)
                    nc.scalar.activation(qT_part[0][:], turn_ps[:, 0:G * S], ACT.Copy, scale=qws[:, 0:1]).then_inc(qT_hi, 1)
                if attend:
                    high_p(s, g, range(KT - 1))

            def high_p(s, g, tiles):
                for t in tiles:
                    act.wait_ge(p_turned, 3 * s + t + 1)
                    nc.scalar.copy(pT_part[0][:, t, :], pT_ps[(3 * g + t) % 2][0:TK, 0:G * S]).then_inc(pT_hi, 1)

            def attended(attend, s, g):
                if attend and not (isinstance(s, int) and s == 0):
                    out_of(s - 1, (g - 1) % NKV)

            def out_of(s, g):
                act.wait_ge(pv_done, s + 1)
                wait(act, o_stored, 16 * s)
                nc.scalar.activation(o_sb[:], o_ps[:, 0:G * S], ACT.Identity, bias=bv_sb[:, g:g + 1]).then_inc(o_made, 1)

            def tail():
                high_p(4 * B - 1, NKV - 1, [KT - 1])
                wo_high(act, (3,))
                out_of(4 * B - 1, NKV - 1)
            run(act, slot, tail)
            later_act(act)

        @block.vector
        def _(dve):
            def split_ctx(c):
                dve.wait_ge(ctx_loaded, 16 * (c + 1))
                wait(dve, v_proj, 3 * c)
                nc.vector.tensor_copy(ctx_part[0][:], ctx_raw[:]).then_inc(ctx_hi, 1)
            split_ctx(0)

            def weights_low(which):
                for j in which:
                    dve.wait_ge(w_hi, j + 1)
                    nc.vector.tensor_tensor(piece_part(j, 1), stage[j % 2][:], piece_part(j, 0).bitcast(F32), ALU.subtract).then_inc(w_lo, 1)
            weights_low(PIECES_BEFORE[0])
            dve.wait_ge(consts_loaded, 16 * 5)
            dve.wait_ge(mask_loaded, 16)
            nc.vector.tensor_scalar(qws[:], qw_sb[:], HD ** -0.5, None, ALU.mult).then_inc(qws_made, 1)
            dve.wait_ge(qws_made, 1)

            def scaled(rows, scales, done):
                for h in range(G):
                    at = slice(h * HD, (h + 1) * HD)
                    last = nc.vector.tensor_scalar(rows[:, at], rows[:, at], scales[:, h:h + 1], None, ALU.mult)
                last.then_inc(done, 1)

            def slot(b, p, g, attend, ahead):
                s, s1, b1 = 4 * b + g, 4 * b + g + 1, b + 1
                next_q = (g == 3 and ahead) or (g < 3 and attend)
                if isinstance(b, int) and b < 0 and g in (1, 2):
                    weights_low(PIECES_BEFORE[g])
                if next_q:
                    dve.wait_ge(q_proj, s1 + 1)
                    gq = (g + 1) % NKV
                    nc.vector.tensor_tensor(q_sb[:], qv_ps[0:S, :], bq_sb[:, gq * G * HD:(gq + 1) * G * HD], ALU.add).then_inc(q_biased, 1)
                if attend and not (isinstance(s, int) and s == 0):
                    low_p(s - 1, (g - 1) % NKV, [KT - 1])
                for h in range(G):
                    if h == 2 and ahead and g == 2:
                        dve.wait_ge(xT_hi, b1 + 1)
                        nc.vector.tensor_tensor(xT_part[1][:].rearrange("p c n -> p (c n)"), turn_ps[:, 0:KC * S],
                                                xT_part[0][:].rearrange("p c n -> p (c n)").bitcast(F32), ALU.subtract).then_inc(xT_lo, 1)
                    if attend:
                        wait_apart(dve, dve_passed, scored, 4 * s + h + 1)
                        nc.vector.tensor_tensor_reduce(probs[:, h, :], score_ps[h % 2][0:S, 0:SE], mask_sb[:], 1.0, LOWEST,
                                                       ALU.add, ALU.max, top[:, h:h + 1]).then_inc(masked, 1)
                if attend:
                    dve.wait_ge(masked, 4 * s + 4)
                    nc.vector.tensor_scalar(neg_top, top, -1.0, None, ALU.mult).then_inc(negated, 1)
                if ahead and g > 0:
                    n = 3 * b1 + g
                    dve.wait_ge(kT_hi, n)
                    at = slice((g - 1) * TK, g * TK)
                    nc.vector.scalar_tensor_tensor(out=kT_part[1 - p][1][:, :, at], in0=turn_ps[:, 0:NKV * TK].rearrange("p (h n) -> p h n", h=NKV),
                                                   scalar=kw_sb[:, 0:1], in1=kT_part[1 - p][0][:, :, at].bitcast(F32),
                                                   op0=ALU.mult, op1=ALU.subtract).then_inc(kT_lo, 1)
                if next_q:
                    dve.wait_ge(q_squared, s1 + 1)
                    nc.vector.tensor_scalar(q_ms, q_ss, 1.0 / HD, RMS_EPS, ALU.mult, ALU.add).then_inc(q_mean, 1)
                if g == 3 and (not isinstance(b, int) or b + 2 < B):
                    split_ctx(b + 2)
                if isinstance(b, int) and b == B - 1 and g >= 2:
                    wo_low(dve, (g - 2,))
                if ahead and g < 3:
                    dve.wait_ge(k_proj, 3 * b1 + g + 1)
                    nc.vector.tensor_tensor(k_sb[:], k_ps[0:TK, :], bk_sb[:], ALU.add).then_inc(k_biased, 1)
                def weigh(half):
                    if not attend:
                        return
                    two = slice(2 * half, 2 * half + 2)
                    dve.wait_ge(exped, 4 * s + 2 * half + 2)
                    nc.vector.reciprocal(inv_total[:, two], total[:, two]).then_inc(inverted, 1)
                    dve.wait_ge(inverted, 2 * s + half + 1)
                    for h in (2 * half, 2 * half + 1):
                        nc.vector.tensor_scalar(probs[:, h, :], probs[:, h, :], inv_total[:, h:h + 1], None, ALU.mult).then_inc(p_normed, 1)
                weigh(0)
                if next_q:
                    dve.wait_ge(q_rsqrt, s1 + 1)
                    scaled(q_sb, q_rs, q_normed)
                weigh(1)
                if isinstance(b, int) and b == B - 1 and g == 3:
                    wo_low(dve, (2,))
                if ahead and g < 3:
                    dve.wait_ge(k_squared, 3 * b1 + g + 1)
                    nc.vector.tensor_scalar(k_ms, k_ss, 1.0 / HD, RMS_EPS, ALU.mult, ALU.add).then_inc(k_mean, 1)
                if ahead and g == 0:
                    dve.wait_ge(x_loaded, 16 * (b1 + 1))
                    nc.vector.bn_stats(bn, x_sb[:]).then_inc(ln_step, 1)
                    wait_apart(dve, dve_passed, ln_step, 2 * b1 + 1)
                    nc.vector.bn_aggr(mv, bn).then_inc(ln_step, 1)
                    dve.wait_ge(ln_step, 2 * b1 + 2)
                    nc.vector.tensor_scalar(ln_var, mv[:, 1:2], LN_EPS, None, ALU.add).then_inc(ln_stats, 1)
                if isinstance(b, int) and b < 0 and g in PIECES_WITHIN:
                    weights_low(PIECES_WITHIN[g])
                if ahead and g in V_TILE:
                    t = V_TILE[g]
                    dve.wait_ge(v_hi, 3 * b1 + t + 1)
                    nc.vector.tensor_tensor(v_part[1 - p][1][:, t, :], k_ps[0:TK, :], v_part[1 - p][0][:, t, :].bitcast(F32),
                                            ALU.subtract).then_inc(v_lo, 1)
                if ahead and g == 1:
                    dve.wait_ge(ln_rsqrt, b1 + 1)
                    nc.vector.tensor_scalar(x_sb[:], x_sb[:], mv[:, 0:1], ln_rs, ALU.subtract, ALU.mult).then_inc(x_normed, 1)
                if next_q:
                    dve.wait_ge(qT_hi, s1 + 1)
                    nc.vector.scalar_tensor_tensor(out=qT_part[1][:], in0=turn_ps[:, 0:G * S], scalar=qws[:, 0:1],
                                                   in1=qT_part[0][:].bitcast(F32), op0=ALU.mult, op1=ALU.subtract).then_inc(qT_lo, 1)
                if attend:
                    low_p(s, g, range(KT - 1))

            def low_p(s, g, tiles):
                for t in tiles:
                    dve.wait_ge(pT_hi, 3 * s + t + 1)
                    nc.vector.tensor_tensor(pT_part[1][:, t, :], pT_ps[(3 * g + t) % 2][0:TK, 0:G * S],
                                            pT_part[0][:, t, :].bitcast(F32), ALU.subtract).then_inc(pT_lo, 1)

            def tail():
                low_p(4 * B - 1, NKV - 1, [KT - 1])
                dve.wait_ge(at_hi, 1)
                nc.vector.tensor_tensor(at_part[0][1][:], at_raw[:], at_part[0][0][:].bitcast(F32), ALU.subtract).then_inc(at_lo, 1)
                wo_low(dve, (3,))
            run(dve, slot, tail)
            later_dve(dve)

        @block.tensor
        def _(pe):
            pe.wait_ge(ident_made, 1)
            pe.wait_ge(key_padded, 4)

            def pv(b, s, g, p):
                pe.wait_ge(pT_lo, 3 * s + 3)
                pe.wait_ge(v_lo, 3 * b + 3)
                wait(pe, o_made, s)
                for t in range(KT):
                    v = [v_part[p][i][:, t, g * HD:(g + 1) * HD] for i in range(2)]
                    pT = [pT_part[i][:, t, :] for i in range(2)]
                    last = products(pe, o_ps[:, 0:G * S], v, pT, t == 0, t == KT - 1)
                last.then_inc(pv_done, 1)

            def turn_p(s, g, tiles):
                for t in tiles:
                    wait(pe, pT_lo, 3 * s + t - 1)
                    for h in range(G):
                        last = nc.tensor.transpose(pT_ps[(3 * g + t) % 2][0:TK, h * S:(h + 1) * S],
                                                   probs[:, h, t * TK:(t + 1) * TK], ident[0:S, 0:S])
                    last.then_inc(p_turned, 1)

            def project_q(b, g, b1, s1, chunks):
                if 0 in chunks:
                    pe.wait_ge(xT_lo, b1 + 1 if g == 3 else b + 1)
                    wait(pe, q_biased, s1)
                    if isinstance(b, int) and b < 0:
                        pe.wait_ge(w_lo, Q_PIECE)
                gq = (g + 1) % NKV
                for c in chunks:
                    last = products(pe, qv_ps[0:S, :], [xT[:, c, :] for xT in xT_part],
                                    [w[:, c, gq * G * HD:(gq + 1) * G * HD] for w in wq_part], c == 0, c == KC - 1)
                if KC - 1 in chunks:
                    last.then_inc(q_proj, 1)

            def turn_x(b1, s):
                pe.wait_ge(x_normed, b1 + 1)
                wait(pe, qT_lo, s + 1)
                pe.wait_ge(kT_lo, 3 * b1 + 1)
                for c in range(KC):
                    last = nc.tensor.transpose(turn_ps[:, c * S:(c + 1) * S], x_sb[:, c * 128:(c + 1) * 128], ident[0:S, 0:S])
                last.then_inc(x_turned, 1)

            def project_k(b, p, g, b1, s1, chunks):
                if 0 in chunks:
                    pe.wait_ge(ctx_lo, b1 + 1)
                    if isinstance(b, int) and b < 0:
                        pe.wait_ge(w_lo, K_PIECE)
                    wait(pe, k_biased, 3 * b1 + g)
                    wait(pe, v_lo, 3 * b1 + V_BEFORE[g])
                for c in chunks:
                    last = products(pe, k_ps[0:TK, :], [a[:, c, g * TK:(g + 1) * TK] for a in ctx_part],
                                    [w[:, c, :] for w in wk_part], c == 0, c == KC - 1)
                if KC - 1 in chunks:
                    last.then_inc(k_proj, 1)

            def project_v(b, p, g, b1, s1, chunks):
                t = V_TILE[g]
                if 0 in chunks:
                    if isinstance(b, int) and b < 0:
                        pe.wait_ge(w_lo, V_PIECE)
                    pe.wait_ge(k_biased, 3 * b1 + min(g + 1, 3))
                for c in chunks:
                    last = products(pe, k_ps[0:TK, :], [a[:, c, t * TK:(t + 1) * TK] for a in ctx_part],
                                    [w[:, c, :] for w in wv_part], c == 0, c == KC - 1)
                if KC - 1 in chunks:
                    last.then_inc(v_proj, 1)

            def slot(b, p, g, attend, ahead):
                s, s1, b1 = 4 * b + g, 4 * b + g + 1, b + 1
                next_q = (g == 3 and ahead) or (g < 3 and attend)
                if next_q:
                    project_q(b, g, b1, s1, range(KC // 2 if g in (0, 3) else 0, KC))
                if attend and not (isinstance(s, int) and s == 0):
                    turn_p(s - 1, (g - 1) % NKV, [KT - 1])
                if attend:
                    pe.wait_ge(qT_lo, s + 1)
                    if g == 0:
                        pe.wait_ge(kT_lo, 3 * b + 3)
                for h in range(G):
                    if attend:
                        wait(pe, masked, 4 * s + h - 1)
                        products(pe, score_ps[h % 2][0:S, 0:SE_EVEN], [q[:, h * S:(h + 1) * S] for q in qT_part],
                                 [k[:, g, :] for k in kT_part[p]], True, True).then_inc(scored, 1)
                    if h == 1 and ahead:
                        if g == 2:
                            turn_x(b1, s)
                        (project_k if g < 3 else project_v)(b, p, g, b1, s1, range(KC // 2))
                    if h == 2 and ahead and g > 0:
                        pe.wait_ge(k_normed, 3 * b1 + g)
                        wait(pe, qT_lo, s + 1)
                        if g == 2:
                            pe.wait_ge(xT_lo, b1 + 1)
                        for hk in range(NKV):
                            last = nc.tensor.transpose(turn_ps[:, hk * TK:(hk + 1) * TK], k_sb[:, hk * HD:(hk + 1) * HD], ident[0:TK, 0:TK])
                        last.then_inc(k_turned, 1)
                if ahead and g < 3:
                    project_k(b, p, g, b1, s1, range(KC // 2, KC))
                if attend and g < 2 and not (isinstance(s, int) and s == 0):
                    pv(b if g else b - 1, s - 1, (g - 1) % NKV, p if g else 1 - p)
                if ahead and g in V_TILE:
                    project_v(b, p, g, b1, s1, range(KC // 2, KC) if g == 3 else range(KC))
                if g > 1 and attend:
                    pv(b, s - 1, g - 1, p)
                if ahead and g in (2, 3):
                    wait(pe, q_biased, s1 + 1)
                    pe.wait_ge(xT_lo, b1 + 1)
                    project_q(b if g == 2 else b1, (g + 1) % NKV, b1 if g == 2 else b1 + 1, s1 + 1, range(KC // 2))
                if next_q:
                    pe.wait_ge(q_normed, s1 + 1)
                    if ahead and g > 0:
                        pe.wait_ge(kT_lo, 3 * b1 + g)
                    for h in range(G):
                        last = nc.tensor.transpose(turn_ps[:, h * S:(h + 1) * S], q_sb[:, h * HD:(h + 1) * HD], ident[0:S, 0:S])
                    last.then_inc(q_turned, 1)
                if attend:
                    pe.wait_ge(p_normed, 4 * s + 4)
                    turn_p(s, g, range(KT - 1))

            def tail():
                turn_p(4 * B - 1, NKV - 1, [KT - 1])
                pv(B - 1, 4 * B - 1, NKV - 1, 1)
            run(pe, slot, tail)
            later_pe(pe)


def kernel(x, ctx_2048, mask_1xSxS2_ff0, L0_xattn_Wq, L0_xattn_bq, L0_xattn_Wk, L0_xattn_bk, L0_xattn_Wv, L0_xattn_bv,
           L0_xattn_Wo, L0_xattn_qn_w, L0_xattn_kn_w, L0_ffn_router_w, L0_ffn_gate_w, L0_ffn_up_w, L0_ffn_down_w,
           L0_ffn_shared_gate_w, L0_ffn_shared_up_w, L0_ffn_shared_down_w):
    import concourse.bacc as bacc
    from concourse.bass_utils import run_bass_kernel_spmd

    ctx = np.asarray(ctx_2048)
    laid = {
        "x": np.asarray(x),
        "ctxT": ctx.reshape(B, SE, KC, 128).transpose(0, 3, 2, 1),
        "mask": np.asarray(mask_1xSxS2_ff0)[0],
        "wq": np.asarray(L0_xattn_Wq),
        "bq_rows": np.broadcast_to(np.asarray(L0_xattn_bq), (S, NH * HD)),
        "wk": np.asarray(L0_xattn_Wk),
        "bk_rows": np.broadcast_to(np.asarray(L0_xattn_bk), (TK, NKV * HD)),
        "wv": np.asarray(L0_xattn_Wv),
        "bv_cols": np.asarray(L0_xattn_bv).reshape(NKV, HD).T,
        "qn_col": np.asarray(L0_xattn_qn_w).reshape(HD, 1),
        "kn_col": np.asarray(L0_xattn_kn_w).reshape(HD, 1),
        "wo": np.asarray(L0_xattn_Wo),
        "router": np.asarray(L0_ffn_router_w),
        "expert_gate": np.asarray(L0_ffn_gate_w),
        "expert_up": np.asarray(L0_ffn_up_w),
        "expert_down": np.asarray(L0_ffn_down_w),
        "shared_gate": np.asarray(L0_ffn_shared_gate_w),
        "shared_up": np.asarray(L0_ffn_shared_up_w),
        "shared_down": np.asarray(L0_ffn_shared_down_w),
    }
    laid = {name: np.ascontiguousarray(a) for name, a in laid.items()}
    nc = bacc.Bacc("TRN2", target_bir_lowering=False, num_devices=1)
    t = {name: nc.dram_tensor(name, a.shape, mybir.dt.from_np(a.dtype), kind="ExternalInput").ap() for name, a in laid.items()}
    out = nc.dram_tensor("out", (B, S, H), F32, kind="ExternalOutput").ap()
    xattn_ffn_kernel(nc, *[t[n] for n in ("x", "ctxT", "mask", "wq", "bq_rows", "wk", "bk_rows", "wv", "bv_cols", "qn_col", "kn_col", "wo", "router")],
                     [t["expert_gate"], t["expert_up"], t["expert_down"]], [t["shared_gate"], t["shared_up"], t["shared_down"]], out)
    result = run_bass_kernel_spmd(nc, [laid], core_ids=[0])
    return result.results[0]["out"]
```
